# Optimizing a Trainium2 kernel written in Bass

```python
import numpy as np
import jax
import jax.numpy as jnp

def _softmax(x, axis=-1):
    return jax.nn.softmax(x, axis=axis)

def _gelu(x):
    return jax.nn.gelu(x, approximate=True)

def _silu(x):
    return jax.nn.silu(x)

def _sigmoid(x):
    return jax.nn.sigmoid(x)

def _layernorm(x, axis=-1, eps=1e-05):
    m = jnp.mean(x, axis=axis, keepdims=True)
    v = jnp.var(x, axis=axis, keepdims=True)
    return (x - m) / jnp.sqrt(v + eps)

def _scatter_add(tgt, idx, src, axis=0):
    return tgt.at[idx].add(src)

def _segment_sum(src, seg, n):
    return jax.ops.segment_sum(src, seg, n)
kernel_name = 'mk_metaformer_d1_conv_nhwc1024_r4_d81d26'

def setup_inputs(seed: int=0):
    np.random.seed(seed)
    _w = jnp.asarray

    def _rec_inputs():
        import jax
        import jax.numpy as jnp
        _gk = jax.random.key(seed)
        x = -0.000125 + 0.9999 * jax.random.normal(jax.random.fold_in(_gk, 1), (1, 64, 32, 256), jnp.float32)
        return x
    x = _rec_inputs()

    def _L0_conv_setup():
        import jax, jax.numpy as jnp
        import numpy as np
        H = 8
        EPS = 1e-05

        def _ln(x, g, b):
            m = jnp.mean(x, axis=-1, keepdims=True)
            v = jnp.mean((x - m) ** 2, axis=-1, keepdims=True)
            return (x - m) * jax.lax.rsqrt(v + EPS) * g + b
        key = jax.random.key(seed)
        B, d_m, n, L, p_d = (1, 64, 32, 256, 32)
        ks = jax.random.split(key, 12)
        s = 0.02
        return {'msa': jax.random.normal(ks[0], (B, d_m, n, L), jnp.float32), 'pairs': jax.random.normal(ks[1], (B, n, n, p_d), jnp.float32), 'ln_m_g': jnp.ones((d_m,), jnp.float32), 'ln_m_b': jnp.zeros((d_m,), jnp.float32), 'ln_p_g': jnp.ones((p_d,), jnp.float32), 'ln_p_b': jnp.zeros((p_d,), jnp.float32), 'Wq': jax.random.normal(ks[2], (d_m, d_m), jnp.float32) * s, 'Wk': jax.random.normal(ks[3], (d_m, d_m), jnp.float32) * s, 'Wv': jax.random.normal(ks[4], (d_m, d_m), jnp.float32) * s, 'Wg': jax.random.normal(ks[5], (d_m, d_m), jnp.float32) * s, 'bg': jnp.zeros((d_m,), jnp.float32), 'Wb': jax.random.normal(ks[6], (p_d, H), jnp.float32) * s, 'Wo': jax.random.normal(ks[7], (d_m, d_m), jnp.float32) * s, 'bo': jnp.zeros((d_m,), jnp.float32)}
    _L0_conv_all = _L0_conv_setup()
    _L0_conv_in = {k: v for k, v in _L0_conv_all.items() if k in ('pairs', 'ln_m_g', 'ln_m_b', 'ln_p_g', 'ln_p_b', 'Wq', 'Wk', 'Wv', 'Wg', 'bg', 'Wb', 'Wo', 'bo')}
    del _L0_conv_all

    def _L0_ffn_setup():
        import jax, jax.numpy as jnp
        import numpy as np
        TOP_K = 2
        key = jax.random.key(seed)
        ks = jax.random.split(key, 8)
        B, S, D, I, E = (4, 512, 256, 512, 8)
        scale = 0.02
        return {'hidden_states': jax.random.normal(ks[0], (B, S, D), dtype=jnp.float32), 'router_w': jax.random.normal(ks[1], (D, E), dtype=jnp.float32) * scale, 'router_b': jnp.zeros((E,), dtype=jnp.float32), 'gate_w': jax.random.normal(ks[2], (E, D, I), dtype=jnp.float32) * scale, 'gate_b': jnp.zeros((E, I), dtype=jnp.float32), 'up_w': jax.random.normal(ks[3], (E, D, I), dtype=jnp.float32) * scale, 'up_b': jnp.zeros((E, I), dtype=jnp.float32), 'down_w': jax.random.normal(ks[4], (E, I, D), dtype=jnp.float32) * scale, 'down_b': jnp.zeros((E, D), dtype=jnp.float32)}
    _L0_ffn_all = _L0_ffn_setup()
    _L0_ffn_in = {k: v for k, v in _L0_ffn_all.items() if k in ('router_w', 'router_b', 'gate_w', 'gate_b', 'up_w', 'up_b', 'down_w', 'down_b')}
    del _L0_ffn_all
    return {'x': x, 'L0_conv_pairs': _L0_conv_in['pairs'], 'L0_conv_ln_m_g': _L0_conv_in['ln_m_g'], 'L0_conv_ln_m_b': _L0_conv_in['ln_m_b'], 'L0_conv_ln_p_g': _L0_conv_in['ln_p_g'], 'L0_conv_ln_p_b': _L0_conv_in['ln_p_b'], 'L0_conv_Wq': _L0_conv_in['Wq'], 'L0_conv_Wk': _L0_conv_in['Wk'], 'L0_conv_Wv': _L0_conv_in['Wv'], 'L0_conv_Wg': _L0_conv_in['Wg'], 'L0_conv_bg': _L0_conv_in['bg'], 'L0_conv_Wb': _L0_conv_in['Wb'], 'L0_conv_Wo': _L0_conv_in['Wo'], 'L0_conv_bo': _L0_conv_in['bo'], 'L0_ffn_router_w': _L0_ffn_in['router_w'], 'L0_ffn_router_b': _L0_ffn_in['router_b'], 'L0_ffn_gate_w': _L0_ffn_in['gate_w'], 'L0_ffn_gate_b': _L0_ffn_in['gate_b'], 'L0_ffn_up_w': _L0_ffn_in['up_w'], 'L0_ffn_up_b': _L0_ffn_in['up_b'], 'L0_ffn_down_w': _L0_ffn_in['down_w'], 'L0_ffn_down_b': _L0_ffn_in['down_b']}

def reference(x, L0_conv_pairs, L0_conv_ln_m_g, L0_conv_ln_m_b, L0_conv_ln_p_g, L0_conv_ln_p_b, L0_conv_Wq, L0_conv_Wk, L0_conv_Wv, L0_conv_Wg, L0_conv_bg, L0_conv_Wb, L0_conv_Wo, L0_conv_bo, L0_ffn_router_w, L0_ffn_router_b, L0_ffn_gate_w, L0_ffn_gate_b, L0_ffn_up_w, L0_ffn_up_b, L0_ffn_down_w, L0_ffn_down_b):
    import jax
    import jax.numpy as jnp

    def _L0_conv_ref(msa, pairs, ln_m_g, ln_m_b, ln_p_g, ln_p_b, Wq, Wk, Wv, Wg, bg, Wb, Wo, bo):
        import jax, jax.numpy as jnp
        import numpy as np
        H = 8
        EPS = 1e-05

        def _ln(x, g, b):
            m = jnp.mean(x, axis=-1, keepdims=True)
            v = jnp.mean((x - m) ** 2, axis=-1, keepdims=True)
            return (x - m) * jax.lax.rsqrt(v + EPS) * g + b
        B, d_m, n, L = msa.shape
        dh = d_m // H
        sqrt_c = jnp.sqrt(jnp.asarray(dh, msa.dtype))
        x = _ln(jnp.transpose(msa, (0, 3, 2, 1)), ln_m_g, ln_m_b)
        p = _ln(pairs, ln_p_g, ln_p_b)
        bias = jnp.transpose(jnp.einsum('bijc,ch->bijh', p, Wb), (0, 3, 1, 2))[:, None]

        def heads(y):
            return jnp.transpose(y.reshape(B, L, n, H, dh), (0, 1, 3, 2, 4))
        q = heads(x @ Wq)
        k = heads(x @ Wk)
        v = heads(x @ Wv)
        g = jax.nn.sigmoid(heads(x @ Wg + bg))
        scores = jnp.einsum('blhnd,blhmd->blhnm', q, k) / sqrt_c + bias
        w = jax.nn.softmax(scores, axis=-1)
        attn = g * jnp.einsum('blhnm,blhmd->blhnd', w, v)
        attn = jnp.transpose(attn, (0, 1, 3, 2, 4)).reshape(B, L, n, d_m)
        out = attn @ Wo + bo
        return jnp.transpose(out, (0, 3, 2, 1))

    def _L0_ffn_ref(hidden_states, router_w, router_b, gate_w, gate_b, up_w, up_b, down_w, down_b):
        import jax, jax.numpy as jnp
        import numpy as np
        TOP_K = 2
        B, S, D = hidden_states.shape
        E = router_w.shape[1]
        x = hidden_states.reshape(-1, D)
        T = x.shape[0]
        logits = x @ router_w + router_b
        probs = jax.nn.softmax(logits, axis=-1)
        top_v, top_i = jax.lax.top_k(probs, TOP_K)
        top_v = top_v / jnp.sum(top_v, axis=-1, keepdims=True)
        weights = jnp.zeros((T, E), dtype=x.dtype).at[jnp.arange(T)[:, None], top_i].set(top_v)
        gate = jnp.einsum('td,edi->eti', x, gate_w) + gate_b[:, None, :]
        up = jnp.einsum('td,edi->eti', x, up_w) + up_b[:, None, :]
        h = jax.nn.silu(gate) * up
        expert_out = jnp.einsum('eti,eid->etd', h, down_w) + down_b[:, None, :]
        y = jnp.einsum('te,etd->td', weights, expert_out)
        return y.reshape(B, S, D)

    def _gn(v, G=32, eps=1e-05):
        B_, H_, W_, C_ = v.shape
        g = v.reshape(B_, H_, W_, G, C_ // G)
        m = jnp.mean(g, axis=(1, 2, 4), keepdims=True)
        s = jnp.var(g, axis=(1, 2, 4), keepdims=True)
        return ((g - m) / jnp.sqrt(s + eps)).reshape(v.shape)

    def _ln_c(v, eps=1e-06):
        m = jnp.mean(v, axis=-1, keepdims=True)
        s = jnp.var(v, axis=-1, keepdims=True)
        return (v - m) / jnp.sqrt(s + eps)

    def _ln_t(v, eps=1e-05):
        m = jnp.mean(v, axis=-1, keepdims=True)
        s = jnp.var(v, axis=-1, keepdims=True)
        return (v - m) / jnp.sqrt(s + eps)

    def _to_tokens(v):
        B_, H_, W_, C_ = v.shape
        return v.reshape(B_, H_ * W_, C_)

    def _from_tokens(t, like):
        return t.reshape(like.shape)
    x = x + _L0_conv_ref(_ln_c(x), L0_conv_pairs, L0_conv_ln_m_g, L0_conv_ln_m_b, L0_conv_ln_p_g, L0_conv_ln_p_b, L0_conv_Wq, L0_conv_Wk, L0_conv_Wv, L0_conv_Wg, L0_conv_bg, L0_conv_Wb, L0_conv_Wo, L0_conv_bo)
    t = _to_tokens(x)
    t = t + _L0_ffn_ref(_ln_t(t), L0_ffn_router_w, L0_ffn_router_b, L0_ffn_gate_w, L0_ffn_gate_b, L0_ffn_up_w, L0_ffn_up_b, L0_ffn_down_w, L0_ffn_down_b)
    x = _from_tokens(t, x)
    return x

_drawn_inputs = setup_inputs


def setup_inputs(seed=0):
    import zlib

    import numpy as np

    out = dict(_drawn_inputs(seed))
    spreads = {'L0_conv_ln_m_g': (1.0, 0.6),
     'L0_conv_ln_m_b': (0.0, 0.8),
     'L0_conv_ln_p_g': (1.0, 0.6),
     'L0_conv_ln_p_b': (0.0, 0.8),
     'L0_conv_bg': (0.0, 0.8),
     'L0_conv_bo': (0.0, 0.1),
     'L0_ffn_router_b': (0.0, 0.1),
     'L0_ffn_gate_b': (0.0, 0.8),
     'L0_ffn_up_b': (0.0, 0.8),
     'L0_ffn_down_b': (0.0, 0.1)}
    factors = {'L0_conv_pairs': 8.0,
     'L0_conv_Wq': 8.0,
     'L0_conv_Wk': 8.0,
     'L0_conv_Wv': 8.0,
     'L0_conv_Wg': 8.0,
     'L0_conv_Wb': 8.0,
     'L0_conv_Wo': 8.0,
     'L0_ffn_gate_w': 3.21,
     'L0_ffn_up_w': 3.181,
     'L0_ffn_down_w': 3.036}
    for name, (base, spread) in spreads.items():
        noise = np.random.default_rng([zlib.crc32(name.encode()), seed]).standard_normal(out[name].shape)
        drawn = base * np.exp(spread * noise) if base else spread * noise
        out[name] = jnp.asarray(drawn.astype(out[name].dtype))
    for name, factor in factors.items():
        out[name] = (out[name] * factor).astype(out[name].dtype)
    return out
```

```python
import concourse.bass as bass
from concourse import mybir
from contextlib import ExitStack

D_MODEL = 64
N_SEQ = 32
L_COL = 256
HEADS = 8
D_HEAD = D_MODEL // HEADS
P_DIM = 32
EXPERTS = 8
FF = 512
P = 128

N_HALF = N_SEQ // 2
QUADS = N_HALF // 4
L_HALF = L_COL // 2

GROUP = 4
CHUNK = 16
PAIR = 2 * CHUNK
PAIRS = L_COL // PAIR
TOK = CHUNK * N_SEQ
VCOL = GROUP * D_HEAD + GROUP
Q_SCALE = float(D_HEAD) ** -0.5

TOKENS = D_MODEL * N_SEQ
TILES = TOKENS // P
TOP_K = 2
SLOTS = P
BLOCKS = (TOKENS * TOP_K + EXPERTS * (SLOTS - 1)) // SLOTS
BODY = (BLOCKS - 3) // 2
W_EXP = 2 * 2 * FF + (FF // P) * L_COL
W_PIECE = W_EXP // 3
ASSIGN = TILES * TOP_K

EPS_COL = 1e-6
EPS_TOK = 1e-5


def build(nc, x, pairs, ln_m_g, ln_m_b, ln_p_g, ln_p_b, Wq, Wk, Wv, Wg, bg, Wb, Wo, bo,
          router_w, router_b, gate_w, gate_b, up_w, up_b, down_w, down_b, out):
    fp32, fp16, i32 = mybir.dt.float32, mybir.dt.float16, mybir.dt.int32
    ALU, ACT, AX = mybir.AluOpType, mybir.ActivationFunctionType, mybir.AxisListType

    ctx = ExitStack()
    with ctx:
        def sb(name, shape, dt=fp32):
            return ctx.enter_context(nc.sbuf_tensor(name, shape, dt))

        def sem(name):
            return ctx.enter_context(nc.semaphore(name))

        x_rows = sb("x_rows", [P, N_HALF, L_COL])
        z_stack = sb("z_stack", [P, L_COL, N_SEQ], fp16)
        w_exp = sb("w_exp", [P, EXPERTS * 2 * W_EXP], fp16)
        w_stage = sb("w_stage", [P, 3, W_PIECE])

        z_pair = sb("z_pair", [P, PAIR * N_SEQ], fp16)
        proj = sb("proj", [P, TOK])
        q_hi = sb("q_hi", [P, TOK], fp16)
        q_lo = sb("q_lo", [P, TOK], fp16)
        k_hi = sb("k_hi", [P, TOK], fp16)
        k_lo = sb("k_lo", [P, TOK], fp16)
        q_exp = sb("q_exp", [P, 2, CHUNK, GROUP, N_SEQ], fp16)
        s_exp = sb("s_exp", [P, 2, 2, TOK])
        e_t = sb("e_t", [P, 2, 2, TOK])
        v_exp = sb("v_exp", [P, 2, 2 * 2 * CHUNK * VCOL])
        gate = sb("gate", [P, 2, 2 * 4 * D_MODEL])
        g_pre = sb("g_pre", [P, 2 * 4 * D_MODEL])
        att_n = sb("att_n", [P, 2, 4 * D_MODEL])
        att = sb("att", [P, 4, 2, D_MODEL])
        att_t = sb("att_t", [P, TOK])

        ident = sb("ident", [P, P])
        ident_h = sb("ident_h", [P, P], fp16)
        ones_h = sb("ones_h", [P, P], fp16)
        w_hi = sb("w_hi", [P, 448], fp16)
        w_lo = sb("w_lo", [P, 448], fp16)
        bias_t = sb("bias_t", [64, 2 * P], fp16)
        pick = sb("pick", [64, N_SEQ], fp16)
        g_row = sb("g_row", [P, D_MODEL])
        v_row = sb("v_row", [P, D_MODEL])
        head_mask = sb("head_mask", [P, GROUP])
        small = sb("small", [P, 216])
        small_i = sb("small_i", [P, 4], i32)
        maxes = sb("maxes", [P, 4, CHUNK])
        rden = sb("rden", [P, 2, 32])
        wo_pad = sb("wo_pad", [P, 2, D_MODEL])
        center = gate[:, 1, 0:P]
        before = k_lo[:, 384:512]
        bank = [ctx.enter_context(nc.psum_tensor(f"bank{i}", [P, 512], fp32)) for i in range(8)]

        et_flat = e_t[:].rearrange("p a b c -> p (a b c)")
        se_flat = s_exp[:].rearrange("p a b c -> p (a b c)")
        qe_flat = q_exp[:].rearrange("p a b c d -> p (a b c d)")
        ve_flat = v_exp[:].rearrange("p a b -> p (a b)")
        x_col = [et_flat[:, 1024 * i:1024 * (i + 1)].rearrange("p (n l) -> p n l", n=4) for i in range(2)]
        squares = [se_flat[:, 512 * h:512 * (h + 1)] for h in range(2)]
        z_tok = [se_flat[:, 1024 + 512 * h:1024 + 512 * (h + 1)] for h in range(2)]
        z_parts = [qe_flat[:, 1024 * h:1024 * (h + 1)].rearrange("p (t s d) -> p t s d", t=8, s=2) for h in range(2)]
        w_raw = ve_flat[:, 0:256]
        w_fold = ve_flat[:, 256:704]
        pair_g = ve_flat[0:32, 704:736]
        pair_b = ve_flat[0:32, 736:768]
        bg_row = ve_flat[:, 768:832]
        b_wide = ve_flat[0:64, 832:960]
        wb_sb = ve_flat[0:32, 960:968]
        pr = [ve_flat[0:32, 1024 * i:1024 * (i + 1)].rearrange("p (i c) -> p i c", c=P_DIM) for i in (1, 2, 3)]
        pair_s = att_n[0:32, :, :].rearrange("p a b -> p (a b)")
        bn = g_pre[:, 0:96].rearrange("p (n s) -> p n s", s=6)
        mv = small[:, 0:32].rearrange("p (n s) -> p n s", s=2)
        g_col, b_col, bo_col, qb_col, kb_col = (small[:, 144 + i:145 + i] for i in range(5))
        v_tile = [v_exp[:, i, :].rearrange("p (s g l c) -> p s g l c", s=2, g=2, c=VCOL) for i in range(2)]
        gate_v = [gate[:, i, :].rearrange("p (s q c) -> p s q c", s=2, q=4) for i in range(2)]

        N_PAR, N_CENTER, N_WIDE = 20, 5, 6
        var_col, sd_col, rs_col, tmp_col = (small[:, 32 + 16 * i:48 + 16 * i] for i in range(4))
        sum_tok, var_tok, sd_tok = (small[:, 96 + 16 * i:112 + 16 * i] for i in range(3))
        rs_tok, tmp_tok = (small[:, 160 + 16 * i:176 + 16 * i] for i in range(2))
        rw_sb = small[:, 192:208].rearrange("p (c e) -> p c e", c=2)
        rb_row = small[:, 208:216]
        wo_pad_raw = g_pre[:, 128:192]
        z_stack_v = z_stack[:].rearrange("p (a l) (h n) -> p a l h n", a=2, h=2)

        xn = z_stack[:].rearrange("p l n -> p (l n)").bitcast(fp32).rearrange("p (n l) -> p n l", n=N_HALF)
        gate_b_all = x_rows[:].rearrange("p n l -> p (n l)")
        up_b_all = xn.rearrange("p n l -> p (n l)")
        down_b_all = et_flat
        xn_t = [et_flat[:, 512 * i:512 * i + 512] for i in range(2)]
        ws_flat = w_stage[:].rearrange("p k w -> p (k w)")
        qe_words = qe_flat.bitcast(fp32)

        def two(flat, at, size, dt=None, parts=None):
            out2 = []
            for i in range(2):
                t = flat[:, at + size * i:at + size * (i + 1)]
                t = t.bitcast(dt) if dt else t
                out2.append(t.rearrange("p (c t) -> p c t", c=parts) if parts else t)
            return out2

        xg = two(ws_flat, 0, L_COL)
        x_hi = two(ws_flat, 512, P, fp16, 2)
        x_lo = two(ws_flat, 768, P, fp16, 2)
        y_sum = two(ws_flat, 1024, L_COL)
        yw = two(ws_flat, 1536, L_COL)
        h_sb = two(ws_flat, 2048, FF)
        g_sum = two(ve_flat, 0, FF)
        g_silu = two(ve_flat, 1024, FF)
        u_sum = two(ve_flat, 2048, FF)
        h_hi = two(qe_words, 0, FF // 2, fp16, 4)
        h_lo = two(qe_words, 512, FF // 2, fp16, 4)
        r_gt = qe_words[:, 0:1024].rearrange("p (n e k) -> p n e k", n=TILES, e=EXPERTS)
        r_eq = qe_words[:, 1024:2048].rearrange("p (n e k) -> p n e k", n=TILES, e=EXPERTS)
        r_place = se_flat.bitcast(fp16).rearrange("p (a t) -> p a t", a=ASSIGN)
        r_values = ve_flat[:, 0:ASSIGN * 3 * BLOCKS // 2].bitcast(fp16).rearrange("p (a t) -> p a t", a=ASSIGN)
        r_block = ve_flat[:, 1872:1872 + ASSIGN * BLOCKS // 2].bitcast(fp16).rearrange("p (a t) -> p a t", a=ASSIGN)
        r_iota128 = att_t[:, 0:128].bitcast(i32)
        iota_f = att_t[:, 128:256]
        r_thr = att_t[:, 256:272].bitcast(i32)
        thr_f = att_t[:, 272:288]
        r_tid = att_t[:, 288:304].bitcast(i32)
        tid_f = att_t[:, 304:320]
        r_lower = att_t[:, 320:384].rearrange("p (e k) -> p e k", e=EXPERTS)
        an_flat = att_n[:].rearrange("p c v -> p (c v)")
        at_flat = att[:].rearrange("p q c v -> p (q c v)")
        r_logit, r_rank, r_chosen, r_prob3 = (an_flat[:, 128 * i:128 * i + 128].rearrange("p (n e) -> p n e", n=TILES)
                                              for i in range(4))
        r_prob = r_prob3
        r_sel = at_flat[:, 0:64].bitcast(fp16)
        r_incl = at_flat[:, 64:128].bitcast(fp16)
        r_scan, r_keep, r_slot = (at_flat[:, 128 * i:128 * i + 128] for i in (1, 2, 3))
        r_first = proj[:, 0:128].rearrange("p (n e) -> p n e", n=TILES)
        r_tmp = proj[:, 128:256].rearrange("p (n e) -> p n e", n=TILES)
        r_slots, r_w = proj[:, 256:288], proj[:, 288:320]
        r_mx, r_sum, r_rs = (proj[:, 320 + 16 * i:336 + 16 * i] for i in range(3))
        r_cnt, r_nb, r_cum, r_base = (proj[:, 368 + 8 * i:376 + 8 * i] for i in range(4))
        r_p, r_b, r_wl = (proj[:, 400 + 32 * i:432 + 32 * i] for i in range(3))
        r_one8 = proj[:, 496:504]
        r_cmp = k_hi[:].bitcast(fp32)[:, 0:128].rearrange("p (e k) -> p e k", e=EXPERTS)
        r_ints = q_hi[:].bitcast(i32)
        r_wh = q_lo[:, 0:32]
        r_ecmp = g_pre[:, 0:BLOCKS * EXPERTS].rearrange("p (b e) -> p b e", b=BLOCKS)
        r_tab = k_lo[:].bitcast(fp32)
        g_idx = [r_ints[:, 128 + i:129 + i] for i in range(2)]
        s_idx = [r_ints[:, 130 + i:131 + i] for i in range(2)]
        ga_flat = gate[:].rearrange("p a b -> p (a b)")
        t_gather, t_scatter, t_expert = (ga_flat[:, 64 * i:64 * i + BLOCKS].bitcast(i32) for i in range(3))
        t_weight = ga_flat[:, 192:192 + BLOCKS]

        def steps(eng, signal):
            count = [0]

            def step(ins):
                ins.then_inc(signal, 1)
                count[0] += 1
                eng.wait_ge(signal, count[0])
                return count[0]
            return step

        names = """x_in0 x_in1 x_in2 x_in3 par_in pairs_in  
            const_p const_v dve_step   pe_prep pe_bias xcol_ready cen_ready sq_ready
            ztok_ready zhi_ready zlo_ready ztr_ready zst_act zst_dve wprep_ready pool_pair
            zpair_ready q_ps k_ps g_ps v_ps s_ps av_ps at_ps wo_ps
            qf_ready qh_ready kf_ready kh_ready gate_ready exp_ready att_t_ready w_hi_done
            q_lo_ready k_lo_ready vb_ready w_lo_done
            max_ready sub_ready et_ready rden_ready norm_ready att_ready gpre_ready qexp_ready vt_ready x1_ready
            xn_ready rt_ps rt_sb logit_ps   route_ps onehot_ps rows_out x1_out
            bias_rows tables_ready gcol_ready scol_ready x_got0 x_got1 y_scattered
            xt_ps xh_ready xl_ready gu_ps gadd_ready silu_ready uadd_ready h_ready ht_ps hh_ready hl_ready
            y_ps yadd_ready y_ready zero_ready pad_out tab_ps pair_v route_p vec_copied bias_copied sel_ready
            onehot_ready r_in w_in0 w_in1 w_in2 root_in root_out shift_ready prob_ready""".split()
        s = {n: sem(n) for n in names}

        token_rows = nc.dram_tensor("token_rows", (TOKENS, L_COL), fp32, kind="Internal").ap()
        block = ctx.enter_context(nc.Block())
        x_view = x[0].rearrange("d (h n) l -> h d n l", h=2)

        @block.sync
        def _(sp):
            for q in range(QUADS):
                for h in range(2):
                    sp.dma_start(x_rows[64 * h:64 * h + 64, 4 * q:4 * q + 4, :],
                                 x_view[h, :, 4 * q:4 * q + 4, :]).then_inc(s[f"x_in{q}"], 16)
            for e in range(EXPERTS):
                parts = (gate_w[e].rearrange("(c p) i -> p c i", p=P), up_w[e].rearrange("(c p) i -> p c i", p=P),
                         down_w[e].rearrange("(c p) l -> p c l", p=P))
                for k in range(3):
                    if e >= 1:
                        sp.wait_ge(s["w_hi_done"], 3 * (e - 1) + k + 1)
                        sp.wait_ge(s["w_lo_done"], 3 * (e - 1) + k + 1)
                    c = 2 if k < 2 else 4
                    sp.dma_start(w_stage[:, k, :].rearrange("p (c i) -> p c i", c=c),
                                 parts[k]).then_inc(s[f"w_in{k}"], 16)
            sp.wait_ge(s["zero_ready"], 1)
            sp.dma_start(out[TOKENS:TOKENS + SLOTS, :], se_flat[:, 0:L_COL]).then_inc(s["pad_out"], 16)
            o_view = out[0:TOKENS, :].rearrange("(d h n) l -> h d n l", h=2, n=N_HALF)
            sp.wait_ge(s["x1_ready"], 2 * PAIRS)
            for h in range(2):
                sp.dma_start(o_view[h], x_rows[64 * h:64 * h + 64, :, :]).then_inc(s["x1_out"], 16)
            r_view = token_rows.rearrange("(d h n) l -> h d n l", h=2, n=N_HALF)
            sp.wait_ge(s["xn_ready"], TILES)
            for h in range(2):
                sp.dma_start(r_view[h], xn[64 * h:64 * h + 64, :, :]).then_inc(s["rows_out"], 16)
            sp.wait_ge(s["x1_out"], 32)
            sp.wait_ge(s["xn_ready"], TILES)
            sp.dma_start(gate_b_all, gate_b.rearrange("e i -> (e i)").partition_broadcast(P)).then_inc(s["bias_rows"], 16)
            sp.wait_ge(s["rt_ps"], 8)
            sp.wait_ge(s["rows_out"], 32)
            sp.dma_start(up_b_all, up_b.rearrange("e i -> (e i)").partition_broadcast(P)).then_inc(s["bias_rows"], 16)
            sp.wait_ge(s["logit_ps"], TILES)
            sp.dma_start(down_b_all, down_b.rearrange("e l -> (e l)").partition_broadcast(P)).then_inc(s["bias_rows"], 16)
            sp.wait_ge(s["x1_out"], 32)
            sp.wait_ge(s["pad_out"], 16)
            sp.wait_ge(s["y_scattered"], 16 * BLOCKS)

        @block.gpsimd
        def _(pool):
            const = steps(pool, s["const_p"])

            def eye(t):
                const(pool.memset(t, 0.0))
                const(pool.affine_select(out=t, in_=t, compare_op=ALU.not_equal, fill=1.0, base=0,
                                         pattern=[[-1, t.shape[1]]], channel_multiplier=1))
            eye(ident[:])
            eye(ident_h[:])
            for h in range(2):
                eye(pick[32 * h:32 * h + 32, :])
            const(pool.iota(small_i[:, 0:1], pattern=[[0, 1]], base=0, channel_multiplier=1))
            pool.wait_ge(s["pairs_in"], 16)
            pool.wait_ge(s["par_in"], 16 * N_PAR)
            pool.wait_ge(s["pair_v"], 1)
            mean_b = pair_s[:, 0:32].unsqueeze(2).broadcast_to([32, N_SEQ, P_DIM])
            rstd_b = pair_s[:, 64:96].unsqueeze(2).broadcast_to([32, N_SEQ, P_DIM])
            pool.tensor_tensor(pr[0], pr[0], mean_b, ALU.subtract).then_inc(s["pool_pair"], 1)
            pool.wait_ge(s["pool_pair"], 1)
            pool.tensor_tensor(pr[1], pr[0], pr[0], ALU.mult).then_inc(s["pool_pair"], 1)
            for q in range(QUADS):
                if q == 2:
                    pool.wait_ge(s["pair_v"], 2)
                    pool.tensor_tensor(pr[0], pr[0], rstd_b, ALU.mult).then_inc(s["pool_pair"], 1)
                    pool.wait_ge(s["pool_pair"], 3)
                    pool.tensor_tensor(pr[0], pr[0], pair_g.unsqueeze(1).broadcast_to([32, N_SEQ, P_DIM]),
                                       ALU.mult).then_inc(s["pool_pair"], 1)
                    pool.wait_ge(s["pool_pair"], 4)
                    pool.tensor_tensor(pr[0], pr[0], pair_b.unsqueeze(1).broadcast_to([32, N_SEQ, P_DIM]),
                                       ALU.add).then_inc(s["pool_pair"], 1)
                for h in range(2):
                    t = 2 * q + h
                    pool.wait_ge(s["zhi_ready"], t + 1)
                    pool.tensor_tensor(z_parts[h][:, :, 1, :], z_tok[h].rearrange("p (t d) -> p t d", t=8),
                                       z_parts[h][:, :, 0, :], ALU.subtract).then_inc(s["zlo_ready"], 1)

            def parts_low(j):
                pool.wait_ge(s["qh_ready"], j + 1)
                pool.tensor_tensor(q_lo[:], proj[:], q_hi[:], ALU.subtract).then_inc(s["q_lo_ready"], 1)
                pool.wait_ge(s["kh_ready"], j + 1)
                pool.tensor_tensor(k_lo[:], proj[:], k_hi[:], ALU.subtract).then_inc(s["k_lo_ready"], 1)

            def value_bias(j):
                for c in range(2):
                    pool.wait_ge(s["norm_ready"], 2 * j + c + 1)
                    t = att_n[:, c, :].rearrange("p (q v) -> p q v", q=4)
                    pool.tensor_tensor(t, t, v_row[:].unsqueeze(1).broadcast_to([P, 4, D_MODEL]),
                                       ALU.add).then_inc(s["vb_ready"], 1)

            def weights_low(e, pieces):
                for k in pieces:
                    pool.wait_ge(s["w_hi_done"], 3 * e + k + 1)
                    hi = w_exp[:, bass.ds(e * 2 * W_EXP + k * W_PIECE, W_PIECE)]
                    lo = w_exp[:, bass.ds(e * 2 * W_EXP + W_EXP + k * W_PIECE, W_PIECE)]
                    pool.tensor_tensor(lo, w_stage[:, k, :], hi, ALU.subtract).then_inc(s["w_lo_done"], 1)

            def pool_step(j, first=False, last=False):
                if not first:
                    value_bias(j - 1)
                weights_low(j, [0])
                if not last:
                    parts_low(j + 1)
                weights_low(j, [1, 2])

            parts_low(0)
            pool_step(0, first=True)
            with pool.Fori(0, PAIRS // 2 - 1) as i:
                pool_step(2 * i + 1)
                pool_step(2 * i + 2)
            pool_step(PAIRS - 1, last=True)
            value_bias(PAIRS - 1)

            pool.wait_ge(s["x1_ready"], 2 * PAIRS)
            n_r = [0]

            def table(ins):
                ins.then_inc(s["route_p"], 1)
                n_r[0] += 1
                pool.wait_ge(s["route_p"], n_r[0])
            table(pool.memset(before, 0.0))
            table(pool.affine_select(out=before, in_=before, compare_op=ALU.is_ge, fill=-1.0, base=-1,
                                     pattern=[[1, P]], channel_multiplier=-1))
            table(pool.iota(r_iota128, pattern=[[1, P]], base=0, channel_multiplier=0))
            table(pool.iota(r_thr, pattern=[[P, TILES]], base=0, channel_multiplier=0))
            for h in range(2):
                table(pool.iota(r_tid[64 * h:64 * h + 64, :], pattern=[[1, TILES]], base=1 + N_HALF * h,
                                channel_multiplier=N_SEQ))
            table(pool.memset(r_lower, 1.0))
            table(pool.affine_select(out=r_lower, in_=r_lower, compare_op=ALU.is_gt, fill=0.0, base=0,
                                     pattern=[[1, EXPERTS], [-1, EXPERTS]], channel_multiplier=0))

            pool.wait_ge(s["tables_ready"], 1)
            pool.wait_ge(s["rows_out"], 32)
            pool.wait_ge(s["x1_out"], 32)
            pool.wait_ge(s["pad_out"], 16)

            hold, one_word = [small[0:1, 152 + i:153 + i] for i in range(4)], t_weight[0:1, 0:1]

            def gather(turn, par, first=False):
                b = 2 * turn + par
                if not first:
                    pool.wait_ge(s["xt_ps"], b - 1)
                    pool.wait_ge(s[f"x_got{par}"], 16 * turn)
                    pool.wait_ge(s["gcol_ready"], b)
                    pool.tensor_tensor(hold[0], one_word, one_word, ALU.mult)
                pool.tensor_copy(g_idx[par], t_gather[:, bass.ds(b, 1)]).then_inc(s["gcol_ready"], 1)
                pool.wait_ge(s["gcol_ready"], b + 1)
                pool.tensor_tensor(hold[1], one_word, one_word, ALU.mult)
                pool.indirect_dma_start(xg[par], None, token_rows, bass.IndirectOffsetOnAxis(g_idx[par], 0))\
                    .then_inc(s[f"x_got{par}"], 16)

            def scatter(b, par):
                pool.wait_ge(s["y_scattered"], 16 * b)
                pool.wait_ge(s["scol_ready"], b)
                pool.tensor_tensor(hold[2], one_word, one_word, ALU.mult)
                pool.tensor_copy(s_idx[par], t_scatter[:, bass.ds(b, 1)]).then_inc(s["scol_ready"], 1)
                pool.wait_ge(s["scol_ready"], b + 1)
                pool.wait_ge(s["y_ready"], b + 1)
                pool.tensor_tensor(hold[3], one_word, one_word, ALU.mult)
                pool.indirect_dma_start(out, bass.IndirectOffsetOnAxis(s_idx[par], 0), yw[par], None,
                                        compute_op=ALU.add).then_inc(s["y_scattered"], 16)

            gather(0, 0, first=True)
            gather(0, 1, first=True)
            gather(1, 0)
            with pool.Fori(0, BODY) as i:
                gather(i + 1, 1)
                scatter(2 * i, 0)
                gather(i + 2, 0)
                scatter(2 * i + 1, 1)
            for b in range(2 * BODY, BLOCKS):
                scatter(b, b % 2)
        @block.tensor
        def _(pe):
            def fold_vectors():
                pe.wait_ge(s["par_in"], 16 * N_PAR)
                pe.wait_ge(s["const_v"], N_WIDE)
                for h in range(2):
                    for k in range(2):
                        pe.matmul(bank[7][64 * h:64 * h + 64, k:k + 1], w_raw[0:64, 64 * k:64 * k + 64],
                                  b_col[0:64, :], start=True, stop=True)
                pe.matmul(bank[6][:, 0:128], b_wide, w_raw[0:64, 128:256], start=True, stop=True)\
                    .then_inc(s["pe_prep"], 1)

            def pair_bias():
                pe.wait_ge(s["pair_v"], 3)
                pe.wait_ge(s["vec_copied"], 1)
                out_v = bank[6][0:32, 0:HEADS * N_SEQ].rearrange("p (h i) -> p h i", i=N_SEQ)
                for i in range(N_SEQ):
                    mm = pe.matmul(out_v[:, :, i], pr[2][:, i, :], wb_sb, start=True, stop=True)
                mm.then_inc(s["pe_bias"], 1)

            def centre(q):
                pe.wait_ge(s["xcol_ready"], 4 * (q + 1))
                if q == 0:
                    pe.wait_ge(s["const_v"], N_CENTER)
                for h in range(2):
                    if q >= 2:
                        pe.wait_ge(s["ztok_ready"], 2 * (q - 2) + h + 1)
                    for i in range(4):
                        mm = pe.matmul(bank[2 * (q % 2) + h][:, P * i:P * i + P],
                                       x_col[q % 2][:, i, L_HALF * h:L_HALF * h + L_HALF], center,
                                       start=True, stop=True)
                    mm.then_inc(s["cen_ready"], 1)

            def stack_tokens(q):
                for h in range(2):
                    pe.wait_ge(s["zlo_ready"], 2 * q + h + 1)
                    if q >= 1:
                        pe.wait_ge(s["zst_act"] if h == 0 else s["zst_dve"], q)
                    dst = bank[4 + h][:].bitcast(fp16)
                    for t in range(8):
                        mm = pe.transpose(dst[:, P * t:P * t + P], z_parts[h][:, t, :, :].rearrange("p s d -> p (s d)"),
                                          ident_h[:])
                    mm.then_inc(s["ztr_ready"], 1)

            pe.wait_ge(s["const_p"], 9)
            fold_vectors()
            centre(0)
            centre(1)
            stack_tokens(0)
            centre(2)
            stack_tokens(1)
            centre(3)
            stack_tokens(2)
            stack_tokens(3)
            pair_bias()

            SC = [[bank[0], bank[1]], [bank[2], bank[3]]]
            PJ = [bank[4], bank[5]]
            AVB, MS = bank[6], bank[7]

            def project(j, first=False, second=False):
                pe.wait_ge(s["zpair_ready"], j + 1)
                if first:
                    pe.wait_ge(s["wprep_ready"], 1)
                    pe.wait_ge(s["zst_act"], QUADS)
                    pe.wait_ge(s["zst_dve"], QUADS)
                if not first:
                    pe.wait_ge(s["vt_ready"], 4 * (j - 1) + 3)
                for k, ready in ((0, "q_ps"), (1, "k_ps")):
                    if k == 1 and not first:
                        pe.wait_ge(s["vt_ready"], 4 * j)
                    for c in range(2):
                        for w, st in ((w_hi, True), (w_lo, False)):
                            mm = pe.matmul(PJ[k][64 * c:64 * c + 64, :], w[:, 64 * k:64 * k + 64],
                                           z_pair[:, TOK * c:TOK * c + TOK], start=st, stop=not st)
                    mm.then_inc(s[ready], 1)
                if not first:
                    pe.wait_ge(s["gpre_ready"], j)
                if not first and not second:
                    pe.wait_ge(s["x1_ready"], 2 * (j - 2))
                for t in range(8):
                    for w, st in ((w_hi, True), (w_lo, False)):
                        mm = pe.matmul(MS[:, 64 * t:64 * t + 64], z_pair[:, P * t:P * t + P], w[:, 384:448],
                                       start=st, stop=not st)
                mm.then_inc(s["g_ps"], 1)
                for c in range(2):
                    for g in range(2):
                        if c == 0:
                            pe.wait_ge(s["qf_ready"] if g == 0 else s["kf_ready"], j + 1)
                        else:
                            pe.wait_ge(s["vt_ready"], 4 * j + g + 1)
                        for w, st in ((w_hi, True), (w_lo, False)):
                            mm = pe.matmul(PJ[g][:], w[:, 128 + P * g:256 + P * g],
                                           z_pair[:, TOK * c:TOK * c + TOK], start=st, stop=not st)
                        mm.then_inc(s["v_ps"], 1)

            def scores(j, c, first=False):
                if not first:
                    pe.wait_ge(s["sub_ready"], 4 * (j - 1) + 2 * c + 2)
                if c == 0:
                    pe.wait_ge(s["qexp_ready"], 8 * (j + 1))
                    pe.wait_ge(s["k_lo_ready"], j + 1)
                for g in range(2):
                    dst = SC[c][g]
                    r0 = 64 * c + 32 * g
                    pe.matmul(dst[:], bias_t[:, P * g:P * g + P],
                              pick[:].unsqueeze(1).broadcast_to([64, CHUNK, N_SEQ]), start=True, stop=False,
                              skip_group_check=True)
                for i in range(CHUNK):
                    for g in range(2):
                        dst = SC[c][g]
                        r0 = 64 * c + 32 * g
                        for part, k in ((0, k_hi), (0, k_lo), (1, k_hi)):
                            mm = pe.matmul(dst[:, 32 * i:32 * i + 32],
                                           q_exp[r0:r0 + 32, part, i, :, :].rearrange("p h n -> p (h n)"),
                                           k[r0:r0 + 32, 32 * i:32 * i + 32], start=False, stop=(part == 1),
                                           skip_group_check=True)
                mm.then_inc(s["s_ps"], 1)

            def attend(j, c, par):
                pe.wait_ge(s["et_ready"], 2 * j + c + 1)
                pe.wait_ge(s["vt_ready"], 4 * (j + 1))
                pe.wait_ge(s["norm_ready"], 2 * j + c)
                for q in range(4):
                    for g in range(2):
                        for u in range(4):
                            i = 4 * q + u
                            mm = pe.matmul(AVB[32 * u:32 * u + 32, 72 * q + VCOL * g:72 * q + VCOL * g + VCOL],
                                           e_t[:, c, g, 32 * i:32 * i + 32], v_tile[par][:, c, g, i, :],
                                           start=True, stop=True)
                mm.then_inc(s["av_ps"], 1)

            def project_out(j, last=False):
                pe.wait_ge(s["att_ready"], 2 * (j + 1))
                pe.wait_ge(s["gpre_ready"], PAIRS if last else j + 3)
                if last:
                    pe.wait_ge(s["x1_ready"], 2 * j)
                for q in range(4):
                    mm = pe.transpose(MS[:, P * q:P * q + P], att[:, q, :, :].rearrange("p c d -> p (c d)"), ident[:])
                mm.then_inc(s["at_ps"], 1)
                pe.wait_ge(s["att_t_ready"], j + 1)
                at_v = att_t[:].rearrange("p (l h n) -> p l h n", l=CHUNK, h=2)
                for c in range(2):
                    for h in range(2):
                        mm = pe.matmul(MS[64 * h:64 * h + 64, 256 * c:256 * c + 256], wo_pad[:, c, :],
                                       at_v[:, :, h, :], start=True, stop=True)
                mm.then_inc(s["wo_ps"], 1)

            def pe_step(j, par, first=False, last=False):
                scores(j, 0, first=first)
                if not first:
                    attend(j - 1, 0, 1 - par)
                scores(j, 1, first=first)
                if not first:
                    attend(j - 1, 1, 1 - par)
                if not last:
                    project(j + 1, second=first)
                if not first:
                    project_out(j - 1, last=last)

            pe.wait_ge(s["bias_copied"], 2)
            project(0, first=True)
            pe_step(0, 0, first=True)
            with pe.Fori(0, PAIRS // 2 - 1) as i:
                pe_step(2 * i + 1, 1)
                pe_step(2 * i + 2, 0)
            pe_step(PAIRS - 1, 1, last=True)
            attend(PAIRS - 1, 0, 1)
            attend(PAIRS - 1, 1, 1)
            project_out(PAIRS - 1, last=True)

            def router_tokens(k):
                pe.wait_ge(s["xn_ready"], 2 * k + 2)
                if k >= 2:
                    pe.wait_ge(s["rt_sb"], k - 1)
                for t in range(2):
                    for c in range(2):
                        mm = pe.transpose(bank[k % 2][:, P * (2 * t + c):P * (2 * t + c) + P],
                                          xn[:, 2 * k + t, P * c:P * c + P], ident[:])
                mm.then_inc(s["rt_ps"], 1)

            def router_logits(k):
                pe.wait_ge(s["rt_sb"], k + 1)
                for t in range(2):
                    n = 2 * k + t
                    for c in range(2):
                        mm = pe.matmul(bank[2][:, 8 * n:8 * n + 8], xn_t[k % 2][:, P * (2 * t + c):P * (2 * t + c) + P],
                                       rw_sb[:, c, :], start=(c == 0), stop=(c == 1))
                    mm.then_inc(s["logit_ps"], 1)

            pe.wait_ge(s["r_in"], 32)
            for k in range(8):
                router_tokens(k)
                if k >= 1:
                    router_logits(k - 1)
            router_logits(7)

            pe.wait_ge(s["sel_ready"], 1)
            pe.matmul(bank[3][:, 128:136], ones_h[:], r_incl[:, TILES - 1:EXPERTS * TILES:TILES], start=True, stop=True)
            pe.matmul(bank[3][:, 0:128], before, r_sel, start=True, stop=False, skip_group_check=True)
            pe.matmul(bank[3][:, 0:128], ones_h[:], r_incl, start=False, stop=True, skip_group_check=True)\
                .then_inc(s["route_ps"], 1)
            pe.wait_ge(s["onehot_ready"], 1)
            for a in range(ASSIGN):
                mm = pe.matmul(bank[4][:, 0:3 * BLOCKS], r_place[:, a, :], r_values[:, a, :], start=(a == 0),
                               stop=(a == ASSIGN - 1))
            mm.then_inc(s["tab_ps"], 1)

            GU = [[bank[0], bank[1]], [bank[2], bank[3]]]
            XT, HT, YB = bank[4], bank[5], bank[6]

            def expert_of(b):
                return pe.value_load(t_expert[0:1, bass.ds(b, 1)], min_val=0, max_val=EXPERTS - 1)

            def tokens_in(turn, par, first=False):
                b = 2 * turn + par
                pe.wait_ge(s[f"x_got{par}"], 16 * (turn + 1))
                if not first:
                    pe.wait_ge(s["xl_ready"], b)
                for c in range(2):
                    mm = pe.transpose(XT[:, P * c:P * c + P], xg[par][:, P * c:P * c + P], ident[:])
                mm.then_inc(s["xt_ps"], 1)

            def hidden(b, par, k, e, first=False):
                if k == 0:
                    pe.wait_ge(s["xl_ready"], b + 1)
                if not first:
                    pe.wait_ge(s["gadd_ready"] if k == 0 else s["uadd_ready"], b - 1)
                n = 0
                for xs, w in ((x_hi, 0), (x_hi, 1), (x_lo, 0)):
                    for c in range(2):
                        mm = pe.matmul(GU[par][k][:], xs[par][:, c, :],
                                       w_exp[:, bass.ds(e * 2 * W_EXP + (w * W_EXP + k * W_PIECE + c * FF), FF)],
                                       start=(n == 0), stop=(n == 5))
                        n += 1
                mm.then_inc(s["gu_ps"], 1)

            def hidden_turned(b, par, first=False):
                pe.wait_ge(s["h_ready"], b + 1)
                if not first:
                    pe.wait_ge(s["hl_ready"], b)
                for c in range(4):
                    mm = pe.transpose(HT[:, P * c:P * c + P], h_sb[par][:, P * c:P * c + P], ident[:])
                mm.then_inc(s["ht_ps"], 1)

            def down(b, par, e, first=False):
                pe.wait_ge(s["hl_ready"], b + 1)
                if not first:
                    pe.wait_ge(s["yadd_ready"], b)
                n = 0
                for hs, w in ((h_hi, 0), (h_hi, 1), (h_lo, 0)):
                    for c in range(4):
                        mm = pe.matmul(YB[:, 0:L_COL], hs[par][:, c, :],
                                       w_exp[:, bass.ds(e * 2 * W_EXP + (w * W_EXP + 2 * W_PIECE + c * L_COL), L_COL)],
                                       start=(n == 0), stop=(n == 11))
                        n += 1
                mm.then_inc(s["y_ps"], 1)

            def pe_block(turn, par, first=False, more=2):
                b = 2 * turn + par
                if more >= 1:
                    e1 = expert_of(b + 1)
                    hidden(b + 1, 1 - par, 0, e1, first=first)
                hidden_turned(b, par, first=first)
                if more >= 1:
                    hidden(b + 1, 1 - par, 1, e1, first=first)
                if more >= 2:
                    tokens_in(turn + 1, par)
                down(b, par, expert_of(b), first=first)

            pe.wait_ge(s["tables_ready"], 1)
            tokens_in(0, 0, first=True)
            tokens_in(0, 1)
            e0 = expert_of(0)
            hidden(0, 0, 0, e0, first=True)
            hidden(0, 0, 1, e0, first=True)
            pe_block(0, 0, first=True)
            with pe.Fori(0, BODY) as i:
                pe_block(i, 1)
                pe_block(i + 1, 0)
            pe_block(BODY, 1, more=1)
            pe_block(BODY + 1, 0, more=0)

        @block.scalar
        def _(act):
            act.dma_start(pr[0], pairs[0].rearrange("i j c -> j i c")).then_inc(s["pairs_in"], 16)
            for h in range(2):
                rows = slice(64 * h, 64 * h + 64)
                for k, w in enumerate((Wq, Wk, Wv, Wg)):
                    act.dma_start(w_raw[rows, 64 * k:64 * k + 64], w).then_inc(s["par_in"], 16)
                for col, v in ((g_col, ln_m_g), (b_col, ln_m_b), (bo_col, bo)):
                    act.dma_start(col[rows, :], v.rearrange("(d a) -> d a", a=1)).then_inc(s["par_in"], 16)
                act.dma_start(wo_pad_raw[rows, :], Wo).then_inc(s["par_in"], 16)
            act.dma_start(pair_g, ln_p_g.partition_broadcast(32)).then_inc(s["par_in"], 16)
            act.dma_start(pair_b, ln_p_b.partition_broadcast(32)).then_inc(s["par_in"], 16)
            act.dma_start(bg_row, bg.partition_broadcast(P)).then_inc(s["par_in"], 16)
            act.dma_start(wb_sb, Wb).then_inc(s["par_in"], 16)
            act.dma_start(rw_sb, router_w.rearrange("(c p) e -> p c e", p=P)).then_inc(s["r_in"], 16)
            act.dma_start(rb_row, router_b.partition_broadcast(P)).then_inc(s["r_in"], 16)

            def root(k, dst, src):
                act.wait_ge(s["root_in"], k + 1)
                act.activation(dst, src, ACT.Sqrt).then_inc(s["root_out"], 1)

            def stack_out(q):
                act.wait_ge(s["ztr_ready"], 2 * q + 1)
                act.activation(z_stack_v[:, 0, :, :, 4 * q:4 * q + 4],
                               bank[4][:].bitcast(fp16).rearrange("p (i h l) -> p l h i", i=4, h=2),
                               ACT.Copy).then_inc(s["zst_act"], 1)

            root(0, sd_col, var_col)
            for q in range(QUADS):
                for h in range(2):
                    act.wait_ge(s["cen_ready"], 2 * q + h + 1)
                    if q >= 1:
                        act.wait_ge(s["root_in"], q + 1 + (q > 2))
                    act.activation(squares[h], bank[2 * (q % 2) + h][:], ACT.Square).then_inc(s["sq_ready"], 1)
                if q >= 1:
                    stack_out(q - 1)
                root(q + 1 + (q > 1), sd_tok, var_tok)
                for h in range(2):
                    act.wait_ge(s["ztok_ready"], 2 * q + h + 1)
                    if q >= 1:
                        act.wait_ge(s["ztr_ready"], 2 * (q - 1) + h + 1)
                    act.activation(z_parts[h][:, :, 0, :], z_tok[h].rearrange("p (t d) -> p t d", t=8),
                                   ACT.Copy).then_inc(s["zhi_ready"], 1)
                if q == 1:
                    root(3, pair_s[:, 96:128], pair_s[:, 32:64])
            stack_out(QUADS - 1)

            def parts_high(j, first=False):
                act.wait_ge(s["q_ps"], j + 1)
                if not first:
                    act.wait_ge(s["k_lo_ready"], j)
                act.activation(proj[:], bank[4][:], ACT.Identity, bias=qb_col, scale=Q_SCALE)\
                    .then_inc(s["qf_ready"], 1)
                act.wait_ge(s["qf_ready"], j + 1)
                if not first:
                    act.wait_ge(s["qexp_ready"], 8 * j)
                act.activation(q_hi[:], proj[:], ACT.Copy).then_inc(s["qh_ready"], 1)
                act.wait_ge(s["k_ps"], j + 1)
                act.wait_ge(s["q_lo_ready"], j + 1)
                act.activation(proj[:], bank[5][:], ACT.Identity, bias=kb_col).then_inc(s["kf_ready"], 1)
                act.wait_ge(s["kf_ready"], j + 1)
                if not first:
                    act.wait_ge(s["s_ps"], 2 * j)
                act.activation(k_hi[:], proj[:], ACT.Copy).then_inc(s["kh_ready"], 1)

            def gate_tanh(j, par, early=False):
                act.wait_ge(s["gpre_ready"], j + 1)
                if not early:
                    act.wait_ge(s["att_ready"], 2 * (j - 1))
                act.activation(gate[:, par, :], g_pre[:], ACT.Tanh, scale=0.5).then_inc(s["gate_ready"], 1)

            def exps(j, c):
                act.wait_ge(s["sub_ready"], 4 * j + 2 * c + 2)
                act.activation(s_exp[:, c, :, :], s_exp[:, c, :, :], ACT.Exp).then_inc(s["exp_ready"], 1)

            def weights_high(e, k):
                act.wait_ge(s[f"w_in{k}"], 16 * (e + 1))
                act.activation(w_exp[:, bass.ds(e * 2 * W_EXP + k * W_PIECE, W_PIECE)], w_stage[:, k, :],
                               ACT.Copy).then_inc(s["w_hi_done"], 1)

            def turned_out(j):
                act.wait_ge(s["at_ps"], j + 1)
                act.activation(att_t[:], bank[7][:], ACT.Copy).then_inc(s["att_t_ready"], 1)

            def act_step(j, par, first=False, last=False):
                exps(j, 0)
                weights_high(j, 0)
                exps(j, 1)
                weights_high(j, 1)
                if not last:
                    parts_high(j + 1)
                    gate_tanh(j + 1, 1 - par, early=first)
                weights_high(j, 2)
                if not first:
                    turned_out(j - 1)

            parts_high(0, first=True)
            gate_tanh(0, 0, early=True)
            act_step(0, 0, first=True)
            with act.Fori(0, PAIRS // 2 - 1) as i:
                act_step(2 * i + 1, 1)
                act_step(2 * i + 2, 0)
            act_step(PAIRS - 1, 1, last=True)
            turned_out(PAIRS - 1)

            root(6, sd_col, var_col)
            for k in range(8):
                act.wait_ge(s["rt_ps"], k + 1)
                if k >= 2:
                    act.wait_ge(s["logit_ps"], 2 * (k - 1))
                act.activation(xn_t[k % 2], bank[k % 2][:], ACT.Copy).then_inc(s["rt_sb"], 1)
            act.wait_ge(s["shift_ready"], 1)
            act.activation(r_prob, r_prob, ACT.Exp).then_inc(s["prob_ready"], 1)

            def tokens_high(b, par, first=False):
                act.wait_ge(s["xt_ps"], b + 1)
                if not first:
                    act.wait_ge(s["gu_ps"], 2 * (b - 1))
                act.activation(x_hi[par], bank[4][:, 0:L_COL].rearrange("p (c t) -> p c t", c=2),
                               ACT.Copy).then_inc(s["xh_ready"], 1)

            def silu(b, par, first=False):
                act.wait_ge(s["gadd_ready"], b + 1)
                if not first:
                    act.wait_ge(s["h_ready"], b - 1)
                act.activation(g_silu[par], g_sum[par], ACT.Silu).then_inc(s["silu_ready"], 1)

            def hidden_high(b, par, first=False):
                act.wait_ge(s["ht_ps"], b + 1)
                if not first:
                    act.wait_ge(s["y_ps"], b - 1)
                act.activation(h_hi[par], bank[5][:].rearrange("p (c t) -> p c t", c=4),
                               ACT.Copy).then_inc(s["hh_ready"], 1)

            def weigh(b, par, first=False):
                act.wait_ge(s["yadd_ready"], b + 1)
                if not first:
                    act.wait_ge(s["y_scattered"], 16 * (b - 1))
                act.activation(yw[par], y_sum[par], ACT.Copy, scale=t_weight[:, bass.ds(b, 1)])\
                    .then_inc(s["y_ready"], 1)

            def act_block(b, par, first=False, more=2):
                if more >= 1:
                    silu(b + 1, 1 - par, first=first)
                hidden_high(b, par, first=first)
                if more >= 2:
                    tokens_high(b + 2, par)
                weigh(b, par, first=first)

            tokens_high(0, 0, first=True)
            tokens_high(1, 1, first=True)
            silu(0, 0, first=True)
            act_block(0, 0, first=True)
            with act.Fori(0, BODY) as i:
                act_block(2 * i + 1, 1)
                act_block(2 * i + 2, 0)
            act_block(BLOCKS - 2, 1, more=1)
            act_block(BLOCKS - 1, 0, more=0)

        @block.vector
        def _(dve):
            step = steps(dve, s["dve_step"])
            n_v = [0]

            def const(ins):
                ins.then_inc(s["const_v"], 1)
                n_v[0] += 1

            def rsqrt(k, y, v, sd, t, ready):
                dve.wait_ge(s["root_out"], k + 1)
                step(dve.reciprocal(y, sd))
                step(dve.tensor_tensor(t, v, y, ALU.mult))
                step(dve.tensor_tensor(t, t, y, ALU.mult))
                step(dve.tensor_scalar(t, t, -0.5, 1.5, ALU.mult, ALU.add))
                last = dve.tensor_tensor(y, y, t, ALU.mult)
                if ready:
                    last.then_inc(ready, 1)
                else:
                    step(last)

            const(dve.memset(ones_h[:], 1.0))
            const(dve.memset(center, 0.0))
            dve.wait_ge(s["const_v"], 2)
            for h in range(2):
                const(dve.memset(center[64 * h:64 * h + 64, 64 * h:64 * h + 64], -1.0 / D_MODEL))
            dve.wait_ge(s["const_v"], 4)
            dve.wait_ge(s["const_p"], 9)
            const(dve.tensor_tensor(center, center, ident[:], ALU.add))
            assert n_v[0] == N_CENTER
            step(dve.tensor_scalar(small_i[:, 1:2], small_i[:, 0:1], 3, 3, ALU.logical_shift_right, ALU.bitwise_and))
            step(dve.tensor_copy(small[:, 150:151], small_i[:, 1:2]))
            for h in range(GROUP):
                step(dve.tensor_scalar(head_mask[:, h:h + 1], small[:, 150:151], float(h), None, ALU.is_equal))
            step(dve.memset(w_fold, 0.0))
            step(dve.memset(w_lo[64:128, :], 0.0))
            step(dve.memset(wo_pad[:], 0.0))
            dve.wait_ge(s["par_in"], 16 * N_PAR)
            const(dve.tensor_copy(b_wide, b_col[0:64, :].broadcast_to([64, P])))
            assert n_v[0] == N_WIDE
            step(dve.tensor_scalar(w_fold[:, 0:128], w_raw[:, 0:128], g_col, None, ALU.mult))
            step(dve.tensor_scalar(w_fold[:, 384:448], w_raw[:, 192:256], g_col, None, ALU.mult))
            for h in range(GROUP):
                c0 = (GROUP * D_HEAD + D_HEAD) * h
                step(dve.tensor_scalar(w_fold[:, 128:384].rearrange("p (g r) -> p g r", g=2)[:, :, c0:c0 + D_HEAD],
                                       w_raw[:, 128:192].rearrange("p (g r) -> p g r", g=2)[:, :, 8 * h:8 * h + 8],
                                       g_col, None, ALU.mult))
            step(dve.tensor_copy(w_hi[:], w_fold))
            step(dve.tensor_tensor(w_lo[0:64, :], w_fold[0:64, :], w_hi[0:64, :], ALU.subtract))
            for c in range(2):
                rows = slice(64 * c, 64 * c + 64)
                step(dve.tensor_scalar(wo_pad[rows, c, :], wo_pad_raw[rows, :], 0.5, None, ALU.mult))
            dve.wait_ge(s["pe_prep"], 1)
            step(dve.tensor_scalar(qb_col, bank[7][:, 0:1], Q_SCALE, None, ALU.mult))
            step(dve.tensor_copy(kb_col, bank[7][:, 1:2]))
            step(dve.tensor_copy(v_row[:], bank[6][:, 0:64]))
            dve.tensor_tensor(g_row[:], bank[6][:, 64:128], bg_row, ALU.add).then_inc(s["vec_copied"], 1)
            dve.wait_ge(s["vec_copied"], 1)
            dve.wait_ge(s["pairs_in"], 16)
            step(dve.tensor_reduce(pair_s[:, 0:32], pr[0], AX.X, ALU.add))
            dve.tensor_scalar(pair_s[:, 0:32], pair_s[:, 0:32], 1.0 / P_DIM, None, ALU.mult).then_inc(s["pair_v"], 1)

            for q in range(QUADS):
                dve.wait_ge(s[f"x_in{q}"], 32)
                for n in range(4 * q, 4 * q + 4):
                    step(dve.bn_stats(bn[:, n, :], x_rows[:, n, :]))
                    step(dve.bn_aggr(mv[:, n, :], bn[:, n, :]))
            dve.tensor_scalar(var_col, mv[:, :, 1], EPS_COL, None, ALU.add).then_inc(s["root_in"], 1)
            dve.wait_ge(s["root_in"], 1)
            rsqrt(0, rs_col, var_col, sd_col, tmp_col, None)

            def columns(q):
                for i in range(4):
                    n = 4 * q + i
                    dve.tensor_scalar(x_col[q % 2][:, i, :], x_rows[:, n, :], mv[:, n, 0:1], rs_col[:, n:n + 1],
                                      ALU.subtract, ALU.mult).then_inc(s["xcol_ready"], 1)

            def stack_out(q):
                dve.wait_ge(s["ztr_ready"], 2 * q + 2)
                dve.tensor_copy(z_stack_v[:, 1, :, :, 4 * q:4 * q + 4],
                                bank[5][:].bitcast(fp16).rearrange("p (i h l) -> p l h i", i=4, h=2))\
                    .then_inc(s["zst_dve"], 1)

            columns(0)
            columns(1)
            for q in range(QUADS):
                for h in range(2):
                    dve.wait_ge(s["sq_ready"], 2 * q + h + 1)
                    step(dve.tensor_reduce(sum_tok[:, 8 * h:8 * h + 8], squares[h].rearrange("p (t d) -> p t d", t=8),
                                           AX.X, ALU.add))
                dve.tensor_scalar(var_tok, sum_tok, 1.0 / D_MODEL, EPS_TOK, ALU.mult, ALU.add)\
                    .then_inc(s["root_in"], 1)
                k = q + 1 + (q > 1)
                dve.wait_ge(s["root_in"], k + 1)
                rsqrt(k, rs_tok, var_tok, sd_tok, tmp_tok, None)
                for h in range(2):
                    if q >= 1:
                        dve.wait_ge(s["zlo_ready"], 2 * (q - 1) + h + 1)
                    r = rs_tok[:, 8 * h:8 * h + 8].unsqueeze(2).broadcast_to([P, 8, D_MODEL])
                    dve.tensor_tensor(z_tok[h].rearrange("p (t d) -> p t d", t=8),
                                      bank[2 * (q % 2) + h][:].rearrange("p (t d) -> p t d", t=8), r,
                                      ALU.mult).then_inc(s["ztok_ready"], 1)
                if q + 2 < QUADS:
                    columns(q + 2)
                if q >= 1:
                    stack_out(q - 1)
                if q == 1:
                    dve.wait_ge(s["pool_pair"], 2)
                    step(dve.tensor_reduce(pair_s[:, 32:64], pr[1], AX.X, ALU.add))
                    dve.tensor_scalar(pair_s[:, 32:64], pair_s[:, 32:64], 1.0 / P_DIM, EPS_TOK, ALU.mult, ALU.add)\
                        .then_inc(s["root_in"], 1)
                    dve.wait_ge(s["root_in"], 4)
                    rsqrt(3, pair_s[:, 64:96], pair_s[:, 32:64], pair_s[:, 96:128], pair_s[:, 128:160], s["pair_v"])
            dve.wait_ge(s["pool_pair"], 5)
            dve.transpose(pr[2].rearrange("p i c -> p (i c)"), pr[0].rearrange("p i c -> p (i c)"))\
                .then_inc(s["pair_v"], 1)
            stack_out(QUADS - 1)
            dve.wait_ge(s["pe_bias"], 1)
            dve.tensor_copy(bias_t[0:32, :], bank[6][0:32, 0:256]).then_inc(s["bias_copied"], 1)
            dve.wait_ge(s["bias_copied"], 1)
            dve.tensor_tensor(bias_t[32:64, :], bank[6][0:32, 0:256], bias_t[0:32, :], ALU.subtract)\
                .then_inc(s["bias_copied"], 1)
            for t in v_tile:
                for c in range(2):
                    step(dve.memset(t[:, c, :, :, 32:36].rearrange("p g l h -> p (g l) h"), 0.0))
                    for h in range(GROUP):
                        step(dve.memset(t[32 * h:32 * h + 32, c, :, :, 32 + h].rearrange("p g l -> p (g l)"), 1.0))

            def pair_tokens(j, first=False):
                if not first:
                    dve.wait_ge(s["v_ps"], 4 * j)
                src = z_stack[:].rearrange("p l n -> p (l n)")[:, bass.ds(j * (PAIR * N_SEQ), PAIR * N_SEQ)]
                dve.tensor_copy(z_pair[:].bitcast(fp32), src.bitcast(fp32)).then_inc(s["zpair_ready"], 1)

            def soften(j, c, first=False):
                dve.wait_ge(s["s_ps"], 2 * j + c + 1)
                for g in range(2):
                    dve.tensor_reduce(maxes[:, 2 * c + g, :],
                                      bank[2 * c + g][:].rearrange("p (l m) -> p l m", l=CHUNK), AX.X, ALU.max)\
                        .then_inc(s["max_ready"], 1)
                if not first:
                    dve.wait_ge(s["et_ready"], 2 * j + c - 1)
                for g in range(2):
                    dve.wait_ge(s["max_ready"], 4 * j + 2 * c + g + 1)
                    dve.tensor_tensor(s_exp[:, c, g, :].rearrange("p (l m) -> p l m", l=CHUNK),
                                      bank[2 * c + g][:].rearrange("p (l m) -> p l m", l=CHUNK),
                                      maxes[:, 2 * c + g, :].unsqueeze(2).broadcast_to([P, CHUNK, N_SEQ]),
                                      ALU.subtract).then_inc(s["sub_ready"], 1)

            def turn(j, c, first=False):
                dve.wait_ge(s["exp_ready"], 2 * j + c + 1)
                if not first:
                    dve.wait_ge(s["av_ps"], 2 * j + c - 1)
                dve.transpose(e_t[:, c, :, :].rearrange("p g t -> p (g t)"),
                              s_exp[:, c, :, :].rearrange("p g t -> p (g t)")).then_inc(s["et_ready"], 1)

            def normalise(j, c, first=False):
                dve.wait_ge(s["av_ps"], 2 * j + c + 1)
                av = bank[6][:, 0:4 * 2 * VCOL].rearrange("p (a v) -> p a v", v=VCOL)
                rd = rden[:, c, :].rearrange("p (a h) -> p a h", h=GROUP)
                dve.reciprocal(rd, av[:, :, 32:36]).then_inc(s["rden_ready"], 1)
                dve.wait_ge(s["rden_ready"], 2 * j + c + 1)
                if not first:
                    dve.wait_ge(s["att_ready"], 2 * j)
                dve.tensor_tensor(att_n[:, c, :].rearrange("p (a h d) -> p a h d", h=GROUP, d=D_HEAD),
                                  av[:, :, 0:32].rearrange("p a (h d) -> p a h d", h=GROUP),
                                  rd.unsqueeze(3).broadcast_to([P, 8, GROUP, D_HEAD]),
                                  ALU.mult).then_inc(s["norm_ready"], 1)

            def apply_gate(j, c, par, first=False):
                dve.wait_ge(s["vb_ready"], 2 * j + c + 1)
                dve.wait_ge(s["gate_ready"], j + 1)
                if not first:
                    dve.wait_ge(s["at_ps"], j)
                dve.scalar_tensor_tensor(out=att[:, :, c, :], in0=gate_v[par][:, c, :, :], scalar=1.0,
                                         in1=att_n[:, c, :].rearrange("p (q v) -> p q v", q=4),
                                         op0=ALU.add, op1=ALU.mult).then_inc(s["att_ready"], 1)

            def gate_sum(j, first=False):
                dve.wait_ge(s["g_ps"], j + 1)
                if not first:
                    dve.wait_ge(s["gate_ready"], j)
                dve.tensor_tensor(g_pre[:].rearrange("p (t v) -> p t v", t=8),
                                  bank[7][:].rearrange("p (t v) -> p t v", t=8),
                                  g_row[:].unsqueeze(1).broadcast_to([P, 8, D_MODEL]), ALU.add)\
                    .then_inc(s["gpre_ready"], 1)

            def values_turned(j, c, g, par, early=False):
                dve.wait_ge(s["v_ps"], 4 * j + 2 * c + g + 1)
                if not early:
                    dve.wait_ge(s["av_ps"], 2 * (j - 1))
                dve.transpose(v_tile[par][:, c, g, :, 0:32], bank[4 + g][:].rearrange("p (l m) -> p l m", l=CHUNK))\
                    .then_inc(s["vt_ready"], 1)

            def spread_queries(j, part, first=False):
                src = (q_hi, q_lo)[part]
                dve.wait_ge(s["q_lo_ready"] if part else s["qh_ready"], j + 1)
                if not first:
                    dve.wait_ge(s["s_ps"], 2 * j)
                for h in range(GROUP):
                    dve.tensor_scalar(q_exp[:, part, :, h, :], src[:].rearrange("p (l n) -> p l n", l=CHUNK),
                                      head_mask[:, h:h + 1], None, ALU.mult).then_inc(s["qexp_ready"], 1)

            def add_rows(j):
                dve.wait_ge(s["wo_ps"], j + 1)
                for c in range(2):
                    dst = x_rows[:, :, bass.ds(PAIR * j + CHUNK * c, CHUNK)]
                    dve.scalar_tensor_tensor(
                        out=dst, in0=bank[7][:, 256 * c:256 * c + 256].rearrange("p (l n) -> p n l", l=CHUNK),
                        scalar=bo_col, in1=dst, op0=ALU.add, op1=ALU.add).then_inc(s["x1_ready"], 1)

            def prepare(j, par, first=False, early=False):
                gate_sum(j, first=first)
                values_turned(j, 0, 0, par, early=early)
                values_turned(j, 0, 1, par, early=early)
                spread_queries(j, 0, first=first)
                values_turned(j, 1, 0, par, early=early)
                spread_queries(j, 1, first=first)
                values_turned(j, 1, 1, par, early=early)

            def dve_step(j, par, first=False, second=False, last=False):
                if not last:
                    pair_tokens(j + 1)
                soften(j, 0, first=first)
                if not first:
                    normalise(j - 1, 0, first=second)
                soften(j, 1, first=first)
                if not first:
                    normalise(j - 1, 1, first=second)
                turn(j, 0, first=first)
                if not first:
                    apply_gate(j - 1, 0, 1 - par, first=second)
                    apply_gate(j - 1, 1, 1 - par, first=second)
                turn(j, 1, first=first)
                if not last:
                    prepare(j + 1, 1 - par, early=first)
                if not first:
                    add_rows(j - 1)

            dve.wait_ge(s["zst_act"], QUADS)
            dve.wait_ge(s["zst_dve"], QUADS)
            dve.memset(small[:, 151:152], 0.0).then_inc(s["wprep_ready"], 1)
            pair_tokens(0, first=True)
            prepare(0, 0, first=True, early=True)
            dve_step(0, 0, first=True)
            with dve.Fori(0, PAIRS // 2 - 1) as i:
                dve_step(2 * i + 1, 1)
                dve_step(2 * i + 2, 0)
            dve_step(PAIRS - 1, 1, last=True)
            for c in range(2):
                normalise(PAIRS - 1, c)
            for c in range(2):
                apply_gate(PAIRS - 1, c, 1)
            add_rows(PAIRS - 1)

            step(dve.memset(se_flat[:, 0:L_COL], 0.0))
            step(dve.memset(r_keep, 1.0))
            step(dve.memset(r_keep.rearrange("p (e n) -> p e n", e=EXPERTS)[:, :, 0:1], 0.0))
            step(dve.memset(r_one8, 1.0))
            dve.memset(small[:, 151:152], 0.0).then_inc(s["zero_ready"], 1)
            for n in range(TILES):
                step(dve.bn_stats(bn[:, n, :], x_rows[:, n, :]))
                step(dve.bn_aggr(mv[:, n, :], bn[:, n, :]))
            dve.tensor_scalar(var_col, mv[:, :, 1], EPS_TOK, None, ALU.add).then_inc(s["root_in"], 1)
            dve.wait_ge(s["root_in"], 7)
            rsqrt(6, rs_col, var_col, sd_col, tmp_col, None)
            for n in range(TILES):
                dve.tensor_scalar(xn[:, n, :], x_rows[:, n, :], mv[:, n, 0:1], rs_col[:, n:n + 1],
                                  ALU.subtract, ALU.mult).then_inc(s["xn_ready"], 1)
            dve.wait_ge(s["route_p"], 8)
            step(dve.tensor_copy(iota_f, r_iota128))
            step(dve.tensor_copy(thr_f, r_thr))
            step(dve.tensor_copy(tid_f, r_tid))
            dve.wait_ge(s["logit_ps"], TILES)
            step(dve.tensor_tensor(r_logit, bank[2][:, 0:128].rearrange("p (n e) -> p n e", n=TILES),
                                   rb_row.unsqueeze(1).broadcast_to([P, TILES, EXPERTS]), ALU.add))
            four = [P, TILES, EXPERTS, EXPERTS]
            other, own = r_logit.unsqueeze(2).broadcast_to(four), r_logit.unsqueeze(3).broadcast_to(four)
            step(dve.tensor_tensor(r_gt, other, own, ALU.is_gt))
            step(dve.tensor_tensor(r_eq, other, own, ALU.is_equal))
            step(dve.tensor_tensor(r_eq, r_eq, r_lower.unsqueeze(1).broadcast_to(four), ALU.mult))
            step(dve.tensor_tensor(r_gt, r_gt, r_eq, ALU.add))
            step(dve.tensor_reduce(r_rank, r_gt, AX.X, ALU.add))
            step(dve.tensor_scalar(r_chosen, r_rank, TOP_K - 0.5, None, ALU.is_lt))
            step(dve.tensor_reduce(r_mx, r_logit, AX.X, ALU.max))
            dve.tensor_tensor(r_prob, r_logit, r_mx.unsqueeze(2).broadcast_to([P, TILES, EXPERTS]), ALU.subtract)\
                .then_inc(s["shift_ready"], 1)
            by_expert = r_chosen.rearrange("p n e -> p e n")
            step(dve.tensor_copy(r_sel.rearrange("p (e n) -> p e n", e=EXPERTS), by_expert))
            step(dve.tensor_copy(r_slot.rearrange("p (e n) -> p e n", e=EXPERTS), by_expert))
            step(dve.tensor_tensor_scan(r_scan, r_keep, r_slot, 0.0, ALU.mult, ALU.add))
            dve.tensor_copy(r_incl, r_scan).then_inc(s["sel_ready"], 1)
            dve.wait_ge(s["prob_ready"], 1)
            step(dve.tensor_tensor(r_prob, r_prob, r_chosen, ALU.mult))
            step(dve.tensor_reduce(r_sum, r_prob, AX.X, ALU.add))
            step(dve.reciprocal(r_rs, r_sum))
            step(dve.tensor_tensor(r_prob, r_prob, r_rs.unsqueeze(2).broadcast_to([P, TILES, EXPERTS]), ALU.mult))
            dve.wait_ge(s["route_ps"], 1)
            step(dve.tensor_copy(r_cnt, bank[3][:, 128:136]))
            step(dve.tensor_tensor(r_cmp, r_cnt.unsqueeze(2).broadcast_to([P, EXPERTS, TILES]),
                                   thr_f.unsqueeze(1).broadcast_to([P, EXPERTS, TILES]), ALU.is_gt))
            step(dve.tensor_reduce(r_nb, r_cmp, AX.X, ALU.add))
            step(dve.tensor_tensor_scan(r_cum, r_one8, r_nb, 0.0, ALU.mult, ALU.add))
            step(dve.tensor_tensor(r_base, r_cum, r_nb, ALU.subtract))
            step(dve.tensor_scalar(r_base, r_base, float(SLOTS), None, ALU.mult))
            step(dve.tensor_tensor(r_slot.rearrange("p (e n) -> p e n", e=EXPERTS),
                                   bank[3][:, 0:128].rearrange("p (e n) -> p e n", e=EXPERTS),
                                   r_base.unsqueeze(2).broadcast_to([P, EXPERTS, TILES]), ALU.add))
            slot_v = r_slot.rearrange("p (e n) -> p n e", e=EXPERTS)
            for k in range(TOP_K):
                step(dve.tensor_scalar(r_first, r_rank, float(k), None, ALU.is_equal))
                step(dve.tensor_tensor(r_tmp, r_first, slot_v, ALU.mult))
                step(dve.tensor_reduce(r_slots[:, TILES * k:TILES * k + TILES], r_tmp, AX.X, ALU.add))
                step(dve.tensor_tensor(r_tmp, r_first, r_prob, ALU.mult))
                step(dve.tensor_reduce(r_w[:, TILES * k:TILES * k + TILES], r_tmp, AX.X, ALU.add))
            step(dve.tensor_copy(r_ints[:, 0:32], r_slots))
            step(dve.tensor_scalar(r_ints[:, 32:64], r_ints[:, 0:32], SLOTS - 1, None, ALU.bitwise_and))
            step(dve.tensor_scalar(r_ints[:, 64:96], r_ints[:, 0:32], 7, None, ALU.logical_shift_right))
            step(dve.tensor_copy(r_p, r_ints[:, 32:64]))
            step(dve.tensor_copy(r_b, r_ints[:, 64:96]))
            step(dve.tensor_copy(r_wh, r_w))
            step(dve.tensor_tensor(r_wl, r_w, r_wh, ALU.subtract))
            dve.wait_ge(s["pad_out"], 16)
            step(dve.tensor_tensor(r_place, iota_f.unsqueeze(1).broadcast_to([P, ASSIGN, P]),
                                   r_p.unsqueeze(2).broadcast_to([P, ASSIGN, P]), ALU.is_equal))
            step(dve.tensor_tensor(r_block, iota_f[:, 0:BLOCKS].unsqueeze(1).broadcast_to([P, ASSIGN, BLOCKS]),
                                   r_b.unsqueeze(2).broadcast_to([P, ASSIGN, BLOCKS]), ALU.is_equal))
            for k in range(TOP_K):
                rows = slice(TILES * k, TILES * k + TILES)
                step(dve.tensor_tensor(r_values[:, rows, 0:BLOCKS], r_block[:, rows, :],
                                       tid_f.unsqueeze(2).broadcast_to([P, TILES, BLOCKS]), ALU.mult))
            step(dve.tensor_tensor(r_values[:, :, BLOCKS:2 * BLOCKS], r_block,
                                   r_wh.unsqueeze(2).broadcast_to([P, ASSIGN, BLOCKS]), ALU.mult))
            dve.tensor_tensor(r_values[:, :, 2 * BLOCKS:3 * BLOCKS], r_block,
                              r_wl.unsqueeze(2).broadcast_to([P, ASSIGN, BLOCKS]), ALU.mult)\
                .then_inc(s["onehot_ready"], 1)
            step(dve.tensor_tensor(r_ecmp, iota_f[:, 0:BLOCKS].unsqueeze(2).broadcast_to([P, BLOCKS, EXPERTS]),
                                   r_cum.unsqueeze(1).broadcast_to([P, BLOCKS, EXPERTS]), ALU.is_ge))
            step(dve.tensor_reduce(r_tab[:, 0:BLOCKS], r_ecmp, AX.X, ALU.add))
            step(dve.tensor_scalar(t_expert, r_tab[:, 0:BLOCKS], EXPERTS - 1.0, None, ALU.min))
            dve.wait_ge(s["tab_ps"], 1)
            step(dve.tensor_copy(t_weight, bank[4][:, BLOCKS:2 * BLOCKS]))
            step(dve.tensor_tensor(t_weight, t_weight, bank[4][:, 2 * BLOCKS:3 * BLOCKS], ALU.add))
            tok = r_tab[:, 64:64 + BLOCKS]
            empty = r_tab[:, 128:128 + BLOCKS]
            step(dve.tensor_copy(tok, bank[4][:, 0:BLOCKS]))
            step(dve.tensor_scalar(t_gather, tok, -1.0, 0.0, ALU.add, ALU.max))
            step(dve.tensor_copy(small[:, 150:151], small_i[:, 0:1]))
            step(dve.tensor_scalar(small[:, 150:151], small[:, 150:151], float(TOKENS + 1), None, ALU.add))
            step(dve.tensor_scalar(empty, tok, 0.0, small[:, 150:151], ALU.is_equal, ALU.mult))
            step(dve.tensor_tensor(empty, empty, tok, ALU.add))
            dve.tensor_scalar(t_scatter, empty, -1.0, None, ALU.add).then_inc(s["tables_ready"], 1)
            dve.wait_ge(s["tables_ready"], 1)
            dve.wait_ge(s["bias_rows"], 48)

            def tokens_low(b, par, first=False):
                dve.wait_ge(s["xh_ready"], b + 1)
                dve.tensor_tensor(x_lo[par], bank[4][:, 0:L_COL].rearrange("p (c t) -> p c t", c=2), x_hi[par],
                                  ALU.subtract).then_inc(s["xl_ready"], 1)

            def expert_of(b):
                return dve.value_load(t_expert[0:1, bass.ds(b, 1)], min_val=0, max_val=EXPERTS - 1)

            def gate_bias(b, par, e, first=False):
                dve.wait_ge(s["gu_ps"], 2 * b + 1)
                if not first:
                    dve.wait_ge(s["silu_ready"], b - 1)
                dve.tensor_tensor(g_sum[par], bank[2 * par][:], gate_b_all[:, bass.ds(e * FF, FF)], ALU.add)\
                    .then_inc(s["gadd_ready"], 1)

            def up_bias(b, par, e, first=False):
                dve.wait_ge(s["gu_ps"], 2 * b + 2)
                dve.tensor_tensor(u_sum[par], bank[2 * par + 1][:], up_b_all[:, bass.ds(e * FF, FF)], ALU.add)\
                    .then_inc(s["uadd_ready"], 1)

            def gated(b, par, first=False):
                dve.wait_ge(s["silu_ready"], b + 1)
                dve.wait_ge(s["uadd_ready"], b + 1)
                if not first:
                    dve.wait_ge(s["ht_ps"], b - 1)
                dve.tensor_tensor(h_sb[par], g_silu[par], u_sum[par], ALU.mult).then_inc(s["h_ready"], 1)

            def hidden_low(b, par):
                dve.wait_ge(s["hh_ready"], b + 1)
                dve.tensor_tensor(h_lo[par], bank[5][:].rearrange("p (c t) -> p c t", c=4), h_hi[par],
                                  ALU.subtract).then_inc(s["hl_ready"], 1)

            def down_bias(b, par, e, first=False):
                dve.wait_ge(s["y_ps"], b + 1)
                if not first:
                    dve.wait_ge(s["y_ready"], b - 1)
                dve.tensor_tensor(y_sum[par], bank[6][:, 0:L_COL], down_b_all[:, bass.ds(e * L_COL, L_COL)], ALU.add)\
                    .then_inc(s["yadd_ready"], 1)

            def dve_block(b, par, first=False, more=2):
                if more >= 1:
                    e1 = expert_of(b + 1)
                    gate_bias(b + 1, 1 - par, e1, first=first)
                hidden_low(b, par)
                if more >= 1:
                    up_bias(b + 1, 1 - par, e1)
                    gated(b + 1, 1 - par, first=first)
                if more >= 2:
                    tokens_low(b + 2, par)
                down_bias(b, par, expert_of(b), first=first)

            tokens_low(0, 0)
            tokens_low(1, 1)
            e0 = expert_of(0)
            gate_bias(0, 0, e0, first=True)
            up_bias(0, 0, e0)
            gated(0, 0, first=True)
            dve_block(0, 0, first=True)
            with dve.Fori(0, BODY) as i:
                dve_block(2 * i + 1, 1)
                dve_block(2 * i + 2, 0)
            dve_block(BLOCKS - 2, 1, more=1)
            dve_block(BLOCKS - 1, 0, more=0)


_INS = ['x', 'L0_conv_pairs', 'L0_conv_ln_m_g', 'L0_conv_ln_m_b', 'L0_conv_ln_p_g', 'L0_conv_ln_p_b', 'L0_conv_Wq',
        'L0_conv_Wk', 'L0_conv_Wv', 'L0_conv_Wg', 'L0_conv_bg', 'L0_conv_Wb', 'L0_conv_Wo', 'L0_conv_bo',
        'L0_ffn_router_w', 'L0_ffn_router_b', 'L0_ffn_gate_w', 'L0_ffn_gate_b', 'L0_ffn_up_w', 'L0_ffn_up_b',
        'L0_ffn_down_w', 'L0_ffn_down_b']


def kernel(**inputs):
    import numpy as _np
    import concourse.bacc as _bacc
    from concourse import mybir as _mybir
    from concourse.bass_utils import run_bass_kernel_spmd as _run

    nc = _bacc.Bacc("TRN2", target_bir_lowering=False, num_devices=1)
    arrays, args = {}, []
    for name in _INS:
        a = _np.ascontiguousarray(inputs[name])
        arrays[f"in_{name}_dram"] = a
        args.append(nc.dram_tensor(f"in_{name}_dram", a.shape, _mybir.dt.from_np(a.dtype), kind="ExternalInput").ap())
    args.append(nc.dram_tensor("out_dram", (TOKENS + SLOTS, L_COL), _mybir.dt.float32, kind="ExternalOutput").ap())
    build(nc, *args)
    r = _run(nc, [arrays], core_ids=[0])
    return r.results[0]["out_dram"][:TOKENS].reshape(1, D_MODEL, N_SEQ, L_COL)
```

```python
import concourse.bass as bass
from concourse import mybir
from contextlib import ExitStack

D_MODEL = 64
N_SEQ = 32
L_COL = 256
HEADS = 8
D_HEAD = D_MODEL // HEADS
P_DIM = 32
EXPERTS = 8
FF = 512
P = 128

N_HALF = N_SEQ // 2
QUADS = N_HALF // 4
L_HALF = L_COL // 2

GROUP = 4
CHUNK = 16
PAIR = 2 * CHUNK
PAIRS = L_COL // PAIR
TOK = CHUNK * N_SEQ
VCOL = GROUP * D_HEAD + GROUP
Q_SCALE = float(D_HEAD) ** -0.5

TOKENS = D_MODEL * N_SEQ
TILES = TOKENS // P
TOP_K = 2
SLOTS = P
BLOCKS = (TOKENS * TOP_K + EXPERTS * (SLOTS - 1)) // SLOTS
BODY = (BLOCKS - 3) // 2
W_EXP = 2 * 2 * FF + (FF // P) * L_COL
W_PIECE = W_EXP // 3
ASSIGN = TILES * TOP_K

EPS_COL = 1e-6
EPS_TOK = 1e-5


def build(nc, x, pairs, ln_m_g, ln_m_b, ln_p_g, ln_p_b, Wq, Wk, Wv, Wg, bg, Wb, Wo, bo,
          router_w, router_b, gate_w, gate_b, up_w, up_b, down_w, down_b, out):
    fp32, fp16, i32 = mybir.dt.float32, mybir.dt.float16, mybir.dt.int32
    ALU, ACT, AX = mybir.AluOpType, mybir.ActivationFunctionType, mybir.AxisListType

    ctx = ExitStack()
    with ctx:
        def sb(name, shape, dt=fp32):
            return ctx.enter_context(nc.sbuf_tensor(name, shape, dt))

        def sem(name):
            return ctx.enter_context(nc.semaphore(name))

        x_rows = sb("x_rows", [P, N_HALF, L_COL])
        z_stack = sb("z_stack", [P, L_COL, N_SEQ], fp16)
        w_exp = sb("w_exp", [P, EXPERTS * 2 * W_EXP], fp16)
        w_stage = sb("w_stage", [P, 3, W_PIECE])

        z_pair = sb("z_pair", [P, PAIR * N_SEQ], fp16)
        proj = sb("proj", [P, TOK])
        q_hi = sb("q_hi", [P, TOK], fp16)
        q_lo = sb("q_lo", [P, TOK], fp16)
        k_hi = sb("k_hi", [P, TOK], fp16)
        k_lo = sb("k_lo", [P, TOK], fp16)
        q_exp = sb("q_exp", [P, 2, CHUNK, GROUP, N_SEQ], fp16)
        s_exp = sb("s_exp", [P, 2, 2, TOK])
        e_t = sb("e_t", [P, 2, 2, TOK])
        v_exp = sb("v_exp", [P, 2, 2 * 2 * CHUNK * VCOL])
        gate = sb("gate", [P, 2, 2 * 4 * D_MODEL])
        g_pre = sb("g_pre", [P, 2 * 4 * D_MODEL])
        att_n = sb("att_n", [P, 2, 4 * D_MODEL])
        att = sb("att", [P, 4, 2, D_MODEL])
        att_t = sb("att_t", [P, TOK])

        ident = sb("ident", [P, P])
        ident_h = sb("ident_h", [P, P], fp16)
        ones_h = sb("ones_h", [P, P], fp16)
        w_hi = sb("w_hi", [P, 448], fp16)
        w_lo = sb("w_lo", [P, 448], fp16)
        bias_t = sb("bias_t", [64, 2 * P], fp16)
        pick = sb("pick", [64, N_SEQ], fp16)
        g_row = sb("g_row", [P, D_MODEL])
        v_row = sb("v_row", [P, D_MODEL])
        head_mask = sb("head_mask", [P, GROUP])
        small = sb("small", [P, 216])
        small_i = sb("small_i", [P, 4], i32)
        maxes = sb("maxes", [P, 4, CHUNK])
        rden = sb("rden", [P, 2, 32])
        wo_pad = sb("wo_pad", [P, 2, D_MODEL])
        center = gate[:, 1, 0:P]
        before = k_lo[:, 384:512]
        bank = [ctx.enter_context(nc.psum_tensor(f"bank{i}", [P, 512], fp32)) for i in range(8)]

        et_flat = e_t[:].rearrange("p a b c -> p (a b c)")
        se_flat = s_exp[:].rearrange("p a b c -> p (a b c)")
        qe_flat = q_exp[:].rearrange("p a b c d -> p (a b c d)")
        ve_flat = v_exp[:].rearrange("p a b -> p (a b)")
        x_col = [et_flat[:, 1024 * i:1024 * (i + 1)].rearrange("p (n l) -> p n l", n=4) for i in range(2)]
        squares = [se_flat[:, 512 * h:512 * (h + 1)] for h in range(2)]
        z_tok = [se_flat[:, 1024 + 512 * h:1024 + 512 * (h + 1)] for h in range(2)]
        z_parts = [qe_flat[:, 1024 * h:1024 * (h + 1)].rearrange("p (t s d) -> p t s d", t=8, s=2) for h in range(2)]
        w_raw = ve_flat[:, 0:256]
        w_fold = ve_flat[:, 256:704]
        pair_g = ve_flat[0:32, 704:736]
        pair_b = ve_flat[0:32, 736:768]
        bg_row = ve_flat[:, 768:832]
        b_wide = ve_flat[0:64, 832:960]
        wb_sb = ve_flat[0:32, 960:968]
        pr = [ve_flat[0:32, 1024 * i:1024 * (i + 1)].rearrange("p (i c) -> p i c", c=P_DIM) for i in (1, 2, 3)]
        pair_s = att_n[0:32, :, :].rearrange("p a b -> p (a b)")
        bn = g_pre[:, 0:96].rearrange("p (n s) -> p n s", s=6)
        mv = small[:, 0:32].rearrange("p (n s) -> p n s", s=2)
        neg_mean = g_pre[:, 96:112]
        g_col, b_col, bo_col, qb_col, kb_col = (small[:, 144 + i:145 + i] for i in range(5))
        v_tile = [v_exp[:, i, :].rearrange("p (s g l c) -> p s g l c", s=2, g=2, c=VCOL) for i in range(2)]
        gate_v = [gate[:, i, :].rearrange("p (s q c) -> p s q c", s=2, q=4) for i in range(2)]

        N_PAR, N_CENTER, N_ONES, N_PREP = 17, 5, 2 * 2 * (1 + GROUP), 3 + 2 + GROUP + 4
        var_col, sd_col, rs_col, tmp_col = (small[:, 32 + 16 * i:48 + 16 * i] for i in range(4))
        sum_tok, var_tok, sd_tok = (small[:, 96 + 16 * i:112 + 16 * i] for i in range(3))
        rs_tok, tmp_tok = (small[:, 160 + 16 * i:176 + 16 * i] for i in range(2))
        rw_sb = small[:, 192:208].rearrange("p (c e) -> p c e", c=2)
        rb_row = small[:, 208:216]
        wo_pad_raw = g_pre[:, 128:192]
        z_stack_v = z_stack[:].rearrange("p (a l) (h n) -> p a l h n", a=2, h=2)

        xn = z_stack[:].rearrange("p l n -> p (l n)").bitcast(fp32).rearrange("p (n l) -> p n l", n=N_HALF)
        gate_b_all = x_rows[:].rearrange("p n l -> p (n l)")
        up_b_all = xn.rearrange("p n l -> p (n l)")
        down_b_all = et_flat
        xn_t = [et_flat[:, 512 * i:512 * i + 512] for i in range(2)]
        ws_flat = w_stage[:].rearrange("p k w -> p (k w)")
        qe_words = qe_flat.bitcast(fp32)

        def two(flat, at, size, dt=None, parts=None):
            out2 = []
            for i in range(2):
                t = flat[:, at + size * i:at + size * (i + 1)]
                t = t.bitcast(dt) if dt else t
                out2.append(t.rearrange("p (c t) -> p c t", c=parts) if parts else t)
            return out2

        xg = two(ws_flat, 0, L_COL)
        x_hi = two(ws_flat, 512, P, fp16, 2)
        x_lo = two(ws_flat, 768, P, fp16, 2)
        y_sum = two(ws_flat, 1024, L_COL)
        yw = two(ws_flat, 1536, L_COL)
        h_sb = two(ws_flat, 2048, FF)
        g_sum = two(ve_flat, 0, FF)
        g_silu = two(ve_flat, 1024, FF)
        u_sum = two(ve_flat, 2048, FF)
        h_hi = two(qe_words, 0, FF // 2, fp16, 4)
        h_lo = two(qe_words, 512, FF // 2, fp16, 4)
        r_gt = qe_words[:, 0:1024].rearrange("p (n e k) -> p n e k", n=TILES, e=EXPERTS)
        r_eq = qe_words[:, 1024:2048].rearrange("p (n e k) -> p n e k", n=TILES, e=EXPERTS)
        r_place = se_flat.bitcast(fp16).rearrange("p (a t) -> p a t", a=ASSIGN)
        r_values = ve_flat[:, 0:ASSIGN * 3 * BLOCKS // 2].bitcast(fp16).rearrange("p (a t) -> p a t", a=ASSIGN)
        r_block = ve_flat[:, 1872:1872 + ASSIGN * BLOCKS // 2].bitcast(fp16).rearrange("p (a t) -> p a t", a=ASSIGN)
        r_iota128 = att_t[:, 0:128].bitcast(i32)
        iota_f = att_t[:, 128:256]
        r_thr = att_t[:, 256:272].bitcast(i32)
        thr_f = att_t[:, 272:288]
        r_tid = att_t[:, 288:304].bitcast(i32)
        tid_f = att_t[:, 304:320]
        r_lower = att_t[:, 320:384].rearrange("p (e k) -> p e k", e=EXPERTS)
        an_flat = att_n[:].rearrange("p c v -> p (c v)")
        at_flat = att[:].rearrange("p q c v -> p (q c v)")
        r_logit, r_rank, r_chosen, r_prob3 = (an_flat[:, 128 * i:128 * i + 128].rearrange("p (n e) -> p n e", n=TILES)
                                              for i in range(4))
        r_prob = r_prob3
        r_sel = at_flat[:, 0:64].bitcast(fp16)
        r_incl = at_flat[:, 64:128].bitcast(fp16)
        r_scan, r_keep, r_slot = (at_flat[:, 128 * i:128 * i + 128] for i in (1, 2, 3))
        r_first = proj[:, 0:128].rearrange("p (n e) -> p n e", n=TILES)
        r_tmp = proj[:, 128:256].rearrange("p (n e) -> p n e", n=TILES)
        r_slots, r_w = proj[:, 256:288], proj[:, 288:320]
        r_mx, r_sum, r_rs = (proj[:, 320 + 16 * i:336 + 16 * i] for i in range(3))
        r_cnt, r_nb, r_cum, r_base = (proj[:, 368 + 8 * i:376 + 8 * i] for i in range(4))
        r_p, r_b, r_wl = (proj[:, 400 + 32 * i:432 + 32 * i] for i in range(3))
        r_one8 = proj[:, 496:504]
        r_cmp = k_hi[:].bitcast(fp32)[:, 0:128].rearrange("p (e k) -> p e k", e=EXPERTS)
        r_ints = q_hi[:].bitcast(i32)
        r_wh = q_lo[:, 0:32]
        r_ecmp = g_pre[:, 0:BLOCKS * EXPERTS].rearrange("p (b e) -> p b e", b=BLOCKS)
        r_tab = k_lo[:].bitcast(fp32)
        g_idx = [r_ints[:, 128 + i:129 + i] for i in range(2)]
        s_idx = [r_ints[:, 130 + i:131 + i] for i in range(2)]
        ga_flat = gate[:].rearrange("p a b -> p (a b)")
        t_gather, t_scatter, t_expert = (ga_flat[:, 64 * i:64 * i + BLOCKS].bitcast(i32) for i in range(3))
        t_weight = ga_flat[:, 192:192 + BLOCKS]

        def steps(eng, signal):
            count = [0]

            def step(ins):
                ins.then_inc(signal, 1)
                count[0] += 1
                eng.wait_ge(signal, count[0])
                return count[0]
            return step

        names = """xcol_act wide_ready pair_par_in w_prep ones_ready stats_ready mean_ready negm_ready x_in0 x_in1 x_in2 x_in3 par_in pairs_in  
            const_p const_v dve_step   pe_prep pe_bias xcol_dve cen_ready sq_ready
            ztok_ready zhi_ready zlo_ready ztr_ready zst_act zst_dve pool_pair
            zpair_ready q_ps k_ps g_ps v_ps s_ps av_ps at_ps wo_ps
            qf_ready qh_ready kf_ready kh_ready gate_ready exp_ready att_t_ready w_hi_done
            q_lo_ready k_lo_ready vb_ready w_lo_done
            max_ready sub_ready et_ready rden_ready norm_ready att_ready gpre_ready qexp_ready vt_ready x1_ready
            xn_ready rt_ps rt_sb logit_ps   route_ps onehot_ps rows_out x1_out
            bias_rows tables_ready gcol_ready scol_ready x_got0 x_got1 y_scattered
            xt_ps xh_ready xl_ready gu_ps gadd_ready silu_ready uadd_ready h_ready ht_ps hh_ready hl_ready
            y_ps yadd_ready y_ready zero_ready pad_out tab_ps pair_v route_p vec_copied bias_copied sel_ready
            onehot_ready r_in w_in0 w_in1 w_in2 root_in root_out shift_ready prob_ready""".split()
        s = {n: sem(n) for n in names}

        token_rows = nc.dram_tensor("token_rows", (TOKENS, L_COL), fp32, kind="Internal").ap()
        block = ctx.enter_context(nc.Block())
        x_view = x[0].rearrange("d (h n) l -> h d n l", h=2)

        @block.sync
        def _(sp):
            for q in range(QUADS):
                for h in range(2):
                    sp.dma_start(x_rows[64 * h:64 * h + 64, 4 * q:4 * q + 4, :],
                                 x_view[h, :, 4 * q:4 * q + 4, :]).then_inc(s[f"x_in{q}"], 16)
            for h in range(2):
                rows = slice(64 * h, 64 * h + 64)
                for k, w in enumerate((Wq, Wk, Wv, Wg)):
                    sp.dma_start(w_raw[rows, 64 * k:64 * k + 64], w).then_inc(s["par_in"], 16)
                for col, v in ((g_col, ln_m_g), (b_col, ln_m_b), (bo_col, bo)):
                    sp.dma_start(col[rows, :], v.rearrange("(d a) -> d a", a=1)).then_inc(s["par_in"], 16)
                sp.dma_start(wo_pad_raw[rows, :], Wo).then_inc(s["par_in"], 16)
            sp.dma_start(bg_row, bg.partition_broadcast(P)).then_inc(s["par_in"], 16)
            sp.dma_start(rw_sb, router_w.rearrange("(c p) e -> p c e", p=P)).then_inc(s["r_in"], 16)
            sp.dma_start(rb_row, router_b.partition_broadcast(P)).then_inc(s["r_in"], 16)
            for e in range(EXPERTS):
                parts = (gate_w[e].rearrange("(c p) i -> p c i", p=P), up_w[e].rearrange("(c p) i -> p c i", p=P),
                         down_w[e].rearrange("(c p) l -> p c l", p=P))
                for k in range(3):
                    if e >= 1:
                        sp.wait_ge(s["w_hi_done"], 3 * (e - 1) + k + 1)
                        sp.wait_ge(s["w_lo_done"], 3 * (e - 1) + k + 1)
                    c = 2 if k < 2 else 4
                    sp.dma_start(w_stage[:, k, :].rearrange("p (c i) -> p c i", c=c),
                                 parts[k]).then_inc(s[f"w_in{k}"], 16)
            sp.wait_ge(s["zero_ready"], 1)
            sp.dma_start(out[TOKENS:TOKENS + SLOTS, :], se_flat[:, 0:L_COL]).then_inc(s["pad_out"], 16)
            o_view = out[0:TOKENS, :].rearrange("(d h n) l -> h d n l", h=2, n=N_HALF)
            sp.wait_ge(s["x1_ready"], 2 * PAIRS)
            for h in range(2):
                sp.dma_start(o_view[h], x_rows[64 * h:64 * h + 64, :, :]).then_inc(s["x1_out"], 16)
            r_view = token_rows.rearrange("(d h n) l -> h d n l", h=2, n=N_HALF)
            sp.wait_ge(s["xn_ready"], TILES)
            for h in range(2):
                sp.dma_start(r_view[h], xn[64 * h:64 * h + 64, :, :]).then_inc(s["rows_out"], 16)
            sp.wait_ge(s["x1_out"], 32)
            sp.wait_ge(s["xn_ready"], TILES)
            sp.dma_start(gate_b_all, gate_b.rearrange("e i -> (e i)").partition_broadcast(P)).then_inc(s["bias_rows"], 16)
            sp.wait_ge(s["rt_ps"], 8)
            sp.wait_ge(s["rows_out"], 32)
            sp.dma_start(up_b_all, up_b.rearrange("e i -> (e i)").partition_broadcast(P)).then_inc(s["bias_rows"], 16)
            sp.wait_ge(s["logit_ps"], TILES)
            sp.dma_start(down_b_all, down_b.rearrange("e l -> (e l)").partition_broadcast(P)).then_inc(s["bias_rows"], 16)
            sp.wait_ge(s["x1_out"], 32)
            sp.wait_ge(s["pad_out"], 16)
            sp.wait_ge(s["y_scattered"], 16 * BLOCKS)

        @block.gpsimd
        def _(pool):
            const = steps(pool, s["const_p"])

            def eye(t):
                const(pool.memset(t, 0.0))
                const(pool.affine_select(out=t, in_=t, compare_op=ALU.not_equal, fill=1.0, base=0,
                                         pattern=[[-1, t.shape[1]]], channel_multiplier=1))
            eye(ident[:])
            eye(ident_h[:])
            for h in range(2):
                eye(pick[32 * h:32 * h + 32, :])
            const(pool.iota(small_i[:, 0:1], pattern=[[0, 1]], base=0, channel_multiplier=1))
            mean_b = pair_s[:, 0:32].unsqueeze(2).broadcast_to([32, N_SEQ, P_DIM])
            rstd_b = pair_s[:, 64:96].unsqueeze(2).broadcast_to([32, N_SEQ, P_DIM])
            pair = steps(pool, s["pool_pair"])
            pool.wait_ge(s["pair_v"], 1)
            pair(pool.tensor_tensor(pr[0], pr[0], mean_b, ALU.subtract))
            pair(pool.tensor_tensor(pr[1], pr[0], pr[0], ALU.mult))
            prep = steps(pool, s["w_prep"])
            prep(pool.memset(w_fold, 0.0))
            prep(pool.memset(w_lo[64:128, :], 0.0))
            prep(pool.memset(wo_pad[:], 0.0))
            pool.wait_ge(s["pair_par_in"], 48)
            pool.wait_ge(s["pair_v"], 2)
            pair(pool.tensor_tensor(pr[0], pr[0], rstd_b, ALU.mult))
            pair(pool.tensor_tensor(pr[0], pr[0], pair_g.unsqueeze(1).broadcast_to([32, N_SEQ, P_DIM]), ALU.mult))
            pair(pool.tensor_tensor(pr[0], pr[0], pair_b.unsqueeze(1).broadcast_to([32, N_SEQ, P_DIM]), ALU.add))

            def prepare_weights():
                pool.wait_ge(s["par_in"], 16 * N_PAR)
                prep(pool.tensor_scalar(w_fold[:, 0:128], w_raw[:, 0:128], g_col, None, ALU.mult))
                prep(pool.tensor_scalar(w_fold[:, 384:448], w_raw[:, 192:256], g_col, None, ALU.mult))
                for h in range(GROUP):
                    c0 = (GROUP * D_HEAD + D_HEAD) * h
                    prep(pool.tensor_scalar(
                        w_fold[:, 128:384].rearrange("p (g r) -> p g r", g=2)[:, :, c0:c0 + D_HEAD],
                        w_raw[:, 128:192].rearrange("p (g r) -> p g r", g=2)[:, :, 8 * h:8 * h + 8],
                        g_col, None, ALU.mult))
                prep(pool.tensor_copy(w_hi[:], w_fold))
                prep(pool.tensor_tensor(w_lo[0:64, :], w_fold[0:64, :], w_hi[0:64, :], ALU.subtract))
                for c in range(2):
                    rows = slice(64 * c, 64 * c + 64)
                    prep(pool.tensor_scalar(wo_pad[rows, c, :], wo_pad_raw[rows, :], 0.5, None, ALU.mult))

            for q in range(QUADS):
                for h in range(2):
                    t = 2 * q + h
                    pool.wait_ge(s["zhi_ready"], t + 1)
                    pool.tensor_tensor(z_parts[h][:, :, 1, :], z_tok[h].rearrange("p (t d) -> p t d", t=8),
                                       z_parts[h][:, :, 0, :], ALU.subtract).then_inc(s["zlo_ready"], 1)
                if q == 0:
                    prepare_weights()

            def parts_low(j):
                pool.wait_ge(s["qh_ready"], j + 1)
                pool.tensor_tensor(q_lo[:], proj[:], q_hi[:], ALU.subtract).then_inc(s["q_lo_ready"], 1)
                pool.wait_ge(s["kh_ready"], j + 1)
                pool.tensor_tensor(k_lo[:], att_t[:], k_hi[:], ALU.subtract).then_inc(s["k_lo_ready"], 1)

            def value_bias(j, c):
                pool.wait_ge(s["norm_ready"], 2 * j + c + 1)
                t = att_n[:, c, :].rearrange("p (q v) -> p q v", q=4)
                pool.tensor_tensor(t, t, v_row[:].unsqueeze(1).broadcast_to([P, 4, D_MODEL]),
                                   ALU.add).then_inc(s["vb_ready"], 1)

            def weights_low(e, pieces):
                for k in pieces:
                    pool.wait_ge(s["w_hi_done"], 3 * e + k + 1)
                    hi = w_exp[:, bass.ds(e * 2 * W_EXP + k * W_PIECE, W_PIECE)]
                    lo = w_exp[:, bass.ds(e * 2 * W_EXP + W_EXP + k * W_PIECE, W_PIECE)]
                    pool.tensor_tensor(lo, w_stage[:, k, :], hi, ALU.subtract).then_inc(s["w_lo_done"], 1)

            def pool_step(j, first=False, last=False):
                weights_low(j, [0])
                if not first:
                    value_bias(j - 1, 0)
                if not last:
                    parts_low(j + 1)
                if not first:
                    value_bias(j - 1, 1)
                weights_low(j, [1, 2])

            parts_low(0)
            ones = steps(pool, s["ones_ready"])
            for t in v_tile:
                for c in range(2):
                    ones(pool.memset(t[:, c, :, :, 32:36].rearrange("p g l h -> p (g l) h"), 0.0))
                    for h in range(GROUP):
                        ones(pool.memset(t[32 * h:32 * h + 32, c, :, :, 32 + h].rearrange("p g l -> p (g l)"), 1.0))
            pool_step(0, first=True)
            with pool.Fori(0, PAIRS // 2 - 1) as i:
                pool_step(2 * i + 1)
                pool_step(2 * i + 2)
            pool_step(PAIRS - 1, last=True)
            value_bias(PAIRS - 1, 0)
            value_bias(PAIRS - 1, 1)

            pool.wait_ge(s["x1_ready"], 2 * PAIRS)
            n_r = [0]

            def table(ins):
                ins.then_inc(s["route_p"], 1)
                n_r[0] += 1
                pool.wait_ge(s["route_p"], n_r[0])
            table(pool.memset(before, 0.0))
            table(pool.affine_select(out=before, in_=before, compare_op=ALU.is_ge, fill=-1.0, base=-1,
                                     pattern=[[1, P]], channel_multiplier=-1))
            table(pool.iota(r_iota128, pattern=[[1, P]], base=0, channel_multiplier=0))
            table(pool.iota(r_thr, pattern=[[P, TILES]], base=0, channel_multiplier=0))
            for h in range(2):
                table(pool.iota(r_tid[64 * h:64 * h + 64, :], pattern=[[1, TILES]], base=1 + N_HALF * h,
                                channel_multiplier=N_SEQ))
            table(pool.memset(r_lower, 1.0))
            table(pool.affine_select(out=r_lower, in_=r_lower, compare_op=ALU.is_gt, fill=0.0, base=0,
                                     pattern=[[1, EXPERTS], [-1, EXPERTS]], channel_multiplier=0))

            pool.wait_ge(s["tables_ready"], 1)
            pool.wait_ge(s["rows_out"], 32)
            pool.wait_ge(s["x1_out"], 32)
            pool.wait_ge(s["pad_out"], 16)

            hold, one_word = [small[0:1, 152 + i:153 + i] for i in range(4)], t_weight[0:1, 0:1]

            def gather(turn, par, first=False):
                b = 2 * turn + par
                if not first:
                    pool.wait_ge(s["xt_ps"], b - 1)
                    pool.wait_ge(s[f"x_got{par}"], 16 * turn)
                    pool.wait_ge(s["gcol_ready"], b)
                    pool.tensor_tensor(hold[0], one_word, one_word, ALU.mult)
                pool.tensor_copy(g_idx[par], t_gather[:, bass.ds(b, 1)]).then_inc(s["gcol_ready"], 1)
                pool.wait_ge(s["gcol_ready"], b + 1)
                pool.tensor_tensor(hold[1], one_word, one_word, ALU.mult)
                pool.indirect_dma_start(xg[par], None, token_rows, bass.IndirectOffsetOnAxis(g_idx[par], 0))\
                    .then_inc(s[f"x_got{par}"], 16)

            def scatter(b, par, first=False):
                if not first:
                    pool.wait_ge(s["y_scattered"], 16 * b)
                    pool.wait_ge(s["scol_ready"], b)
                    pool.tensor_tensor(hold[2], one_word, one_word, ALU.mult)
                pool.tensor_copy(s_idx[par], t_scatter[:, bass.ds(b, 1)]).then_inc(s["scol_ready"], 1)
                pool.wait_ge(s["scol_ready"], b + 1)
                pool.wait_ge(s["y_ready"], b + 1)
                pool.tensor_tensor(hold[3], one_word, one_word, ALU.mult)
                pool.indirect_dma_start(out, bass.IndirectOffsetOnAxis(s_idx[par], 0), yw[par], None,
                                        compute_op=ALU.add).then_inc(s["y_scattered"], 16)

            gather(0, 0, first=True)
            gather(0, 1, first=True)
            gather(1, 0)
            gather(1, 1)
            scatter(0, 0, first=True)
            with pool.Fori(0, BODY - 1) as i:
                gather(i + 2, 0)
                scatter(2 * i + 1, 1)
                gather(i + 2, 1)
                scatter(2 * i + 2, 0)
            gather(BODY + 1, 0)
            for b in range(2 * BODY - 1, BLOCKS):
                scatter(b, b % 2)
        @block.tensor
        def _(pe):
            def fold_vectors():
                pe.wait_ge(s["wide_ready"], 1)
                for h in range(2):
                    for k in range(2):
                        pe.matmul(bank[7][64 * h:64 * h + 64, k:k + 1], w_raw[0:64, 64 * k:64 * k + 64],
                                  b_col[0:64, :], start=True, stop=True)
                pe.matmul(bank[6][:, 0:128], b_wide, w_raw[0:64, 128:256], start=True, stop=True)\
                    .then_inc(s["pe_prep"], 1)

            def pair_bias():
                pe.wait_ge(s["pair_v"], 3)
                pe.wait_ge(s["vec_copied"], 1)
                out_v = bank[6][0:32, 0:HEADS * N_SEQ].rearrange("p (h i) -> p h i", i=N_SEQ)
                for i in range(N_SEQ):
                    mm = pe.matmul(out_v[:, :, i], pr[2][:, i, :], wb_sb, start=True, stop=True)
                mm.then_inc(s["pe_bias"], 1)

            def centre(q):
                if q == 0:
                    pe.wait_ge(s["xcol_dve"], 4)
                else:
                    pe.wait_ge(s["xcol_act"], 4 * q)
                if q == 0:
                    pe.wait_ge(s["const_v"], N_CENTER)
                for h in range(2):
                    if q >= 2:
                        pe.wait_ge(s["ztok_ready"], 2 * (q - 2) + h + 1)
                    for i in range(4):
                        mm = pe.matmul(bank[2 * (q % 2) + h][:, P * i:P * i + P],
                                       x_col[q % 2][:, i, L_HALF * h:L_HALF * h + L_HALF], center,
                                       start=True, stop=True)
                    mm.then_inc(s["cen_ready"], 1)

            def stack_tokens(q):
                for h in range(2):
                    pe.wait_ge(s["zlo_ready"], 2 * q + h + 1)
                    if q >= 1:
                        pe.wait_ge(s["zst_act"] if h == 0 else s["zst_dve"], q)
                    dst = bank[4 + h][:].bitcast(fp16)
                    for t in range(8):
                        mm = pe.transpose(dst[:, P * t:P * t + P], z_parts[h][:, t, :, :].rearrange("p s d -> p (s d)"),
                                          ident_h[:])
                    mm.then_inc(s["ztr_ready"], 1)

            pe.wait_ge(s["const_p"], 9)
            centre(0)
            centre(1)
            stack_tokens(0)
            centre(2)
            fold_vectors()
            stack_tokens(1)
            centre(3)
            pair_bias()
            stack_tokens(2)
            stack_tokens(3)

            SC = [[bank[0], bank[1]], [bank[2], bank[3]]]
            PJ = [bank[4], bank[5]]
            AVB, MS = bank[6], bank[7]

            def project(j, first=False):
                pe.wait_ge(s["zpair_ready"], j + 1)
                if first:
                    pe.wait_ge(s["w_prep"], N_PREP)
                    pe.wait_ge(s["zst_act"], QUADS)
                    pe.wait_ge(s["zst_dve"], QUADS)
                if not first:
                    pe.wait_ge(s["vt_ready"], 4 * (j - 1) + 3)
                for k, ready in ((0, "q_ps"), (1, "k_ps")):
                    if k == 1 and not first:
                        pe.wait_ge(s["vt_ready"], 4 * j)
                    for c in range(2):
                        for w, st in ((w_hi, True), (w_lo, False)):
                            mm = pe.matmul(PJ[k][64 * c:64 * c + 64, :], w[:, 64 * k:64 * k + 64],
                                           z_pair[:, TOK * c:TOK * c + TOK], start=st, stop=not st)
                    mm.then_inc(s[ready], 1)

            def gates(j, first=False):
                if not first:
                    pe.wait_ge(s["gpre_ready"], j)
                for t in range(8):
                    for w, st in ((w_hi, True), (w_lo, False)):
                        mm = pe.matmul(MS[:, 64 * t:64 * t + 64], z_pair[:, P * t:P * t + P], w[:, 384:448],
                                       start=st, stop=not st)
                mm.then_inc(s["g_ps"], 1)

            def values(j, c):
                for g in range(2):
                    if c == 0:
                        pe.wait_ge(s["qf_ready"] if g == 0 else s["kf_ready"], j + 1)
                    else:
                        pe.wait_ge(s["vt_ready"], 4 * j + g + 1)
                    for w, st in ((w_hi, True), (w_lo, False)):
                        mm = pe.matmul(PJ[g][:], w[:, 128 + P * g:256 + P * g],
                                       z_pair[:, TOK * c:TOK * c + TOK], start=st, stop=not st)
                    mm.then_inc(s["v_ps"], 1)

            def scores(j, c, first=False):
                if not first:
                    pe.wait_ge(s["sub_ready"], 4 * (j - 1) + 2 * c + 2)
                if c == 0:
                    pe.wait_ge(s["qexp_ready"], 8 * (j + 1))
                    pe.wait_ge(s["k_lo_ready"], j + 1)
                for g in range(2):
                    dst = SC[c][g]
                    r0 = 64 * c + 32 * g
                    pe.matmul(dst[:], bias_t[:, P * g:P * g + P],
                              pick[:].unsqueeze(1).broadcast_to([64, CHUNK, N_SEQ]), start=True, stop=False,
                              skip_group_check=True)
                for i in range(CHUNK):
                    for g in range(2):
                        dst = SC[c][g]
                        r0 = 64 * c + 32 * g
                        for part, k in ((0, k_hi), (0, k_lo), (1, k_hi)):
                            mm = pe.matmul(dst[:, 32 * i:32 * i + 32],
                                           q_exp[r0:r0 + 32, part, i, :, :].rearrange("p h n -> p (h n)"),
                                           k[r0:r0 + 32, 32 * i:32 * i + 32], start=False, stop=(part == 1),
                                           skip_group_check=True)
                mm.then_inc(s["s_ps"], 1)

            def attend(j, c, par):
                pe.wait_ge(s["et_ready"], 2 * j + c + 1)
                pe.wait_ge(s["vt_ready"], 4 * (j + 1))
                if c == 1:
                    pe.wait_ge(s["norm_ready"], 2 * j + c)
                for q in range(4):
                    for g in range(2):
                        for u in range(4):
                            i = 4 * q + u
                            mm = pe.matmul(AVB[32 * u:32 * u + 32, 72 * q + VCOL * g:72 * q + VCOL * g + VCOL],
                                           e_t[:, c, g, 32 * i:32 * i + 32], v_tile[par][:, c, g, i, :],
                                           start=True, stop=True)
                mm.then_inc(s["av_ps"], 1)

            def turn_result(j, last=False):
                pe.wait_ge(s["att_ready"], 2 * (j + 1))
                pe.wait_ge(s["gpre_ready"], PAIRS if last else j + 3)
                if last:
                    pe.wait_ge(s["x1_ready"], 2 * j)
                for q in range(4):
                    mm = pe.transpose(MS[:, P * q:P * q + P], att[:, q, :, :].rearrange("p c d -> p (c d)"), ident[:])
                mm.then_inc(s["at_ps"], 1)

            def project_out(j):
                pe.wait_ge(s["att_t_ready"], j + 1)
                at_v = att_t[:].rearrange("p (l h n) -> p l h n", l=CHUNK, h=2)
                for c in range(2):
                    for h in range(2):
                        mm = pe.matmul(MS[64 * h:64 * h + 64, 256 * c:256 * c + 256], wo_pad[:, c, :],
                                       at_v[:, :, h, :], start=True, stop=True)
                mm.then_inc(s["wo_ps"], 1)

            def pe_step(j, par, first=False, last=False):
                scores(j, 0, first=first)
                scores(j, 1, first=first)
                if not first:
                    attend(j - 1, 0, 1 - par)
                if not last:
                    project(j + 1)
                if not first:
                    attend(j - 1, 1, 1 - par)
                if not last:
                    gates(j + 1)
                    values(j + 1, 0)
                if not first:
                    turn_result(j - 1, last=last)
                if not last:
                    values(j + 1, 1)
                if not first:
                    project_out(j - 1)

            pe.wait_ge(s["bias_copied"], 2)
            project(0, first=True)
            gates(0, first=True)
            values(0, 0)
            values(0, 1)
            pe_step(0, 0, first=True)
            pe.wait_ge(s["ones_ready"], N_ONES)
            with pe.Fori(0, PAIRS // 2 - 1) as i:
                pe_step(2 * i + 1, 1)
                pe_step(2 * i + 2, 0)
            pe_step(PAIRS - 1, 1, last=True)
            attend(PAIRS - 1, 0, 1)
            attend(PAIRS - 1, 1, 1)
            turn_result(PAIRS - 1, last=True)
            project_out(PAIRS - 1)

            def router_tokens(k):
                pe.wait_ge(s["xn_ready"], 2 * k + 2)
                if k >= 2:
                    pe.wait_ge(s["rt_sb"], k - 1)
                for t in range(2):
                    for c in range(2):
                        mm = pe.transpose(bank[k % 2][:, P * (2 * t + c):P * (2 * t + c) + P],
                                          xn[:, 2 * k + t, P * c:P * c + P], ident[:])
                mm.then_inc(s["rt_ps"], 1)

            def router_logits(k):
                pe.wait_ge(s["rt_sb"], k + 1)
                for t in range(2):
                    n = 2 * k + t
                    for c in range(2):
                        mm = pe.matmul(bank[2][:, 8 * n:8 * n + 8], xn_t[k % 2][:, P * (2 * t + c):P * (2 * t + c) + P],
                                       rw_sb[:, c, :], start=(c == 0), stop=(c == 1))
                    mm.then_inc(s["logit_ps"], 1)

            pe.wait_ge(s["r_in"], 32)
            for k in range(8):
                router_tokens(k)
                if k >= 1:
                    router_logits(k - 1)
            router_logits(7)

            pe.wait_ge(s["sel_ready"], 1)
            pe.matmul(bank[3][:, 128:136], ones_h[:], r_incl[:, TILES - 1:EXPERTS * TILES:TILES], start=True, stop=True)
            pe.matmul(bank[3][:, 0:128], before, r_sel, start=True, stop=False, skip_group_check=True)
            pe.matmul(bank[3][:, 0:128], ones_h[:], r_incl, start=False, stop=True, skip_group_check=True)\
                .then_inc(s["route_ps"], 1)
            pe.wait_ge(s["onehot_ready"], 1)
            for a in range(ASSIGN):
                mm = pe.matmul(bank[4][:, 0:3 * BLOCKS], r_place[:, a, :], r_values[:, a, :], start=(a == 0),
                               stop=(a == ASSIGN - 1))
            mm.then_inc(s["tab_ps"], 1)

            GU = [[bank[0], bank[1]], [bank[2], bank[3]]]
            XT, HT, YB = bank[4], bank[5], bank[6]

            def expert_of(b):
                return pe.value_load(t_expert[0:1, bass.ds(b, 1)], min_val=0, max_val=EXPERTS - 1)

            def tokens_in(turn, par, first=False):
                b = 2 * turn + par
                pe.wait_ge(s[f"x_got{par}"], 16 * (turn + 1))
                if not first:
                    pe.wait_ge(s["xl_ready"], b)
                for c in range(2):
                    mm = pe.transpose(XT[:, P * c:P * c + P], xg[par][:, P * c:P * c + P], ident[:])
                mm.then_inc(s["xt_ps"], 1)

            def hidden(b, par, k, e, first=False):
                if k == 0:
                    pe.wait_ge(s["xl_ready"], b + 1)
                if not first:
                    pe.wait_ge(s["gadd_ready"] if k == 0 else s["uadd_ready"], b - 1)
                n = 0
                for xs, w in ((x_hi, 0), (x_hi, 1), (x_lo, 0)):
                    for c in range(2):
                        mm = pe.matmul(GU[par][k][:], xs[par][:, c, :],
                                       w_exp[:, bass.ds(e * 2 * W_EXP + (w * W_EXP + k * W_PIECE + c * FF), FF)],
                                       start=(n == 0), stop=(n == 5))
                        n += 1
                mm.then_inc(s["gu_ps"], 1)

            def hidden_turned(b, par, first=False):
                pe.wait_ge(s["h_ready"], b + 1)
                if not first:
                    pe.wait_ge(s["hl_ready"], b)
                for c in range(4):
                    mm = pe.transpose(HT[:, P * c:P * c + P], h_sb[par][:, P * c:P * c + P], ident[:])
                mm.then_inc(s["ht_ps"], 1)

            def down(b, par, e, first=False):
                pe.wait_ge(s["hl_ready"], b + 1)
                if not first:
                    pe.wait_ge(s["yadd_ready"], b)
                n = 0
                for hs, w in ((h_hi, 0), (h_hi, 1), (h_lo, 0)):
                    for c in range(4):
                        mm = pe.matmul(YB[:, 0:L_COL], hs[par][:, c, :],
                                       w_exp[:, bass.ds(e * 2 * W_EXP + (w * W_EXP + 2 * W_PIECE + c * L_COL), L_COL)],
                                       start=(n == 0), stop=(n == 11))
                        n += 1
                mm.then_inc(s["y_ps"], 1)

            def pe_block(turn, par, first=False, more=2):
                b = 2 * turn + par
                if more >= 1:
                    e1 = expert_of(b + 1)
                    hidden(b + 1, 1 - par, 0, e1, first=first)
                hidden_turned(b, par, first=first)
                if more >= 1:
                    hidden(b + 1, 1 - par, 1, e1, first=first)
                if more >= 2:
                    tokens_in(turn + 1, par)
                down(b, par, expert_of(b), first=first)

            pe.wait_ge(s["tables_ready"], 1)
            tokens_in(0, 0, first=True)
            tokens_in(0, 1)
            e0 = expert_of(0)
            hidden(0, 0, 0, e0, first=True)
            hidden(0, 0, 1, e0, first=True)
            pe_block(0, 0, first=True)
            with pe.Fori(0, BODY) as i:
                pe_block(i, 1)
                pe_block(i + 1, 0)
            pe_block(BODY, 1, more=1)
            pe_block(BODY + 1, 0, more=0)

        @block.scalar
        def _(act):
            act.dma_start(pr[0], pairs[0].rearrange("i j c -> j i c")).then_inc(s["pairs_in"], 16)
            act.dma_start(pair_g, ln_p_g.partition_broadcast(32)).then_inc(s["pair_par_in"], 16)
            act.dma_start(pair_b, ln_p_b.partition_broadcast(32)).then_inc(s["pair_par_in"], 16)
            act.dma_start(wb_sb, Wb).then_inc(s["pair_par_in"], 16)

            def root(k, dst, src):
                act.wait_ge(s["root_in"], k + 1)
                act.activation(dst, src, ACT.Sqrt).then_inc(s["root_out"], 1)

            def stack_out(q):
                act.wait_ge(s["ztr_ready"], 2 * q + 1)
                act.activation(z_stack_v[:, 0, :, :, 4 * q:4 * q + 4],
                               bank[4][:].bitcast(fp16).rearrange("p (i h l) -> p l h i", i=4, h=2),
                               ACT.Copy).then_inc(s["zst_act"], 1)

            def columns(q):
                act.wait_ge(s["negm_ready"], 1)
                if q >= 2:
                    act.wait_ge(s["cen_ready"], 2 * (q - 2) + 2)
                for n in range(4 * q, 4 * q + 4):
                    act.activation(x_col[q % 2][:, n - 4 * q, :], x_rows[:, n, :], ACT.Identity,
                                   bias=neg_mean[:, n:n + 1], scale=rs_col[:, n:n + 1]).then_inc(s["xcol_act"], 1)

            root(0, pair_s[:, 96:128], pair_s[:, 32:64])
            root(1, sd_col, var_col)
            columns(1)
            for q in range(QUADS):
                for h in range(2):
                    act.wait_ge(s["cen_ready"], 2 * q + h + 1)
                    if q >= 1:
                        act.wait_ge(s["root_in"], q + 2)
                    act.activation(squares[h], bank[2 * (q % 2) + h][:], ACT.Square).then_inc(s["sq_ready"], 1)
                if q >= 1:
                    stack_out(q - 1)
                root(q + 2, sd_tok, var_tok)
                for h in range(2):
                    act.wait_ge(s["ztok_ready"], 2 * q + h + 1)
                    if q >= 1:
                        act.wait_ge(s["ztr_ready"], 2 * (q - 1) + h + 1)
                    act.activation(z_parts[h][:, :, 0, :], z_tok[h].rearrange("p (t d) -> p t d", t=8),
                                   ACT.Copy).then_inc(s["zhi_ready"], 1)
                if q + 2 < QUADS:
                    columns(q + 2)
            stack_out(QUADS - 1)

            def parts_high(j, first=False):
                act.wait_ge(s["q_ps"], j + 1)
                if not first:
                    act.wait_ge(s["q_lo_ready"], j)
                act.activation(proj[:], bank[4][:], ACT.Identity, bias=qb_col, scale=Q_SCALE)\
                    .then_inc(s["qf_ready"], 1)
                act.wait_ge(s["qf_ready"], j + 1)
                if not first:
                    act.wait_ge(s["qexp_ready"], 8 * j)
                act.activation(q_hi[:], proj[:], ACT.Copy).then_inc(s["qh_ready"], 1)
                act.wait_ge(s["k_ps"], j + 1)
                if not first:
                    act.wait_ge(s["s_ps"], 2 * j)
                act.activation(att_t[:], bank[5][:], ACT.Identity, bias=kb_col).then_inc(s["kf_ready"], 1)
                act.wait_ge(s["kf_ready"], j + 1)
                act.activation(k_hi[:], att_t[:], ACT.Copy).then_inc(s["kh_ready"], 1)

            def gate_tanh(j, par, early=False):
                act.wait_ge(s["gpre_ready"], j + 1)
                if not early:
                    act.wait_ge(s["att_ready"], 2 * (j - 1))
                act.activation(gate[:, par, :], g_pre[:], ACT.Tanh, scale=0.5).then_inc(s["gate_ready"], 1)

            def exps(j, c):
                act.wait_ge(s["sub_ready"], 4 * j + 2 * c + 2)
                act.activation(s_exp[:, c, :, :], s_exp[:, c, :, :], ACT.Exp).then_inc(s["exp_ready"], 1)

            def weights_high(e, k):
                act.wait_ge(s[f"w_in{k}"], 16 * (e + 1))
                act.activation(w_exp[:, bass.ds(e * 2 * W_EXP + k * W_PIECE, W_PIECE)], w_stage[:, k, :],
                               ACT.Copy).then_inc(s["w_hi_done"], 1)

            def turned_out(j, last=False):
                act.wait_ge(s["at_ps"], j + 1)
                if last:
                    act.wait_ge(s["wo_ps"], j)
                else:
                    act.wait_ge(s["k_lo_ready"], j + 3)
                act.activation(att_t[:], bank[7][:], ACT.Copy).then_inc(s["att_t_ready"], 1)

            def act_step(j, par, first=False, last=False):
                exps(j, 0)
                weights_high(j, 0)
                exps(j, 1)
                if not last:
                    parts_high(j + 1)
                    gate_tanh(j + 1, 1 - par, early=first)
                weights_high(j, 1)
                if not first:
                    turned_out(j - 1, last=last)
                weights_high(j, 2)

            parts_high(0, first=True)
            gate_tanh(0, 0, early=True)
            act_step(0, 0, first=True)
            with act.Fori(0, PAIRS // 2 - 1) as i:
                act_step(2 * i + 1, 1)
                act_step(2 * i + 2, 0)
            act_step(PAIRS - 1, 1, last=True)
            turned_out(PAIRS - 1, last=True)

            root(6, sd_col, var_col)
            for k in range(8):
                act.wait_ge(s["rt_ps"], k + 1)
                if k >= 2:
                    act.wait_ge(s["logit_ps"], 2 * (k - 1))
                act.activation(xn_t[k % 2], bank[k % 2][:], ACT.Copy).then_inc(s["rt_sb"], 1)
            act.wait_ge(s["shift_ready"], 1)
            act.activation(r_prob, r_prob, ACT.Exp).then_inc(s["prob_ready"], 1)

            def tokens_high(b, par, first=False):
                act.wait_ge(s["xt_ps"], b + 1)
                if not first:
                    act.wait_ge(s["gu_ps"], 2 * (b - 1))
                act.activation(x_hi[par], bank[4][:, 0:L_COL].rearrange("p (c t) -> p c t", c=2),
                               ACT.Copy).then_inc(s["xh_ready"], 1)

            def silu(b, par, first=False):
                act.wait_ge(s["gadd_ready"], b + 1)
                if not first:
                    act.wait_ge(s["h_ready"], b - 1)
                act.activation(g_silu[par], g_sum[par], ACT.Silu).then_inc(s["silu_ready"], 1)

            def hidden_high(b, par, first=False):
                act.wait_ge(s["ht_ps"], b + 1)
                act.activation(h_hi[par], bank[5][:].rearrange("p (c t) -> p c t", c=4),
                               ACT.Copy).then_inc(s["hh_ready"], 1)

            def weigh(b, par, first=False):
                act.wait_ge(s["yadd_ready"], b + 1)
                if not first:
                    act.wait_ge(s["scol_ready"], b)
                act.activation(yw[par], y_sum[par], ACT.Copy, scale=t_weight[:, bass.ds(b, 1)])\
                    .then_inc(s["y_ready"], 1)

            def act_block(b, par, first=False, more=2):
                hidden_high(b, par, first=first)
                if more >= 1:
                    silu(b + 1, 1 - par, first=first)
                if more >= 2:
                    tokens_high(b + 2, par)
                weigh(b, par, first=first)

            tokens_high(0, 0, first=True)
            tokens_high(1, 1, first=True)
            silu(0, 0, first=True)
            act_block(0, 0, first=True)
            with act.Fori(0, BODY) as i:
                act_block(2 * i + 1, 1)
                act_block(2 * i + 2, 0)
            act_block(BLOCKS - 2, 1, more=1)
            act_block(BLOCKS - 1, 0, more=0)

        @block.vector
        def _(dve):
            step = steps(dve, s["dve_step"])
            n_v = [0]

            def const(ins):
                ins.then_inc(s["const_v"], 1)
                n_v[0] += 1

            def rsqrt(k, y, v, sd, t, ready):
                dve.wait_ge(s["root_out"], k + 1)
                step(dve.reciprocal(y, sd))
                step(dve.tensor_tensor(t, v, y, ALU.mult))
                step(dve.tensor_tensor(t, t, y, ALU.mult))
                step(dve.tensor_scalar(t, t, -0.5, 1.5, ALU.mult, ALU.add))
                last = dve.tensor_tensor(y, y, t, ALU.mult)
                if ready:
                    last.then_inc(ready, 1)
                else:
                    step(last)

            const(dve.memset(ones_h[:], 1.0))
            const(dve.memset(center, 0.0))
            dve.wait_ge(s["const_v"], 2)
            for h in range(2):
                const(dve.memset(center[64 * h:64 * h + 64, 64 * h:64 * h + 64], -1.0 / D_MODEL))
            dve.wait_ge(s["const_v"], 4)
            dve.wait_ge(s["const_p"], 9)
            const(dve.tensor_tensor(center, center, ident[:], ALU.add))
            assert n_v[0] == N_CENTER
            step(dve.tensor_scalar(small_i[:, 1:2], small_i[:, 0:1], 3, 3, ALU.logical_shift_right, ALU.bitwise_and))
            step(dve.tensor_copy(small[:, 150:151], small_i[:, 1:2]))
            for h in range(GROUP):
                step(dve.tensor_scalar(head_mask[:, h:h + 1], small[:, 150:151], float(h), None, ALU.is_equal))
            dve.wait_ge(s["pairs_in"], 16)
            step(dve.tensor_reduce(pair_s[:, 0:32], pr[0], AX.X, ALU.add))
            dve.tensor_scalar(pair_s[:, 0:32], pair_s[:, 0:32], 1.0 / P_DIM, None, ALU.mult).then_inc(s["pair_v"], 1)

            def statistics(rows, done):
                for n in rows:
                    dve.bn_stats(bn[:, n, :], x_rows[:, n, :]).then_inc(s["stats_ready"], 1)
                dve.wait_ge(s["stats_ready"], done + len(rows))
                for n in rows:
                    dve.bn_aggr(mv[:, n, :], bn[:, n, :]).then_inc(s["mean_ready"], 1)

            for q in range(QUADS):
                dve.wait_ge(s[f"x_in{q}"], 32)
                statistics(range(4 * q, 4 * q + 4), 4 * q)
                if q == 1:
                    dve.wait_ge(s["pool_pair"], 2)
                    step(dve.tensor_reduce(pair_s[:, 32:64], pr[1], AX.X, ALU.add))
                    dve.tensor_scalar(pair_s[:, 32:64], pair_s[:, 32:64], 1.0 / P_DIM, EPS_TOK, ALU.mult, ALU.add)\
                        .then_inc(s["root_in"], 1)
                    dve.wait_ge(s["root_in"], 1)
                if q == 2:
                    rsqrt(0, pair_s[:, 64:96], pair_s[:, 32:64], pair_s[:, 96:128], pair_s[:, 128:160], s["pair_v"])
            dve.wait_ge(s["mean_ready"], N_HALF)
            dve.tensor_scalar(var_col, mv[:, :, 1], EPS_COL, None, ALU.add).then_inc(s["root_in"], 1)
            dve.wait_ge(s["root_in"], 2)
            rsqrt(1, rs_col, var_col, sd_col, tmp_col, None)
            dve.scalar_tensor_tensor(out=neg_mean, in0=mv[:, :, 0], scalar=-1.0, in1=rs_col, op0=ALU.mult,
                                     op1=ALU.mult).then_inc(s["negm_ready"], 1)

            def columns(q):
                for i in range(4):
                    n = 4 * q + i
                    dve.tensor_scalar(x_col[q % 2][:, i, :], x_rows[:, n, :], mv[:, n, 0:1], rs_col[:, n:n + 1],
                                      ALU.subtract, ALU.mult).then_inc(s["xcol_dve"], 1)

            def stack_out(q):
                dve.wait_ge(s["ztr_ready"], 2 * q + 2)
                dve.tensor_copy(z_stack_v[:, 1, :, :, 4 * q:4 * q + 4],
                                bank[5][:].bitcast(fp16).rearrange("p (i h l) -> p l h i", i=4, h=2))\
                    .then_inc(s["zst_dve"], 1)

            columns(0)
            for q in range(QUADS):
                for h in range(2):
                    dve.wait_ge(s["sq_ready"], 2 * q + h + 1)
                    step(dve.tensor_reduce(sum_tok[:, 8 * h:8 * h + 8], squares[h].rearrange("p (t d) -> p t d", t=8),
                                           AX.X, ALU.add))
                dve.tensor_scalar(var_tok, sum_tok, 1.0 / D_MODEL, EPS_TOK, ALU.mult, ALU.add)\
                    .then_inc(s["root_in"], 1)
                dve.wait_ge(s["root_in"], q + 3)
                rsqrt(q + 2, rs_tok, var_tok, sd_tok, tmp_tok, None)
                for h in range(2):
                    if q >= 1:
                        dve.wait_ge(s["zlo_ready"], 2 * (q - 1) + h + 1)
                    r = rs_tok[:, 8 * h:8 * h + 8].unsqueeze(2).broadcast_to([P, 8, D_MODEL])
                    dve.tensor_tensor(z_tok[h].rearrange("p (t d) -> p t d", t=8),
                                      bank[2 * (q % 2) + h][:].rearrange("p (t d) -> p t d", t=8), r,
                                      ALU.mult).then_inc(s["ztok_ready"], 1)
                if q == 0:
                    dve.wait_ge(s["pool_pair"], 5)
                    dve.transpose(pr[2].rearrange("p i c -> p (i c)"), pr[0].rearrange("p i c -> p (i c)"))\
                        .then_inc(s["pair_v"], 1)
                    dve.wait_ge(s["par_in"], 16 * N_PAR)
                    dve.tensor_copy(b_wide, b_col[0:64, :].broadcast_to([64, P])).then_inc(s["wide_ready"], 1)
                else:
                    stack_out(q - 1)
                if q == 1:
                    dve.wait_ge(s["pe_prep"], 1)
                    step(dve.tensor_scalar(qb_col, bank[7][:, 0:1], Q_SCALE, None, ALU.mult))
                    step(dve.tensor_copy(kb_col, bank[7][:, 1:2]))
                    step(dve.tensor_copy(v_row[:], bank[6][:, 0:64]))
                    dve.tensor_tensor(g_row[:], bank[6][:, 64:128], bg_row, ALU.add).then_inc(s["vec_copied"], 1)
                    dve.wait_ge(s["vec_copied"], 1)
            dve.wait_ge(s["pe_bias"], 1)
            dve.tensor_copy(bias_t[0:32, :], bank[6][0:32, 0:256]).then_inc(s["bias_copied"], 1)
            dve.wait_ge(s["bias_copied"], 1)
            dve.tensor_tensor(bias_t[32:64, :], bank[6][0:32, 0:256], bias_t[0:32, :], ALU.subtract)\
                .then_inc(s["bias_copied"], 1)
            stack_out(QUADS - 1)

            def pair_tokens(j, first=False):
                if not first:
                    dve.wait_ge(s["v_ps"], 4 * j)
                src = z_stack[:].rearrange("p l n -> p (l n)")[:, bass.ds(j * (PAIR * N_SEQ), PAIR * N_SEQ)]
                dve.tensor_copy(z_pair[:].bitcast(fp32), src.bitcast(fp32)).then_inc(s["zpair_ready"], 1)

            def soften(j, c, first=False):
                dve.wait_ge(s["s_ps"], 2 * j + c + 1)
                for g in range(2):
                    dve.tensor_reduce(maxes[:, 2 * c + g, :],
                                      bank[2 * c + g][:].rearrange("p (l m) -> p l m", l=CHUNK), AX.X, ALU.max)\
                        .then_inc(s["max_ready"], 1)
                if not first:
                    dve.wait_ge(s["et_ready"], 2 * j + c - 1)
                for g in range(2):
                    dve.wait_ge(s["max_ready"], 4 * j + 2 * c + g + 1)
                    dve.tensor_tensor(s_exp[:, c, g, :].rearrange("p (l m) -> p l m", l=CHUNK),
                                      bank[2 * c + g][:].rearrange("p (l m) -> p l m", l=CHUNK),
                                      maxes[:, 2 * c + g, :].unsqueeze(2).broadcast_to([P, CHUNK, N_SEQ]),
                                      ALU.subtract).then_inc(s["sub_ready"], 1)

            def turn(j, c, first=False):
                dve.wait_ge(s["exp_ready"], 2 * j + c + 1)
                if not first:
                    dve.wait_ge(s["av_ps"], 2 * j + c - 1)
                dve.transpose(e_t[:, c, :, :].rearrange("p g t -> p (g t)"),
                              s_exp[:, c, :, :].rearrange("p g t -> p (g t)")).then_inc(s["et_ready"], 1)

            def normalise(j, c, last=False):
                dve.wait_ge(s["av_ps"], 2 * j + c + 1)
                av = bank[6][:, 0:4 * 2 * VCOL].rearrange("p (a v) -> p a v", v=VCOL)
                rd = rden[:, c, :].rearrange("p (a h) -> p a h", h=GROUP)
                dve.reciprocal(rd, av[:, :, 32:36]).then_inc(s["rden_ready"], 1)
                dve.wait_ge(s["rden_ready"], 2 * j + c + 1)
                if not last:
                    dve.wait_ge(s["et_ready"], 2 * (j + 1))
                dve.tensor_tensor(att_n[:, c, :].rearrange("p (a h d) -> p a h d", h=GROUP, d=D_HEAD),
                                  av[:, :, 0:32].rearrange("p a (h d) -> p a h d", h=GROUP),
                                  rd.unsqueeze(3).broadcast_to([P, 8, GROUP, D_HEAD]),
                                  ALU.mult).then_inc(s["norm_ready"], 1)

            def apply_gate(j, c, par):
                dve.wait_ge(s["vb_ready"], 2 * j + c + 1)
                dve.wait_ge(s["gate_ready"], j + 1)
                dve.scalar_tensor_tensor(out=att[:, :, c, :], in0=gate_v[par][:, c, :, :], scalar=1.0,
                                         in1=att_n[:, c, :].rearrange("p (q v) -> p q v", q=4),
                                         op0=ALU.add, op1=ALU.mult).then_inc(s["att_ready"], 1)

            def gate_sum(j, first=False):
                dve.wait_ge(s["g_ps"], j + 1)
                if not first:
                    dve.wait_ge(s["gate_ready"], j)
                dve.tensor_tensor(g_pre[:].rearrange("p (t v) -> p t v", t=8),
                                  bank[7][:].rearrange("p (t v) -> p t v", t=8),
                                  g_row[:].unsqueeze(1).broadcast_to([P, 8, D_MODEL]), ALU.add)\
                    .then_inc(s["gpre_ready"], 1)

            def values_turned(j, c, g, par, early=False):
                dve.wait_ge(s["v_ps"], 4 * j + 2 * c + g + 1)
                if not early:
                    dve.wait_ge(s["av_ps"], 2 * (j - 1))
                dve.transpose(v_tile[par][:, c, g, :, 0:32], bank[4 + g][:].rearrange("p (l m) -> p l m", l=CHUNK))\
                    .then_inc(s["vt_ready"], 1)

            def spread_queries(j, part, first=False):
                src = (q_hi, q_lo)[part]
                dve.wait_ge(s["q_lo_ready"] if part else s["qh_ready"], j + 1)
                if not first:
                    dve.wait_ge(s["s_ps"], 2 * j)
                for h in range(GROUP):
                    dve.tensor_scalar(q_exp[:, part, :, h, :], src[:].rearrange("p (l n) -> p l n", l=CHUNK),
                                      head_mask[:, h:h + 1], None, ALU.mult).then_inc(s["qexp_ready"], 1)

            def add_rows(j):
                dve.wait_ge(s["wo_ps"], j + 1)
                for c in range(2):
                    dst = x_rows[:, :, bass.ds(PAIR * j + CHUNK * c, CHUNK)]
                    dve.scalar_tensor_tensor(
                        out=dst, in0=bank[7][:, 256 * c:256 * c + 256].rearrange("p (l n) -> p n l", l=CHUNK),
                        scalar=bo_col, in1=dst, op0=ALU.add, op1=ALU.add).then_inc(s["x1_ready"], 1)

            def dve_step(j, par, first=False, last=False):
                if not last:
                    pair_tokens(j + 1)
                soften(j, 0, first=first)
                soften(j, 1, first=first)
                if not first:
                    normalise(j - 1, 0)
                turn(j, 0, first=first)
                if not last:
                    spread_queries(j + 1, 0)
                    spread_queries(j + 1, 1)
                if not first:
                    normalise(j - 1, 1)
                if not last:
                    gate_sum(j + 1)
                if not first:
                    apply_gate(j - 1, 0, 1 - par)
                    apply_gate(j - 1, 1, 1 - par)
                if not last:
                    values_turned(j + 1, 0, 0, 1 - par, early=first)
                    values_turned(j + 1, 0, 1, 1 - par, early=first)
                turn(j, 1, first=first)
                if not last:
                    values_turned(j + 1, 1, 0, 1 - par, early=first)
                    values_turned(j + 1, 1, 1, 1 - par, early=first)
                if not first:
                    add_rows(j - 1)

            dve.wait_ge(s["zst_act"], QUADS)
            dve.wait_ge(s["zst_dve"], QUADS)
            pair_tokens(0, first=True)
            spread_queries(0, 0, first=True)
            spread_queries(0, 1, first=True)
            gate_sum(0, first=True)
            for c in range(2):
                for g in range(2):
                    values_turned(0, c, g, 0, early=True)
            dve_step(0, 0, first=True)
            with dve.Fori(0, PAIRS // 2 - 1) as i:
                dve_step(2 * i + 1, 1)
                dve_step(2 * i + 2, 0)
            dve_step(PAIRS - 1, 1, last=True)
            for c in range(2):
                normalise(PAIRS - 1, c)
            for c in range(2):
                apply_gate(PAIRS - 1, c, 1)
            add_rows(PAIRS - 1)

            step(dve.memset(se_flat[:, 0:L_COL], 0.0))
            step(dve.memset(r_keep, 1.0))
            step(dve.memset(r_keep.rearrange("p (e n) -> p e n", e=EXPERTS)[:, :, 0:1], 0.0))
            step(dve.memset(r_one8, 1.0))
            dve.memset(small[:, 151:152], 0.0).then_inc(s["zero_ready"], 1)
            statistics(range(TILES), TILES)
            dve.wait_ge(s["mean_ready"], 2 * TILES)
            dve.tensor_scalar(var_col, mv[:, :, 1], EPS_TOK, None, ALU.add).then_inc(s["root_in"], 1)
            dve.wait_ge(s["root_in"], 7)
            rsqrt(6, rs_col, var_col, sd_col, tmp_col, None)
            for n in range(TILES):
                dve.tensor_scalar(xn[:, n, :], x_rows[:, n, :], mv[:, n, 0:1], rs_col[:, n:n + 1],
                                  ALU.subtract, ALU.mult).then_inc(s["xn_ready"], 1)
            dve.wait_ge(s["route_p"], 8)
            step(dve.tensor_copy(iota_f, r_iota128))
            step(dve.tensor_copy(thr_f, r_thr))
            step(dve.tensor_copy(tid_f, r_tid))
            dve.wait_ge(s["logit_ps"], TILES)
            step(dve.tensor_tensor(r_logit, bank[2][:, 0:128].rearrange("p (n e) -> p n e", n=TILES),
                                   rb_row.unsqueeze(1).broadcast_to([P, TILES, EXPERTS]), ALU.add))
            four = [P, TILES, EXPERTS, EXPERTS]
            other, own = r_logit.unsqueeze(2).broadcast_to(four), r_logit.unsqueeze(3).broadcast_to(four)
            step(dve.tensor_tensor(r_gt, other, own, ALU.is_gt))
            step(dve.tensor_tensor(r_eq, other, own, ALU.is_equal))
            step(dve.tensor_tensor(r_eq, r_eq, r_lower.unsqueeze(1).broadcast_to(four), ALU.mult))
            step(dve.tensor_tensor(r_gt, r_gt, r_eq, ALU.add))
            step(dve.tensor_reduce(r_rank, r_gt, AX.X, ALU.add))
            step(dve.tensor_scalar(r_chosen, r_rank, TOP_K - 0.5, None, ALU.is_lt))
            step(dve.tensor_reduce(r_mx, r_logit, AX.X, ALU.max))
            dve.tensor_tensor(r_prob, r_logit, r_mx.unsqueeze(2).broadcast_to([P, TILES, EXPERTS]), ALU.subtract)\
                .then_inc(s["shift_ready"], 1)
            by_expert = r_chosen.rearrange("p n e -> p e n")
            step(dve.tensor_copy(r_sel.rearrange("p (e n) -> p e n", e=EXPERTS), by_expert))
            step(dve.tensor_copy(r_slot.rearrange("p (e n) -> p e n", e=EXPERTS), by_expert))
            step(dve.tensor_tensor_scan(r_scan, r_keep, r_slot, 0.0, ALU.mult, ALU.add))
            dve.tensor_copy(r_incl, r_scan).then_inc(s["sel_ready"], 1)
            dve.wait_ge(s["prob_ready"], 1)
            step(dve.tensor_tensor(r_prob, r_prob, r_chosen, ALU.mult))
            step(dve.tensor_reduce(r_sum, r_prob, AX.X, ALU.add))
            step(dve.reciprocal(r_rs, r_sum))
            step(dve.tensor_tensor(r_prob, r_prob, r_rs.unsqueeze(2).broadcast_to([P, TILES, EXPERTS]), ALU.mult))
            dve.wait_ge(s["route_ps"], 1)
            step(dve.tensor_copy(r_cnt, bank[3][:, 128:136]))
            step(dve.tensor_tensor(r_cmp, r_cnt.unsqueeze(2).broadcast_to([P, EXPERTS, TILES]),
                                   thr_f.unsqueeze(1).broadcast_to([P, EXPERTS, TILES]), ALU.is_gt))
            step(dve.tensor_reduce(r_nb, r_cmp, AX.X, ALU.add))
            step(dve.tensor_tensor_scan(r_cum, r_one8, r_nb, 0.0, ALU.mult, ALU.add))
            step(dve.tensor_tensor(r_base, r_cum, r_nb, ALU.subtract))
            step(dve.tensor_scalar(r_base, r_base, float(SLOTS), None, ALU.mult))
            step(dve.tensor_tensor(r_slot.rearrange("p (e n) -> p e n", e=EXPERTS),
                                   bank[3][:, 0:128].rearrange("p (e n) -> p e n", e=EXPERTS),
                                   r_base.unsqueeze(2).broadcast_to([P, EXPERTS, TILES]), ALU.add))
            slot_v = r_slot.rearrange("p (e n) -> p n e", e=EXPERTS)
            for k in range(TOP_K):
                step(dve.tensor_scalar(r_first, r_rank, float(k), None, ALU.is_equal))
                step(dve.tensor_tensor(r_tmp, r_first, slot_v, ALU.mult))
                step(dve.tensor_reduce(r_slots[:, TILES * k:TILES * k + TILES], r_tmp, AX.X, ALU.add))
                step(dve.tensor_tensor(r_tmp, r_first, r_prob, ALU.mult))
                step(dve.tensor_reduce(r_w[:, TILES * k:TILES * k + TILES], r_tmp, AX.X, ALU.add))
            step(dve.tensor_copy(r_ints[:, 0:32], r_slots))
            step(dve.tensor_scalar(r_ints[:, 32:64], r_ints[:, 0:32], SLOTS - 1, None, ALU.bitwise_and))
            step(dve.tensor_scalar(r_ints[:, 64:96], r_ints[:, 0:32], 7, None, ALU.logical_shift_right))
            step(dve.tensor_copy(r_p, r_ints[:, 32:64]))
            step(dve.tensor_copy(r_b, r_ints[:, 64:96]))
            step(dve.tensor_copy(r_wh, r_w))
            step(dve.tensor_tensor(r_wl, r_w, r_wh, ALU.subtract))
            dve.wait_ge(s["pad_out"], 16)
            step(dve.tensor_tensor(r_place, iota_f.unsqueeze(1).broadcast_to([P, ASSIGN, P]),
                                   r_p.unsqueeze(2).broadcast_to([P, ASSIGN, P]), ALU.is_equal))
            step(dve.tensor_tensor(r_block, iota_f[:, 0:BLOCKS].unsqueeze(1).broadcast_to([P, ASSIGN, BLOCKS]),
                                   r_b.unsqueeze(2).broadcast_to([P, ASSIGN, BLOCKS]), ALU.is_equal))
            for k in range(TOP_K):
                rows = slice(TILES * k, TILES * k + TILES)
                step(dve.tensor_tensor(r_values[:, rows, 0:BLOCKS], r_block[:, rows, :],
                                       tid_f.unsqueeze(2).broadcast_to([P, TILES, BLOCKS]), ALU.mult))
            step(dve.tensor_tensor(r_values[:, :, BLOCKS:2 * BLOCKS], r_block,
                                   r_wh.unsqueeze(2).broadcast_to([P, ASSIGN, BLOCKS]), ALU.mult))
            dve.tensor_tensor(r_values[:, :, 2 * BLOCKS:3 * BLOCKS], r_block,
                              r_wl.unsqueeze(2).broadcast_to([P, ASSIGN, BLOCKS]), ALU.mult)\
                .then_inc(s["onehot_ready"], 1)
            step(dve.tensor_tensor(r_ecmp, iota_f[:, 0:BLOCKS].unsqueeze(2).broadcast_to([P, BLOCKS, EXPERTS]),
                                   r_cum.unsqueeze(1).broadcast_to([P, BLOCKS, EXPERTS]), ALU.is_ge))
            step(dve.tensor_reduce(r_tab[:, 0:BLOCKS], r_ecmp, AX.X, ALU.add))
            step(dve.tensor_scalar(t_expert, r_tab[:, 0:BLOCKS], EXPERTS - 1.0, None, ALU.min))
            dve.wait_ge(s["tab_ps"], 1)
            step(dve.tensor_copy(t_weight, bank[4][:, BLOCKS:2 * BLOCKS]))
            step(dve.tensor_tensor(t_weight, t_weight, bank[4][:, 2 * BLOCKS:3 * BLOCKS], ALU.add))
            tok = r_tab[:, 64:64 + BLOCKS]
            empty = r_tab[:, 128:128 + BLOCKS]
            step(dve.tensor_copy(tok, bank[4][:, 0:BLOCKS]))
            step(dve.tensor_scalar(t_gather, tok, -1.0, 0.0, ALU.add, ALU.max))
            step(dve.tensor_copy(small[:, 150:151], small_i[:, 0:1]))
            step(dve.tensor_scalar(small[:, 150:151], small[:, 150:151], float(TOKENS + 1), None, ALU.add))
            step(dve.tensor_scalar(empty, tok, 0.0, small[:, 150:151], ALU.is_equal, ALU.mult))
            step(dve.tensor_tensor(empty, empty, tok, ALU.add))
            dve.tensor_scalar(t_scatter, empty, -1.0, None, ALU.add).then_inc(s["tables_ready"], 1)
            dve.wait_ge(s["tables_ready"], 1)
            dve.wait_ge(s["bias_rows"], 48)

            def tokens_low(b, par, first=False):
                dve.wait_ge(s["xh_ready"], b + 1)
                dve.tensor_tensor(x_lo[par], bank[4][:, 0:L_COL].rearrange("p (c t) -> p c t", c=2), x_hi[par],
                                  ALU.subtract).then_inc(s["xl_ready"], 1)

            def expert_of(b):
                return dve.value_load(t_expert[0:1, bass.ds(b, 1)], min_val=0, max_val=EXPERTS - 1)

            def gate_bias(b, par, e, first=False):
                dve.wait_ge(s["gu_ps"], 2 * b + 1)
                if not first:
                    dve.wait_ge(s["silu_ready"], b - 1)
                dve.tensor_tensor(g_sum[par], bank[2 * par][:], gate_b_all[:, bass.ds(e * FF, FF)], ALU.add)\
                    .then_inc(s["gadd_ready"], 1)

            def up_bias(b, par, e, first=False):
                dve.wait_ge(s["gu_ps"], 2 * b + 2)
                dve.tensor_tensor(u_sum[par], bank[2 * par + 1][:], up_b_all[:, bass.ds(e * FF, FF)], ALU.add)\
                    .then_inc(s["uadd_ready"], 1)

            def gated(b, par, first=False):
                dve.wait_ge(s["silu_ready"], b + 1)
                dve.wait_ge(s["uadd_ready"], b + 1)
                if not first:
                    dve.wait_ge(s["ht_ps"], b - 1)
                dve.tensor_tensor(h_sb[par], g_silu[par], u_sum[par], ALU.mult).then_inc(s["h_ready"], 1)

            def hidden_low(b, par):
                dve.wait_ge(s["hh_ready"], b + 1)
                dve.tensor_tensor(h_lo[par], bank[5][:].rearrange("p (c t) -> p c t", c=4), h_hi[par],
                                  ALU.subtract).then_inc(s["hl_ready"], 1)

            def down_bias(b, par, e, first=False):
                dve.wait_ge(s["y_ps"], b + 1)
                dve.tensor_tensor(y_sum[par], bank[6][:, 0:L_COL], down_b_all[:, bass.ds(e * L_COL, L_COL)], ALU.add)\
                    .then_inc(s["yadd_ready"], 1)

            def dve_block(b, par, first=False, more=2):
                if more >= 1:
                    e1 = expert_of(b + 1)
                    gate_bias(b + 1, 1 - par, e1, first=first)
                hidden_low(b, par)
                if more >= 1:
                    up_bias(b + 1, 1 - par, e1)
                if more >= 2:
                    tokens_low(b + 2, par)
                if more >= 1:
                    gated(b + 1, 1 - par, first=first)
                down_bias(b, par, expert_of(b), first=first)

            tokens_low(0, 0)
            tokens_low(1, 1)
            e0 = expert_of(0)
            gate_bias(0, 0, e0, first=True)
            up_bias(0, 0, e0)
            gated(0, 0, first=True)
            dve_block(0, 0, first=True)
            with dve.Fori(0, BODY) as i:
                dve_block(2 * i + 1, 1)
                dve_block(2 * i + 2, 0)
            dve_block(BLOCKS - 2, 1, more=1)
            dve_block(BLOCKS - 1, 0, more=0)


_INS = ['x', 'L0_conv_pairs', 'L0_conv_ln_m_g', 'L0_conv_ln_m_b', 'L0_conv_ln_p_g', 'L0_conv_ln_p_b', 'L0_conv_Wq',
        'L0_conv_Wk', 'L0_conv_Wv', 'L0_conv_Wg', 'L0_conv_bg', 'L0_conv_Wb', 'L0_conv_Wo', 'L0_conv_bo',
        'L0_ffn_router_w', 'L0_ffn_router_b', 'L0_ffn_gate_w', 'L0_ffn_gate_b', 'L0_ffn_up_w', 'L0_ffn_up_b',
        'L0_ffn_down_w', 'L0_ffn_down_b']


def kernel(**inputs):
    import numpy as _np
    import concourse.bacc as _bacc
    from concourse import mybir as _mybir
    from concourse.bass_utils import run_bass_kernel_spmd as _run

    nc = _bacc.Bacc("TRN2", target_bir_lowering=False, num_devices=1)
    arrays, args = {}, []
    for name in _INS:
        a = _np.ascontiguousarray(inputs[name])
        arrays[f"in_{name}_dram"] = a
        args.append(nc.dram_tensor(f"in_{name}_dram", a.shape, _mybir.dt.from_np(a.dtype), kind="ExternalInput").ap())
    args.append(nc.dram_tensor("out_dram", (TOKENS + SLOTS, L_COL), _mybir.dt.float32, kind="ExternalOutput").ap())
    build(nc, *args)
    r = _run(nc, [arrays], core_ids=[0])
    return r.results[0]["out_dram"][:TOKENS].reshape(1, D_MODEL, N_SEQ, L_COL)
```

```python
import concourse.bass as bass
from concourse import mybir
from contextlib import ExitStack

D_MODEL = 64
N_SEQ = 32
L_COL = 256
HEADS = 8
D_HEAD = D_MODEL // HEADS
P_DIM = 32
EXPERTS = 8
FF = 512
P = 128

N_HALF = N_SEQ // 2
QUADS = N_HALF // 4
L_HALF = L_COL // 2

GROUP = 4
CHUNK = 16
PAIR = 2 * CHUNK
PAIRS = L_COL // PAIR
TOK = CHUNK * N_SEQ
VCOL = GROUP * D_HEAD + GROUP
Q_SCALE = float(D_HEAD) ** -0.5

TOKENS = D_MODEL * N_SEQ
TILES = TOKENS // P
TOP_K = 2
SLOTS = P
BLOCKS = (TOKENS * TOP_K + EXPERTS * (SLOTS - 1)) // SLOTS
BODY = (BLOCKS - 3) // 4
W_EXP = 2 * 2 * FF + (FF // P) * L_COL
W_PIECE = W_EXP // 3
ASSIGN = TILES * TOP_K
PIECES = 4
PIECE = ASSIGN // PIECES

EPS_COL = 1e-6
EPS_TOK = 1e-5


def build(nc, x, pairs, ln_m_g, ln_m_b, ln_p_g, ln_p_b, Wq, Wk, Wv, Wg, bg, Wb, Wo, bo,
          router_w, router_b, gate_w, gate_b, up_w, up_b, down_w, down_b, out):
    fp32, fp16, i32 = mybir.dt.float32, mybir.dt.float16, mybir.dt.int32
    ALU, ACT, AX = mybir.AluOpType, mybir.ActivationFunctionType, mybir.AxisListType

    ctx = ExitStack()
    with ctx:
        def sb(name, shape, dt=fp32):
            return ctx.enter_context(nc.sbuf_tensor(name, shape, dt))

        def sem(name):
            return ctx.enter_context(nc.semaphore(name))

        x_rows = sb("x_rows", [P, N_HALF, L_COL])
        z_stack = sb("z_stack", [P, L_COL, N_SEQ], fp16)
        w_exp = sb("w_exp", [P, EXPERTS * 2 * W_EXP], fp16)
        w_stage = sb("w_stage", [P, 3, W_PIECE])

        z_pair = sb("z_pair", [P, PAIR * N_SEQ], fp16)
        proj = sb("proj", [P, TOK])
        q_hi = sb("q_hi", [P, TOK], fp16)
        q_lo = sb("q_lo", [P, TOK], fp16)
        k_hi = sb("k_hi", [P, TOK], fp16)
        k_lo = sb("k_lo", [P, TOK], fp16)
        q_exp = sb("q_exp", [P, 2, CHUNK, GROUP, N_SEQ], fp16)
        s_exp = sb("s_exp", [P, 2, 2, TOK])
        e_t = sb("e_t", [P, 2, 2, TOK])
        v_exp = sb("v_exp", [P, 2, 2 * 2 * CHUNK * VCOL])
        gate = sb("gate", [P, 2, 2 * 4 * D_MODEL])
        g_pre = sb("g_pre", [P, 2 * 4 * D_MODEL])
        att_n = sb("att_n", [P, 2, 4 * D_MODEL])
        att = sb("att", [P, 4, 2, D_MODEL])
        att_t = sb("att_t", [P, TOK])

        ident = sb("ident", [P, P])
        ident_h = sb("ident_h", [P, P], fp16)
        ones_h = sb("ones_h", [P, P], fp16)
        w_hi = sb("w_hi", [P, 448], fp16)
        w_lo = sb("w_lo", [P, 448], fp16)
        bias_t = sb("bias_t", [64, 2 * P], fp16)
        pick = sb("pick", [64, N_SEQ], fp16)
        g_row = sb("g_row", [P, D_MODEL])
        v_row = sb("v_row", [P, D_MODEL])
        head_mask = sb("head_mask", [P, GROUP])
        small = sb("small", [P, 218])
        small_i = sb("small_i", [P, 2], i32)
        maxes = sb("maxes", [P, 4, CHUNK])
        rden = sb("rden", [P, 2, 32])
        wo_parts = sb("wo_parts", [P, 2, D_MODEL], fp16)
        center = gate[:, 1, 0:P]
        before = k_lo[:, 384:512]
        bank = [ctx.enter_context(nc.psum_tensor(f"bank{i}", [P, 512], fp32)) for i in range(8)]

        centred = [(bank[i], bank[i + 1]) for i in (0, 2, 6, 0)]

        stacked = [(bank[i], bank[i + 1]) for i in (4, 4, 4, 6)]

        et_flat = e_t[:].rearrange("p a b c -> p (a b c)")
        se_flat = s_exp[:].rearrange("p a b c -> p (a b c)")
        qe_flat = q_exp[:].rearrange("p a b c d -> p (a b c d)")
        ve_flat = v_exp[:].rearrange("p a b -> p (a b)")
        x_col = [t[:, 1024 * i:1024 * (i + 1)].rearrange("p (n l) -> p n l", n=4)
                 for t, i in ((et_flat, 0), (et_flat, 1), (qe_flat.bitcast(fp32), 1))]
        x_col = [[t[:, n, :] for n in range(4)] for t in x_col]
        x_col.append([t[:, L_COL * n:L_COL * (n + 1)] for t in (proj, att_t) for n in range(2)])
        squares = [se_flat[:, 512 * h:512 * (h + 1)] for h in range(2)]
        z_tok = [se_flat[:, 1024 + 512 * h:1024 + 512 * (h + 1)] for h in range(2)]
        z_parts = [qe_flat[:, 1024 * h:1024 * (h + 1)].rearrange("p (t s d) -> p t s d", t=8, s=2) for h in range(2)]
        w_raw = ve_flat[:, 0:256]
        w_fold = ve_flat[:, 256:704]
        pair_g = ve_flat[0:32, 704:736]
        pair_b = ve_flat[0:32, 736:768]
        bg_row = ve_flat[:, 768:832]
        b_wide = ve_flat[0:64, 832:960]
        wb_sb = ve_flat[0:32, 960:968]
        pr = [ve_flat[0:32, 1024 * i:1024 * (i + 1)].rearrange("p (i c) -> p i c", c=P_DIM) for i in (1, 2, 3)]
        pair_s = att_n[0:32, :, :].rearrange("p a b -> p (a b)")
        bn = g_pre[:, 0:96].rearrange("p (n s) -> p n s", s=6)
        bn2 = g_pre[:, 128:320].rearrange("p (n s) -> p n s", s=12)
        mv = small[:, 0:32].rearrange("p (n s) -> p n s", s=2)
        neg_mean = g_pre[:, 96:112]
        g_col, b_col, bo_col, qb_col, kb_col = (small[:, 144 + i:145 + i] for i in range(5))
        v_tile = [v_exp[:, i, :].rearrange("p (s g l c) -> p s g l c", s=2, g=2, c=VCOL) for i in range(2)]
        gate_v = [gate[:, i, :].rearrange("p (s q c) -> p s q c", s=2, q=4) for i in range(2)]

        N_TABLES = 11
        N_PAR, N_CENTER, N_ONES, N_PREP = 17, 5, 2 * 2 * (1 + GROUP), 3 + 2 + GROUP + 5
        var_col, sd_col, rs_col, tmp_col = (small[:, 32 + 16 * i:48 + 16 * i] for i in range(4))
        sum_tok, var_tok, sd_tok = (small[:, 96 + 16 * i:112 + 16 * i] for i in range(3))
        rs_tok, tmp_tok = (small[:, 160 + 16 * i:176 + 16 * i] for i in range(2))
        rw_sb = small[:, 192:208].rearrange("p (c e) -> p c e", c=2)
        rb_row = small[:, 208:216]
        spare_row = small[:, 216:217]
        minus_mean = att[:].rearrange("p q c v -> p (q c v)")[:, 0:P]
        wo_half = g_pre[:, 128:192]
        att_parts = att_n[:].rearrange("p c v -> p (c v)").bitcast(fp16)\
            .rearrange("p (c q s v) -> p c q s v", c=2, q=4, s=2)
        att_high, att_low = (att_parts[:, :, :, i, :].rearrange("p c q v -> p q c v") for i in range(2))
        att_turned = att_t[:].bitcast(fp16)
        z_stack_v = z_stack[:].rearrange("p (a l) (h n) -> p a l h n", a=2, h=2)

        xn = z_stack[:].rearrange("p l n -> p (l n)").bitcast(fp32).rearrange("p (n l) -> p n l", n=N_HALF)
        gate_b_all = x_rows[:].rearrange("p n l -> p (n l)")
        up_b_all = xn.rearrange("p n l -> p (n l)")
        down_b_all = et_flat
        qe_words = qe_flat.bitcast(fp32)
        x_t = [[half[:, TOK * k:TOK * k + TOK] for k in range(4)] for half in (qe_words, se_flat)]
        ws_flat = w_stage[:].rearrange("p k w -> p (k w)")
        def two(flat, at, size, dt=None, parts=None):
            out2 = []
            for i in range(2):
                t = flat[:, at + size * i:at + size * (i + 1)]
                t = t.bitcast(dt) if dt else t
                out2.append(t.rearrange("p (c t) -> p c t", c=parts) if parts else t)
            return out2

        xg = two(ws_flat, 0, L_COL)
        x_hi = two(ws_flat, 512, P, fp16, 2)
        x_lo = two(ws_flat, 768, P, fp16, 2)
        y_sum = two(ws_flat, 1024, L_COL)
        yw = two(ws_flat, 1536, L_COL)
        h_sb = two(ws_flat, 2048, FF)
        g_sum = two(ve_flat, 0, FF)
        g_silu = two(ve_flat, 1024, FF)
        u_sum = two(ve_flat, 2048, FF)
        h_hi = two(qe_words, 0, FF // 2, fp16, 4)
        h_lo = two(qe_words, 512, FF // 2, fp16, 4)
        r_place = se_flat.bitcast(fp16).rearrange("p (a t) -> p a t", a=ASSIGN)
        r_values = ve_flat[:, 0:ASSIGN * 3 * BLOCKS // 2].bitcast(fp16).rearrange("p (a t) -> p a t", a=ASSIGN)
        r_block = ve_flat[:, 1872:1872 + ASSIGN * BLOCKS // 2].bitcast(fp16).rearrange("p (a t) -> p a t", a=ASSIGN)
        r_iota128 = att_t[:, 0:128].bitcast(i32)
        iota_f = att_t[:, 128:256]
        r_thr = att_t[:, 256:272].bitcast(i32)
        thr_f = att_t[:, 272:288]
        r_tid = att_t[:, 288:304].bitcast(i32)
        tid_f = att_t[:, 304:320]
        r_rev = att_t[:, 320:328].bitcast(i32)
        rev_f = att_t[:, 328:336]
        an_flat = att_n[:].rearrange("p c v -> p (c v)")
        at_flat = att[:].rearrange("p q c v -> p (q c v)")
        r_logit = an_flat[:, 0:128].rearrange("p (n e) -> p n e", n=TILES)
        r_top = an_flat[:, 128:384].rearrange("p (k n e) -> p k n e", k=TOP_K, n=TILES)
        r_mark = an_flat[:, 384:512].rearrange("p (n e) -> p n e", n=TILES)
        r_sel = at_flat[:, 0:64].bitcast(fp16)
        r_incl = at_flat[:, 64:128].bitcast(fp16)
        r_keep, r_slot = at_flat[:, 128:256], at_flat[:, 256:384]
        r_rest = at_flat[:, 384:512].rearrange("p (n e) -> p n e", n=TILES)
        r_tmp = proj[:, 0:256].rearrange("p (k n e) -> p k n e", k=TOP_K, n=TILES)
        r_slots, r_w = proj[:, 256:288], proj[:, 288:320]
        r_m1, r_m2, r_first, r_exp, r_den = (proj[:, 320 + 16 * i:336 + 16 * i] for i in range(5))
        r_p, r_b = (proj[:, 400 + 32 * i:432 + 32 * i] for i in range(2))
        r_one8, r_nb = proj[:, 496:504], proj[:, 504:512]
        r_cum, r_base = g_pre[:, 480:488], g_pre[:, 488:496]
        rw_pad = maxes[:].rearrange("p a l -> p (a l)").rearrange("p (c e) -> p c e", c=2)
        logit_t = ve_flat[:, 0:TOK]
        r_cmp = k_hi[:].bitcast(fp32)[:, 0:128].rearrange("p (e k) -> p e k", e=EXPERTS)
        r_ints = q_hi[:].bitcast(i32)
        r_wh, r_wl = q_lo[:, 0:ASSIGN], q_lo[:, ASSIGN:2 * ASSIGN]
        r_ecmp = g_pre[:, 0:BLOCKS * EXPERTS].rearrange("p (b e) -> p b e", b=BLOCKS)
        r_tab = k_lo[:].bitcast(fp32)
        g_idx = [r_ints[:, 128 + i:129 + i] for i in range(2)]
        s_idx = [r_ints[:, 130 + i:131 + i] for i in range(2)]
        ga_flat = gate[:].rearrange("p a b -> p (a b)")
        t_gather, t_scatter, t_expert = (ga_flat[:, 64 * i:64 * i + BLOCKS].bitcast(i32) for i in range(3))
        t_weight = ga_flat[:, 192:192 + BLOCKS]

        def steps(eng, signal):
            count = [0]

            def step(ins):
                ins.then_inc(signal, 1)
                count[0] += 1
                eng.wait_ge(signal, count[0])
                return count[0]
            return step

        names = """
            const_p const_v dve_step x_in0 x_in1 x_in2 x_in3 par_in pairs_in pair_par_in r_in
            w_in0 w_in1 w_in2 w_prep ones_ready wide_ready pair_v pool_pair root_in root_out table_loaded
            stats_ready mean_ready negm_ready xcol_dve xcol_act cen_ready sq_ready
            ztok_ready zhi_ready zlo_ready zlo_last ztr_ready zst0 zst1 zst_last
            pe_prep pe_bias vec_copied bias_copied
            zpair_ready q_ps k_ps g_ps v_ps s_ps av_ps at_ps wo_ps
            qf_ready qh_ready kf_ready kh_ready q_lo_ready k_lo_ready qexp_hi_ready qexp_lo_ready
            max_ready sub_ready exp_ready et_ready vt_ready rden_ready norm_ready vb_ready
            gpre_ready gate_ready att_ready att_hi_ready att_lo_ready att_t_ready x1_ready w_hi_done w_lo_done
            rw_ready rt_ps rt_sb logit_ps lt_ready lt_ps rs_ready xn_act xn_pool rows_out x1_out
            route_p sel_ready route_ps shift_ready prob_ready den_ready wfirst_ready w_ready
            block_ready values_pool place_ready tab_ps tables_ready bias_rows up_rows zero_ready pad_out
            gcol_ready scol_ready x_got0 x_got1 xt_ps xh_ready xl_ready gu_ps gadd_ready silu_ready uadd_ready
            h_ready ht_ps hh_ready hl_ready y_ps yadd_ready y_ready y_scattered""".split()
        s = {n: sem(n) for n in names}

        token_rows = nc.dram_tensor("token_rows", (TOKENS, L_COL), fp32, kind="Internal").ap()
        block = ctx.enter_context(nc.Block())
        x_view = x[0].rearrange("d (h n) l -> h d n l", h=2)

        @block.sync
        def _(sp):
            for q in range(QUADS):
                for h in range(2):
                    sp.dma_start(x_rows[64 * h:64 * h + 64, 4 * q:4 * q + 4, :],
                                 x_view[h, :, 4 * q:4 * q + 4, :]).then_inc(s[f"x_in{q}"], 16)
            for h in range(2):
                rows = slice(64 * h, 64 * h + 64)
                for k, w in enumerate((Wq, Wk, Wv, Wg)):
                    sp.dma_start(w_raw[rows, 64 * k:64 * k + 64], w).then_inc(s["par_in"], 16)
                for col, v in ((g_col, ln_m_g), (b_col, ln_m_b), (bo_col, bo)):
                    sp.dma_start(col[rows, :], v.rearrange("(d a) -> d a", a=1)).then_inc(s["par_in"], 16)
                sp.dma_start(wo_half[rows, :], Wo).then_inc(s["par_in"], 16)
            sp.dma_start(bg_row, bg.partition_broadcast(P)).then_inc(s["par_in"], 16)
            sp.dma_start(rw_sb, router_w.rearrange("(c p) e -> p c e", p=P)).then_inc(s["r_in"], 16)
            sp.dma_start(rb_row, router_b.partition_broadcast(P)).then_inc(s["r_in"], 16)
            for e in range(EXPERTS):
                parts = (gate_w[e].rearrange("(c p) i -> p c i", p=P), up_w[e].rearrange("(c p) i -> p c i", p=P),
                         down_w[e].rearrange("(c p) l -> p c l", p=P))
                for k in range(3):
                    if e >= 1:
                        sp.wait_ge(s["w_hi_done"], 3 * (e - 1) + k + 1)
                        sp.wait_ge(s["w_lo_done"], 3 * (e - 1) + k + 1)
                    c = 2 if k < 2 else 4
                    sp.dma_start(w_stage[:, k, :].rearrange("p (c i) -> p c i", c=c),
                                 parts[k]).then_inc(s[f"w_in{k}"], 16)
            o_view = out[0:TOKENS, :].rearrange("(d h n) l -> h d n l", h=2, n=N_HALF)
            for part in range(2):
                sp.wait_ge(s["x1_ready"], PAIRS * (part + 1))
                cols = slice(L_HALF * part, L_HALF * (part + 1))
                for h in range(2):
                    sp.dma_start(o_view[h, :, :, cols], x_rows[64 * h:64 * h + 64, :, cols])\
                        .then_inc(s["x1_out"], 16)
            sp.wait_ge(s["zero_ready"], 1)
            sp.dma_start(out[TOKENS:TOKENS + SLOTS, :], ws_flat[:, 0:L_COL]).then_inc(s["pad_out"], 16)
            sp.dma_start(down_b_all, down_b.rearrange("e l -> (e l)").partition_broadcast(P)).then_inc(s["bias_rows"], 16)
            r_view = token_rows.rearrange("(d h n) l -> h d n l", h=2, n=N_HALF)
            for part in range(2):
                if part == 0:
                    sp.wait_ge(s["xn_act"], TILES // 2)
                else:
                    sp.wait_ge(s["xn_act"], TILES - 4)
                    sp.wait_ge(s["xn_pool"], 4)
                tiles = slice(TILES // 2 * part, TILES // 2 * (part + 1))
                for h in range(2):
                    sp.dma_start(r_view[h, :, tiles, :], xn[64 * h:64 * h + 64, tiles, :])\
                        .then_inc(s["rows_out"], 16)
            sp.wait_ge(s["x1_out"], 64)
            sp.wait_ge(s["rt_ps"], 2 * (TILES // 4))
            sp.dma_start(gate_b_all, gate_b.rearrange("e i -> (e i)").partition_broadcast(P)).then_inc(s["bias_rows"], 16)
            sp.wait_ge(s["rows_out"], 64)
            up_rows = up_b.rearrange("e i -> (e i)")
            for part in range(2):
                if part == 1:
                    sp.wait_ge(s["x_got0"], 16)
                half = slice(EXPERTS * FF // 2 * part, EXPERTS * FF // 2 * (part + 1))
                sp.dma_start(up_b_all[:, half], up_rows[half].partition_broadcast(P)).then_inc(s["up_rows"], 16)
            sp.wait_ge(s["x1_out"], 64)
            sp.wait_ge(s["pad_out"], 16)
            sp.wait_ge(s["y_scattered"], 16 * BLOCKS)

        @block.gpsimd
        def _(pool):
            const = steps(pool, s["const_p"])

            def eye(t):
                const(pool.memset(t, 0.0))
                const(pool.affine_select(out=t, in_=t, compare_op=ALU.not_equal, fill=1.0, base=0,
                                         pattern=[[-1, t.shape[1]]], channel_multiplier=1))
            eye(ident[:])
            eye(ident_h[:])
            for h in range(2):
                eye(pick[32 * h:32 * h + 32, :])
            const(pool.iota(small_i[:, 0:1], pattern=[[0, 1]], base=0, channel_multiplier=1))
            mean_b = pair_s[:, 0:32].unsqueeze(2).broadcast_to([32, N_SEQ, P_DIM])
            rstd_b = pair_s[:, 64:96].unsqueeze(2).broadcast_to([32, N_SEQ, P_DIM])
            pair = steps(pool, s["pool_pair"])
            pool.wait_ge(s["pair_v"], 1)
            pair(pool.tensor_tensor(pr[0], pr[0], mean_b, ALU.subtract))
            pair(pool.tensor_tensor(pr[1], pr[0], pr[0], ALU.mult))
            prep = steps(pool, s["w_prep"])
            prep(pool.memset(w_fold, 0.0))
            prep(pool.memset(w_lo[64:128, :], 0.0))
            prep(pool.memset(wo_parts[:], 0.0))
            pool.wait_ge(s["pair_par_in"], 48)
            pool.wait_ge(s["pair_v"], 2)
            pair(pool.tensor_tensor(pr[0], pr[0], rstd_b, ALU.mult))
            pair(pool.tensor_tensor(pr[0], pr[0], pair_g.unsqueeze(1).broadcast_to([32, N_SEQ, P_DIM]), ALU.mult))
            pair(pool.tensor_tensor(pr[0], pr[0], pair_b.unsqueeze(1).broadcast_to([32, N_SEQ, P_DIM]), ALU.add))

            def prepare_weights():
                pool.wait_ge(s["par_in"], 16 * N_PAR)
                prep(pool.tensor_scalar(w_fold[:, 0:128], w_raw[:, 0:128], g_col, None, ALU.mult))
                prep(pool.tensor_scalar(w_fold[:, 384:448], w_raw[:, 192:256], g_col, None, ALU.mult))
                for h in range(GROUP):
                    c0 = (GROUP * D_HEAD + D_HEAD) * h
                    prep(pool.tensor_scalar(
                        w_fold[:, 128:384].rearrange("p (g r) -> p g r", g=2)[:, :, c0:c0 + D_HEAD],
                        w_raw[:, 128:192].rearrange("p (g r) -> p g r", g=2)[:, :, 8 * h:8 * h + 8],
                        g_col, None, ALU.mult))

            def split_weights():
                prep(pool.tensor_tensor(w_lo[0:64, :], w_fold[0:64, :], w_hi[0:64, :], ALU.subtract))
                prep(pool.tensor_scalar(wo_half, wo_half, 0.5, None, ALU.mult))
                prep(pool.tensor_copy(wo_parts[:, 0, :], wo_half))
                prep(pool.tensor_tensor(wo_parts[0:64, 1, :], wo_half[0:64, :], wo_parts[0:64, 0, :], ALU.subtract))

            for q in range(QUADS):
                for h in range(2 if q < QUADS - 1 else 1):
                    t = 2 * q + h
                    pool.wait_ge(s["zhi_ready"], t + 1)
                    pool.tensor_tensor(z_parts[h][:, :, 1, :], z_tok[h].rearrange("p (t d) -> p t d", t=8),
                                       z_parts[h][:, :, 0, :], ALU.subtract).then_inc(s["zlo_ready"], 1)
                if q == 0:
                    prepare_weights()
                if q == 1:
                    prep(pool.tensor_copy(w_hi[:], w_fold))
                if q == 2:
                    split_weights()

            def parts_low(j):
                pool.wait_ge(s["qh_ready"], j + 1)
                pool.tensor_tensor(q_lo[:], proj[:], q_hi[:], ALU.subtract).then_inc(s["q_lo_ready"], 1)
                pool.wait_ge(s["kh_ready"], j + 1)
                pool.tensor_tensor(k_lo[:], att_t[:], k_hi[:], ALU.subtract).then_inc(s["k_lo_ready"], 1)

            def value_bias(j, c):
                pool.wait_ge(s["norm_ready"], 2 * j + c + 1)
                t = att_n[:, c, :].rearrange("p (q v) -> p q v", q=4)
                pool.tensor_tensor(t, t, v_row[:].unsqueeze(1).broadcast_to([P, 4, D_MODEL]),
                                   ALU.add).then_inc(s["vb_ready"], 1)

            def weights_low(e, pieces):
                for k in pieces:
                    pool.wait_ge(s["w_hi_done"], 3 * e + k + 1)
                    hi = w_exp[:, bass.ds(e * 2 * W_EXP + k * W_PIECE, W_PIECE)]
                    lo = w_exp[:, bass.ds(e * 2 * W_EXP + W_EXP + k * W_PIECE, W_PIECE)]
                    pool.tensor_tensor(lo, w_stage[:, k, :], hi, ALU.subtract).then_inc(s["w_lo_done"], 1)

            def pool_step(j, first=False, last=False):
                weights_low(j, [0])
                if not first:
                    value_bias(j - 1, 0)
                if not last:
                    parts_low(j + 1)
                if not first:
                    value_bias(j - 1, 1)
                if not last:
                    weights_low(j, [1])
                if not first:
                    pool.wait_ge(s["att_hi_ready"], j)
                    pool.tensor_tensor(att_low, att[:], att_high, ALU.subtract).then_inc(s["att_lo_ready"], 1)
                weights_low(j, [1, 2] if last else [2])

            parts_low(0)
            ones = steps(pool, s["ones_ready"])
            for t in v_tile:
                for c in range(2):
                    ones(pool.memset(t[:, c, :, :, 32:36].rearrange("p g l h -> p (g l) h"), 0.0))
                    for h in range(GROUP):
                        ones(pool.memset(t[32 * h:32 * h + 32, c, :, :, 32 + h].rearrange("p g l -> p (g l)"), 1.0))
            pool_step(0, first=True)
            pool_step(1)
            with pool.Fori(0, PAIRS // 2 - 2) as i:
                pool_step(2 * i + 2)
                pool_step(2 * i + 3)
            pool_step(PAIRS - 2)
            pool_step(PAIRS - 1, last=True)
            value_bias(PAIRS - 1, 0)
            value_bias(PAIRS - 1, 1)

            pool.wait_ge(s["x1_ready"], 2 * PAIRS)
            n_r = [0]

            def table(ins):
                ins.then_inc(s["route_p"], 1)
                n_r[0] += 1
                pool.wait_ge(s["route_p"], n_r[0])
            table(pool.memset(ws_flat[:, 0:L_COL], 0.0))
            pool.sem_inc(s["zero_ready"], 1)
            table(pool.memset(before, 0.0))
            table(pool.affine_select(out=before, in_=before, compare_op=ALU.is_ge, fill=-1.0, base=-1,
                                     pattern=[[1, P]], channel_multiplier=-1))
            table(pool.iota(r_iota128, pattern=[[1, P]], base=0, channel_multiplier=0))
            table(pool.iota(r_thr, pattern=[[P, TILES]], base=0, channel_multiplier=0))
            for h in range(2):
                table(pool.iota(r_tid[64 * h:64 * h + 64, :], pattern=[[1, TILES]], base=1 + N_HALF * h,
                                channel_multiplier=N_SEQ))
            table(pool.iota(r_rev, pattern=[[-1, EXPERTS]], base=EXPERTS, channel_multiplier=0))
            table(pool.memset(r_keep, 1.0))
            table(pool.memset(r_keep.rearrange("p (e n) -> p e n", e=EXPERTS)[:, :, 0:1], 0.0))
            table(pool.memset(r_one8, 1.0))
            assert n_r[0] == N_TABLES
            pool.wait_ge(s["rs_ready"], 1)
            for n in range(TILES - 4, TILES):
                pool.tensor_scalar(xn[:, n, :], x_rows[:, n, :], mv[:, n, 0:1], rs_col[:, n:n + 1],
                                   ALU.subtract, ALU.mult).then_inc(s["xn_pool"], 1)
            pool.wait_ge(s["prob_ready"], 1)
            pool.tensor_scalar(r_den, r_exp, 1.0, None, ALU.add).then_inc(s["den_ready"], 1)
            weight = steps(pool, s["w_ready"])
            pool.wait_ge(s["wfirst_ready"], 1)
            weight(pool.tensor_tensor(r_w[:, TILES:2 * TILES], r_exp, r_w[:, 0:TILES], ALU.mult))
            weight(pool.tensor_copy(r_wh, r_w))
            weight(pool.tensor_tensor(r_wl, r_w, r_wh, ALU.subtract))
            pool.wait_ge(s["block_ready"], 1)
            for piece in range(PIECES):
                if piece == PIECES // 2:
                    pool.tensor_tensor(r_values[:, TILES:, 0:BLOCKS], r_block[:, TILES:, :],
                                       tid_f.unsqueeze(2).broadcast_to([P, TILES, BLOCKS]), ALU.mult)                        .then_inc(s["values_pool"], 1)
                cols = slice(PIECE * piece, PIECE * (piece + 1))
                for part, w in ((1, r_wh), (2, r_wl)):
                    pool.tensor_tensor(r_values[:, cols, BLOCKS * part:BLOCKS * (part + 1)], r_block[:, cols, :],
                                       w[:, cols].unsqueeze(2).broadcast_to([P, PIECE, BLOCKS]), ALU.mult)\
                        .then_inc(s["values_pool"], 1)

            pool.wait_ge(s["tables_ready"], 1)
            pool.wait_ge(s["rows_out"], 64)
            pool.wait_ge(s["x1_out"], 64)
            pool.wait_ge(s["pad_out"], 16)

            hold, one_word = [small[0:1, 152 + i:153 + i] for i in range(4)], t_weight[0:1, 0:1]

            def gather(turn, par, first=False):
                b = 2 * turn + par
                if not first:
                    pool.wait_ge(s["xt_ps"], b - 1)
                    pool.wait_ge(s[f"x_got{par}"], 16 * turn)
                    pool.wait_ge(s["gcol_ready"], b)
                    pool.tensor_tensor(hold[0], one_word, one_word, ALU.mult)
                pool.tensor_copy(g_idx[par], t_gather[:, bass.ds(b, 1)]).then_inc(s["gcol_ready"], 1)
                pool.wait_ge(s["gcol_ready"], b + 1)
                pool.tensor_tensor(hold[1], one_word, one_word, ALU.mult)
                pool.indirect_dma_start(xg[par], None, token_rows, bass.IndirectOffsetOnAxis(g_idx[par], 0))\
                    .then_inc(s[f"x_got{par}"], 16)

            def scatter(b, par, first=False):
                if not first:
                    pool.wait_ge(s["y_scattered"], 16 * b)
                    pool.wait_ge(s["scol_ready"], b)
                    pool.tensor_tensor(hold[2], one_word, one_word, ALU.mult)
                pool.tensor_copy(s_idx[par], t_scatter[:, bass.ds(b, 1)]).then_inc(s["scol_ready"], 1)
                pool.wait_ge(s["scol_ready"], b + 1)
                pool.wait_ge(s["y_ready"], b + 1)
                pool.tensor_tensor(hold[3], one_word, one_word, ALU.mult)
                pool.indirect_dma_start(out, bass.IndirectOffsetOnAxis(s_idx[par], 0), yw[par], None,
                                        compute_op=ALU.add).then_inc(s["y_scattered"], 16)

            gather(0, 0, first=True)
            gather(0, 1, first=True)
            gather(1, 0)
            gather(1, 1)
            scatter(0, 0, first=True)
            with pool.Fori(0, 2 * BODY - 1) as i:
                gather(i + 2, 0)
                scatter(2 * i + 1, 1)
                gather(i + 2, 1)
                scatter(2 * i + 2, 0)
            gather(2 * BODY + 1, 0)
            for b in range(4 * BODY - 1, BLOCKS):
                scatter(b, b % 2)
        @block.tensor
        def _(pe):
            def keep_warm(count, free_bank=bank[7]):
                for _ in range(count):
                    pe.matmul(free_bank[:], ident_h[:], ones_h[:].unsqueeze(1).broadcast_to([P, 4, P]),
                              start=True, stop=True)

            def fold_vectors():
                pe.wait_ge(s["wide_ready"], 1)
                for h in range(2):
                    for k in range(2):
                        pe.matmul(bank[7][64 * h:64 * h + 64, k:k + 1], w_raw[0:64, 64 * k:64 * k + 64],
                                  b_col[0:64, :], start=True, stop=True)
                pe.wait_ge(s["r_in"], 32)
                for c in range(2):
                    pe.matmul(bank[7][:, 8:16], minus_mean, rw_sb[:, c, :], start=(c == 0), stop=(c == 1))
                pe.matmul(bank[7][:, 128:256], b_wide, w_raw[0:64, 128:256], start=True, stop=True)\
                    .then_inc(s["pe_prep"], 1)

            def pair_bias():
                pe.wait_ge(s["pair_v"], 3)
                out_v = bank[2][0:32, 0:HEADS * N_SEQ].rearrange("p (h i) -> p h i", i=N_SEQ)
                for i in range(N_SEQ):
                    mm = pe.matmul(out_v[:, :, i], pr[2][:, i, :], wb_sb, start=True, stop=True)
                mm.then_inc(s["pe_bias"], 1)

            def centre(q):
                if q == 1:
                    pe.wait_ge(s["xcol_act"], 4)
                else:
                    pe.wait_ge(s["xcol_dve"], 4 * max(q, 1))
                if q == 0:
                    pe.wait_ge(s["const_v"], N_CENTER)
                for h in range(2):
                    if q == 3:
                        pe.wait_ge(s["ztok_ready"], h + 1)
                    for i in range(4):
                        mm = pe.matmul(centred[q][h][:, P * i:P * i + P],
                                       x_col[q][i][:, L_HALF * h:L_HALF * h + L_HALF], center,
                                       start=True, stop=True)
                    mm.then_inc(s["cen_ready"], 1)

            def stack_tokens(q):
                for h in range(2):
                    if q == QUADS - 1 and h == 1:
                        pe.wait_ge(s["zlo_last"], 1)
                    else:
                        pe.wait_ge(s["zlo_ready"], 2 * q + h + 1)
                    if 1 <= q < QUADS - 1:
                        pe.wait_ge(s[f"zst{h}"], q)
                    dst = stacked[q][h][:].bitcast(fp16)
                    for t in range(8):
                        mm = pe.transpose(dst[:, P * t:P * t + P], z_parts[h][:, t, :, :].rearrange("p s d -> p (s d)"),
                                          ident_h[:])
                    mm.then_inc(s["ztr_ready"], 1)

            pe.wait_ge(s["const_p"], 9)
            pe.wait_ge(s["const_v"], N_CENTER)
            centre(0)
            centre(1)
            centre(2)
            stack_tokens(0)
            centre(3)
            stack_tokens(1)
            pe.wait_ge(s["ztok_ready"], 4)
            pair_bias()
            pe.wait_ge(s["ztok_ready"], 6)
            fold_vectors()
            stack_tokens(2)
            stack_tokens(3)

            SC = [[bank[0], bank[1]], [bank[2], bank[3]]]
            PJ = [bank[4], bank[5]]
            MS = bank[7]

            def project(j, first=False):
                pe.wait_ge(s["zpair_ready"], j + 1)
                if first:
                    pe.wait_ge(s["w_prep"], N_PREP)
                    pe.wait_ge(s["zst0"], QUADS - 1)
                    pe.wait_ge(s["zst1"], QUADS - 1)
                if not first:
                    pe.wait_ge(s["vt_ready"], 4 * (j - 1) + 3)
                for k, ready in ((0, "q_ps"), (1, "k_ps")):
                    if k == 1 and not first:
                        pe.wait_ge(s["vt_ready"], 4 * j)
                    for c in range(2):
                        for w, st in ((w_hi, True), (w_lo, False)):
                            mm = pe.matmul(PJ[k][64 * c:64 * c + 64, :], w[:, 64 * k:64 * k + 64],
                                           z_pair[:, TOK * c:TOK * c + TOK], start=st, stop=not st)
                    mm.then_inc(s[ready], 1)

            def gates(j, first=False, second=False):
                if first:
                    pe.wait_ge(s["zst_last"], 1)
                else:
                    pe.wait_ge(s["gpre_ready"], j)
                if not first and not second:
                    pe.wait_ge(s["x1_ready"], 2 * (j - 2))
                for t in range(8):
                    for w, st in ((w_hi, True), (w_lo, False)):
                        mm = pe.matmul(MS[:, 64 * t:64 * t + 64], z_pair[:, P * t:P * t + P], w[:, 384:448],
                                       start=st, stop=not st)
                mm.then_inc(s["g_ps"], 1)

            def values(j, c):
                for g in range(2):
                    if c == 0:
                        pe.wait_ge(s["qf_ready"] if g == 0 else s["kf_ready"], j + 1)
                    else:
                        pe.wait_ge(s["vt_ready"], 4 * j + g + 1)
                    for w, st in ((w_hi, True), (w_lo, False)):
                        mm = pe.matmul(PJ[g][:], w[:, 128 + P * g:256 + P * g],
                                       z_pair[:, TOK * c:TOK * c + TOK], start=st, stop=not st)
                    mm.then_inc(s["v_ps"], 1)

            def scores(j, c, first=False):
                if not first:
                    pe.wait_ge(s["sub_ready"], 4 * (j - 1) + 2 * c + 2)
                if c == 0:
                    pe.wait_ge(s["qexp_hi_ready"], GROUP * (j + 1))
                    pe.wait_ge(s["qexp_lo_ready"], GROUP * (j + 1))
                    pe.wait_ge(s["k_lo_ready"], j + 1)
                for g in range(2):
                    dst = SC[c][g]
                    pe.matmul(dst[:], bias_t[:, P * g:P * g + P],
                              pick[:].unsqueeze(1).broadcast_to([64, CHUNK, N_SEQ]), start=True, stop=False,
                              skip_group_check=True)
                for i in range(CHUNK):
                    for g in range(2):
                        dst = SC[c][g]
                        r0 = 64 * c + 32 * g
                        for part, k in ((0, k_hi), (0, k_lo), (1, k_hi)):
                            mm = pe.matmul(dst[:, 32 * i:32 * i + 32],
                                           q_exp[r0:r0 + 32, part, i, :, :].rearrange("p h n -> p (h n)"),
                                           k[r0:r0 + 32, 32 * i:32 * i + 32], start=False, stop=(part == 1),
                                           skip_group_check=True)
                mm.then_inc(s["s_ps"], 1)

            def attend(j, c, par, out_bank=bank[6], waits=True):
                pe.wait_ge(s["et_ready"], 2 * j + c + 1)
                pe.wait_ge(s["vt_ready"], 4 * (j + 1))
                if c == 1 and waits:
                    pe.wait_ge(s["norm_ready"], 2 * j + c)
                for q in range(4):
                    for g in range(2):
                        for u in range(4):
                            i = 4 * q + u
                            mm = pe.matmul(out_bank[32 * u:32 * u + 32, 72 * q + VCOL * g:72 * q + VCOL * g + VCOL],
                                           e_t[:, c, g, 32 * i:32 * i + 32], v_tile[par][:, c, g, i, :],
                                           start=True, stop=True)
                mm.then_inc(s["av_ps"], 1)

            def turn_result(j, last=False):
                pe.wait_ge(s["att_lo_ready"], j + 1)
                if last:
                    pe.wait_ge(s["x1_ready"], 2 * j)
                else:
                    pe.wait_ge(s["gpre_ready"], j + 3)
                dst = MS[:].bitcast(fp16)
                for c in range(2):
                    for q in range(4):
                        mm = pe.transpose(dst[:, TOK * c + P * q:TOK * c + P * q + P],
                                          att_parts[:, c, q, :, :].rearrange("p s v -> p (s v)"), ident_h[:])
                mm.then_inc(s["at_ps"], 1)

            def project_out(j):
                pe.wait_ge(s["att_t_ready"], j + 1)
                at_v = att_turned.rearrange("p (c l h n) -> p c l h n", c=2, l=CHUNK, h=2)
                for c in range(2):
                    for h in range(2):
                        for part in range(2):
                            mm = pe.matmul(MS[64 * h:64 * h + 64, 256 * c:256 * c + 256], wo_parts[:, part, :],
                                           at_v[:, c, :, h, :], start=(part == 0), stop=(part == 1))
                mm.then_inc(s["wo_ps"], 1)

            def pe_step(j, par, first=False, second=False):
                scores(j, 0, first=first)
                if first:
                    values(0, 1)
                scores(j, 1, first=first)
                if not first and not second:
                    turn_result(j - 2)
                if not first:
                    attend(j - 1, 0, 1 - par)
                if not first and not second:
                    project_out(j - 2)
                project(j + 1)
                gates(j + 1, second=first or second)
                values(j + 1, 0)
                if not first:
                    attend(j - 1, 1, 1 - par)
                values(j + 1, 1)

            pe.wait_ge(s["bias_copied"], 2)
            project(0, first=True)
            gates(0, first=True)
            values(0, 0)
            pe_step(0, 0, first=True)
            pe.wait_ge(s["ones_ready"], N_ONES)
            pe_step(1, 1, second=True)
            with pe.Fori(0, PAIRS // 2 - 2) as i:
                pe_step(2 * i + 2, 0)
                pe_step(2 * i + 3, 1)
            pe_step(PAIRS - 2, 0)

            def router_tokens(c, k):
                if c == 1:
                    pe.wait_ge(s["rt_sb"], k + 1)
                for t in range(4):
                    mm = pe.transpose(bank[k][:, P * t:P * t + P], x_rows[:, 4 * k + t, P * c:P * c + P], ident[:])
                mm.then_inc(s["rt_ps"], 1)

            def router_logits(c, k):
                pe.wait_ge(s["rt_sb"], 4 * c + k + 1)
                mm = pe.matmul(bank[4][32 * k:32 * k + 32, :], rw_pad[:, c, :], x_t[c][k], start=(c == 0),
                               stop=(c == 1), skip_group_check=True)
                if c == 1 and k == 3:
                    mm.then_inc(s["logit_ps"], 1)

            scores(PAIRS - 1, 0)
            scores(PAIRS - 1, 1)
            turn_result(PAIRS - 3)
            attend(PAIRS - 2, 0, 0)
            project_out(PAIRS - 3)
            pe.wait_ge(s["vt_ready"], 4 * PAIRS)
            attend(PAIRS - 2, 1, 0, out_bank=bank[4], waits=False)
            pe.wait_ge(s["x1_ready"], PAIRS)
            pe.wait_ge(s["sub_ready"], 4 * PAIRS)
            router_tokens(0, 0)
            router_tokens(0, 1)
            attend(PAIRS - 1, 0, 1, out_bank=bank[5], waits=False)
            turn_result(PAIRS - 2, last=True)
            router_tokens(0, 2)
            pe.wait_ge(s["rw_ready"], 2)
            pe.wait_ge(s["norm_ready"], 2 * (PAIRS - 1))
            router_logits(0, 0)
            attend(PAIRS - 1, 1, 1)
            project_out(PAIRS - 2)
            router_tokens(0, 3)
            router_logits(0, 1)
            pe.wait_ge(s["norm_ready"], 2 * PAIRS - 1)
            keep_warm(11, bank[5])
            turn_result(PAIRS - 1, last=True)
            router_logits(0, 2)
            keep_warm(4, bank[5])
            project_out(PAIRS - 1)
            router_logits(0, 3)
            keep_warm(4, bank[5])

            pe.wait_ge(s["x1_ready"], 2 * PAIRS)
            router_tokens(1, 0)
            router_tokens(1, 1)
            router_logits(1, 0)
            router_tokens(1, 2)
            router_logits(1, 1)
            router_tokens(1, 3)
            router_logits(1, 2)
            router_logits(1, 3)
            pe.wait_ge(s["lt_ready"], 1)
            for k in range(4):
                mm = pe.transpose(bank[6][:, P * k:P * k + P], logit_t[:, P * k:P * k + P], ident[:])
            mm.then_inc(s["lt_ps"], 1)

            pe.wait_ge(s["sel_ready"], 1)
            pe.matmul(bank[3][:, 128:136], ones_h[:], r_incl[:, TILES - 1:EXPERTS * TILES:TILES], start=True, stop=True)
            pe.matmul(bank[3][:, 0:128], before, r_sel, start=True, stop=False, skip_group_check=True)
            pe.matmul(bank[3][:, 0:128], ones_h[:], r_incl, start=False, stop=True, skip_group_check=True)\
                .then_inc(s["route_ps"], 1)
            pe.wait_ge(s["block_ready"], 1)
            keep_warm(8)
            for a in range(ASSIGN):
                if a % PIECE == 0:
                    piece = a // PIECE
                    pe.wait_ge(s["place_ready"], piece + 1)
                    pe.wait_ge(s["values_pool"], 2 * (piece + 1) + (piece >= PIECES // 2))
                mm = pe.matmul(bank[4][:, 0:3 * BLOCKS], r_place[:, a, :], r_values[:, a, :], start=(a == 0),
                               stop=(a == ASSIGN - 1))
            mm.then_inc(s["tab_ps"], 1)
            keep_warm(21)

            GU = [[bank[0], bank[1]], [bank[2], bank[3]]]
            XT, HT, YB = bank[4], bank[5], bank[6]

            expert_reg = [pe.alloc_register(f"pe_expert{i}") for i in range(2)]

            def load_expert(b, par):
                pe.reg_load(expert_reg[par], t_expert[0:1, bass.ds(b, 1)])

            def weights_of(par):
                return pe.snap(expert_reg[par], min_val=0, max_val=EXPERTS - 1) * (2 * W_EXP)

            def tokens_in(turn, par, first=False):
                b = 2 * turn + par
                pe.wait_ge(s[f"x_got{par}"], 16 * (turn + 1))
                if not first:
                    pe.wait_ge(s["xl_ready"], b)
                for c in range(2):
                    mm = pe.transpose(XT[:, P * c:P * c + P], xg[par][:, P * c:P * c + P], ident[:])
                mm.then_inc(s["xt_ps"], 1)

            def hidden(b, par, k, e, first=False):
                if k == 0:
                    pe.wait_ge(s["xl_ready"], b + 1)
                if not first:
                    pe.wait_ge(s["gadd_ready"] if k == 0 else s["uadd_ready"], b - 1)
                n = 0
                for xs, w in ((x_hi, 0), (x_hi, 1), (x_lo, 0)):
                    for c in range(2):
                        mm = pe.matmul(GU[par][k][:], xs[par][:, c, :],
                                       w_exp[:, w * W_EXP + k * W_PIECE + c * FF:][:, bass.ds(e, FF)],
                                       start=(n == 0), stop=(n == 5))
                        n += 1
                mm.then_inc(s["gu_ps"], 1)

            def hidden_turned(b, par, first=False):
                pe.wait_ge(s["h_ready"], b + 1)
                if not first:
                    pe.wait_ge(s["hl_ready"], b)
                for c in range(4):
                    mm = pe.transpose(HT[:, P * c:P * c + P], h_sb[par][:, P * c:P * c + P], ident[:])
                mm.then_inc(s["ht_ps"], 1)

            def down(b, par, e, first=False):
                pe.wait_ge(s["hl_ready"], b + 1)
                if not first:
                    pe.wait_ge(s["yadd_ready"], b)
                n = 0
                for c in range(4):
                    for hs, w in ((h_hi, 0), (h_lo, 0), (h_hi, 1)):
                        mm = pe.matmul(YB[:, 0:L_COL], hs[par][:, c, :],
                                       w_exp[:, w * W_EXP + 2 * W_PIECE + c * L_COL:][:, bass.ds(e, L_COL)],
                                       start=(n == 0), stop=(n == 11))
                        n += 1
                mm.then_inc(s["y_ps"], 1)

            def pe_block(turn, par, first=False, more=2):
                b = 2 * turn + par
                if more >= 1:
                    e1 = weights_of(1 - par)
                    hidden(b + 1, 1 - par, 0, e1, first=first)
                hidden_turned(b, par, first=first)
                if more >= 1:
                    hidden(b + 1, 1 - par, 1, e1, first=first)
                e0 = weights_of(par)
                if more >= 2:
                    load_expert(b + 2, par)
                    tokens_in(turn + 1, par)
                down(b, par, e0, first=first)

            pe.wait_ge(s["tables_ready"], 1)
            load_expert(0, 0)
            load_expert(1, 1)
            tokens_in(0, 0, first=True)
            keep_warm(4)
            e0 = weights_of(0)
            hidden(0, 0, 0, e0, first=True)
            tokens_in(0, 1)
            hidden(0, 0, 1, e0, first=True)
            pe_block(0, 0, first=True)
            with pe.Fori(0, BODY) as i:
                pe_block(2 * i, 1)
                pe_block(2 * i + 1, 0)
                pe_block(2 * i + 1, 1)
                pe_block(2 * i + 2, 0)
            pe_block(2 * BODY, 1, more=1)
            pe_block(2 * BODY + 1, 0, more=0)

        @block.scalar
        def _(act):
            act.dma_start(pr[0], pairs[0].rearrange("i j c -> j i c")).then_inc(s["pairs_in"], 16)
            act.dma_start(pair_g, ln_p_g.partition_broadcast(32)).then_inc(s["pair_par_in"], 16)
            act.dma_start(pair_b, ln_p_b.partition_broadcast(32)).then_inc(s["pair_par_in"], 16)
            act.dma_start(wb_sb, Wb).then_inc(s["pair_par_in"], 16)

            def root(k, dst, src):
                act.wait_ge(s["root_in"], k + 1)
                act.activation(dst, src, ACT.Sqrt).then_inc(s["root_out"], 1)

            def stack_out(q, h):
                act.wait_ge(s["ztr_ready"], 2 * q + h + 1)
                act.activation(z_stack_v[:, h, :, :, 4 * q:4 * q + 4],
                               stacked[q][h][:].bitcast(fp16).rearrange("p (i h l) -> p l h i", i=4, h=2),
                               ACT.Copy).then_inc(s[f"zst{h}"], 1)

            root(0, pair_s[:, 96:128], pair_s[:, 32:64])
            root(1, sd_col, var_col)
            act.wait_ge(s["negm_ready"], 1)
            for i in range(4):
                n = 4 + i
                act.activation(x_col[1][i], x_rows[:, n, :], ACT.Identity, bias=neg_mean[:, n:n + 1],
                               scale=rs_col[:, n:n + 1]).then_inc(s["xcol_act"], 1)

            def squared(q):
                for h in range(2):
                    act.wait_ge(s["cen_ready"], 2 * q + h + 1)
                    if q >= 1:
                        act.wait_ge(s["root_in"], q + 2)
                    act.activation(squares[h], centred[q][h][:], ACT.Square).then_inc(s["sq_ready"], 1)

            squared(0)
            for q in range(QUADS):
                root(q + 2, sd_tok, var_tok)
                if q + 1 < QUADS:
                    squared(q + 1)
                if 1 <= q < QUADS - 1:
                    stack_out(q - 1, 1)
                for h in range(2):
                    act.wait_ge(s["ztok_ready"], 2 * q + h + 1)
                    if q >= 1:
                        act.wait_ge(s["ztr_ready"], 2 * (q - 1) + h + 1)
                    act.activation(z_parts[h][:, :, 0, :], z_tok[h].rearrange("p (t d) -> p t d", t=8),
                                   ACT.Copy).then_inc(s["zhi_ready"], 1)
                if q == QUADS - 1:
                    stack_out(q - 1, 1)
                if q >= 1:
                    stack_out(q - 1, 0)
            stack_out(QUADS - 1, 0)

            def parts_high(j, first=False, early=False):
                act.wait_ge(s["q_ps"], j + 1)
                if not first:
                    act.wait_ge(s["q_lo_ready"], j)
                act.activation(proj[:], bank[4][:], ACT.Identity, bias=qb_col, scale=Q_SCALE)\
                    .then_inc(s["qf_ready"], 1)
                act.wait_ge(s["qf_ready"], j + 1)
                if not first:
                    act.wait_ge(s["qexp_hi_ready"], GROUP * j)
                act.activation(q_hi[:], proj[:], ACT.Copy).then_inc(s["qh_ready"], 1)
                act.wait_ge(s["k_ps"], j + 1)
                if not first:
                    act.wait_ge(s["s_ps"], 2 * j)
                if not early:
                    act.wait_ge(s["wo_ps"], j - 2)
                act.activation(att_t[:], bank[5][:], ACT.Identity, bias=kb_col).then_inc(s["kf_ready"], 1)
                act.wait_ge(s["kf_ready"], j + 1)
                act.activation(k_hi[:], att_t[:], ACT.Copy).then_inc(s["kh_ready"], 1)

            def spread_queries_high(j):
                act.wait_ge(s["qh_ready"], j + 1)
                for h in range(GROUP):
                    act.activation(q_exp[:, 0, :, h, :], q_hi[:].rearrange("p (l n) -> p l n", l=CHUNK),
                                   ACT.Copy, scale=head_mask[:, h:h + 1]).then_inc(s["qexp_hi_ready"], 1)

            def gate_tanh(j, par, early=False):
                act.wait_ge(s["gpre_ready"], j + 1)
                if not early:
                    act.wait_ge(s["att_ready"], 2 * (j - 1))
                act.activation(gate[:, par, :], g_pre[:], ACT.Tanh, scale=0.5).then_inc(s["gate_ready"], 1)

            def exps(j, c):
                act.wait_ge(s["sub_ready"], 4 * j + 2 * c + 2)
                act.activation(s_exp[:, c, :, :], s_exp[:, c, :, :], ACT.Exp).then_inc(s["exp_ready"], 1)

            def weights_high(e, k):
                act.wait_ge(s[f"w_in{k}"], 16 * (e + 1))
                act.activation(w_exp[:, bass.ds(e * 2 * W_EXP + k * W_PIECE, W_PIECE)], w_stage[:, k, :],
                               ACT.Copy).then_inc(s["w_hi_done"], 1)

            def turned_out(j, last=False):
                act.wait_ge(s["at_ps"], j + 1)
                if last:
                    act.wait_ge(s["wo_ps"], j)
                else:
                    act.wait_ge(s["k_lo_ready"], j + 3)
                act.activation(att_turned, bank[7][:].bitcast(fp16), ACT.Copy).then_inc(s["att_t_ready"], 1)

            def attention_high(j):
                act.wait_ge(s["att_ready"], 2 * (j + 1))
                act.activation(att_high, att[:], ACT.Copy)\
                    .then_inc(s["att_hi_ready"], 1)

            def act_step(j, par, first=False, second=False, last=False):
                exps(j, 0)
                if not first and not second:
                    turned_out(j - 2)
                weights_high(j, 0)
                if first:
                    parts_high(j + 1, early=True)
                exps(j, 1)
                if not first and not last:
                    parts_high(j + 1, early=second)
                if not last:
                    spread_queries_high(j + 1)
                weights_high(j, 1)
                weights_high(j, 2)
                if not last:
                    gate_tanh(j + 1, 1 - par, early=first)
                if not first:
                    attention_high(j - 1)

            parts_high(0, first=True, early=True)
            gate_tanh(0, 0, early=True)
            act_step(0, 0, first=True)
            act_step(1, 1, second=True)
            with act.Fori(0, PAIRS // 2 - 2) as i:
                act_step(2 * i + 2, 0)
                act_step(2 * i + 3, 1)
            act_step(PAIRS - 2, 0)
            act_step(PAIRS - 1, 1, last=True)

            def tokens_out(c, k):
                act.wait_ge(s["rt_ps"], 4 * c + k + 1)
                act.activation(x_t[c][k], bank[k][:], ACT.Copy).then_inc(s["rt_sb"], 1)

            tokens_out(0, 0)
            tokens_out(0, 1)
            turned_out(PAIRS - 2, last=True)
            tokens_out(0, 2)
            tokens_out(0, 3)
            attention_high(PAIRS - 1)
            turned_out(PAIRS - 1, last=True)

            def normalised(n):
                act.activation(xn[:, n, :], x_rows[:, n, :], ACT.Identity, bias=neg_mean[:, n:n + 1],
                               scale=rs_col[:, n:n + 1]).then_inc(s["xn_act"], 1)

            act.activation(sd_tok[:, 1:2], sd_tok[:, 0:1], ACT.Sqrt).then_inc(s["table_loaded"], 1)
            tokens_out(1, 0)
            tokens_out(1, 1)
            tokens_out(1, 2)
            tokens_out(1, 3)
            root(6, sd_col, var_col)
            act.wait_ge(s["logit_ps"], 1)
            act.activation(logit_t, bank[4][:], ACT.Copy).then_inc(s["lt_ready"], 1)
            act.wait_ge(s["rs_ready"], 1)
            for n in range(TILES - 4):
                normalised(n)
            act.wait_ge(s["shift_ready"], 1)
            act.activation(r_exp, r_exp, ACT.Exp).then_inc(s["prob_ready"], 1)
            act.activation(sd_tok[:, 1:2], sd_tok[:, 0:1], ACT.Silu).then_inc(s["table_loaded"], 1)

            def tokens_high(b, par, first=False):
                act.wait_ge(s["xt_ps"], b + 1)
                if not first:
                    act.wait_ge(s["gu_ps"], 2 * (b - 1))
                act.activation(x_hi[par], bank[4][:, 0:L_COL].rearrange("p (c t) -> p c t", c=2),
                               ACT.Copy).then_inc(s["xh_ready"], 1)

            def silu(b, par, first=False):
                act.wait_ge(s["gadd_ready"], b + 1)
                if not first:
                    act.wait_ge(s["h_ready"], b - 1)
                act.activation(g_silu[par], g_sum[par], ACT.Silu).then_inc(s["silu_ready"], 1)

            def hidden_high(b, par, first=False):
                act.wait_ge(s["ht_ps"], b + 1)
                act.activation(h_hi[par], bank[5][:].rearrange("p (c t) -> p c t", c=4),
                               ACT.Copy).then_inc(s["hh_ready"], 1)

            def weigh(b, par, first=False):
                act.wait_ge(s["yadd_ready"], b + 1)
                if not first:
                    act.wait_ge(s["scol_ready"], b)
                act.activation(yw[par], y_sum[par], ACT.Copy, scale=t_weight[:, bass.ds(b, 1)])\
                    .then_inc(s["y_ready"], 1)

            def act_block(b, par, first=False, more=2):
                hidden_high(b, par, first=first)
                if more >= 1:
                    silu(b + 1, 1 - par, first=first)
                if more >= 2:
                    tokens_high(b + 2, par)
                weigh(b, par, first=first)

            tokens_high(0, 0, first=True)
            tokens_high(1, 1, first=True)
            silu(0, 0, first=True)
            act_block(0, 0, first=True)
            with act.Fori(0, BODY) as i:
                for k in range(4):
                    act_block(4 * i + k + 1, (k + 1) % 2)
            act_block(BLOCKS - 2, 1, more=1)
            act_block(BLOCKS - 1, 0, more=0)

        @block.vector
        def _(dve):
            step = steps(dve, s["dve_step"])
            n_v = [0]

            def const(ins):
                ins.then_inc(s["const_v"], 1)
                n_v[0] += 1

            def rsqrt(k, y, v, sd, t, ready):
                dve.wait_ge(s["root_out"], k + 1)
                step(dve.reciprocal(y, sd))
                step(dve.tensor_tensor(t, v, y, ALU.mult))
                step(dve.tensor_tensor(t, t, y, ALU.mult))
                step(dve.tensor_scalar(t, t, -0.5, 1.5, ALU.mult, ALU.add))
                last = dve.tensor_tensor(y, y, t, ALU.mult)
                if ready:
                    last.then_inc(ready, 1)
                else:
                    step(last)

            const(dve.memset(ones_h[:], 1.0))
            step(dve.memset(minus_mean, -1.0 / L_COL))
            const(dve.memset(center, 0.0))
            dve.wait_ge(s["const_v"], 2)
            for h in range(2):
                const(dve.memset(center[64 * h:64 * h + 64, 64 * h:64 * h + 64], -1.0 / D_MODEL))
            dve.wait_ge(s["const_v"], 4)
            dve.wait_ge(s["const_p"], 9)
            const(dve.tensor_tensor(center, center, ident[:], ALU.add))
            assert n_v[0] == N_CENTER
            step(dve.tensor_scalar(small_i[:, 1:2], small_i[:, 0:1], 3, 3, ALU.logical_shift_right, ALU.bitwise_and))
            step(dve.tensor_copy(small[:, 150:151], small_i[:, 1:2]))
            for h in range(GROUP):
                step(dve.tensor_scalar(head_mask[:, h:h + 1], small[:, 150:151], float(h), None, ALU.is_equal))
            dve.wait_ge(s["pairs_in"], 16)
            step(dve.tensor_reduce(pair_s[:, 0:32], pr[0], AX.X, ALU.add))
            dve.tensor_scalar(pair_s[:, 0:32], pair_s[:, 0:32], 1.0 / P_DIM, None, ALU.mult).then_inc(s["pair_v"], 1)

            def statistics(rows, done):
                for n in rows:
                    dve.bn_stats(bn[:, n, :], x_rows[:, n, :]).then_inc(s["stats_ready"], 1)
                dve.wait_ge(s["stats_ready"], done + len(rows))
                for n in rows:
                    dve.bn_aggr(mv[:, n, :], bn[:, n, :]).then_inc(s["mean_ready"], 1)

            for q in range(QUADS):
                dve.wait_ge(s[f"x_in{q}"], 32)
                statistics(range(4 * q, 4 * q + 4), 4 * q)
                if q == 1:
                    dve.wait_ge(s["pool_pair"], 2)
                    step(dve.tensor_reduce(pair_s[:, 32:64], pr[1], AX.X, ALU.add))
                    dve.tensor_scalar(pair_s[:, 32:64], pair_s[:, 32:64], 1.0 / P_DIM, EPS_TOK, ALU.mult, ALU.add)\
                        .then_inc(s["root_in"], 1)
                    dve.wait_ge(s["root_in"], 1)
                if q == 2:
                    rsqrt(0, pair_s[:, 64:96], pair_s[:, 32:64], pair_s[:, 96:128], pair_s[:, 128:160], s["pair_v"])
            dve.wait_ge(s["mean_ready"], N_HALF)
            dve.tensor_scalar(var_col, mv[:, :, 1], EPS_COL, None, ALU.add).then_inc(s["root_in"], 1)
            dve.wait_ge(s["root_in"], 2)
            rsqrt(1, rs_col, var_col, sd_col, tmp_col, None)
            dve.scalar_tensor_tensor(out=neg_mean, in0=mv[:, :, 0], scalar=-1.0, in1=rs_col, op0=ALU.mult,
                                     op1=ALU.mult).then_inc(s["negm_ready"], 1)

            def columns(q):
                for i in range(4):
                    n = 4 * q + i
                    dve.tensor_scalar(x_col[q][i], x_rows[:, n, :], mv[:, n, 0:1], rs_col[:, n:n + 1],
                                      ALU.subtract, ALU.mult).then_inc(s["xcol_dve"], 1)

            columns(0)
            columns(2)
            columns(3)
            for q in range(QUADS):
                for h in range(2):
                    dve.wait_ge(s["sq_ready"], 2 * q + h + 1)
                    step(dve.tensor_reduce(sum_tok[:, 8 * h:8 * h + 8], squares[h].rearrange("p (t d) -> p t d", t=8),
                                           AX.X, ALU.add))
                dve.tensor_scalar(var_tok, sum_tok, 1.0 / D_MODEL, EPS_TOK, ALU.mult, ALU.add)\
                    .then_inc(s["root_in"], 1)
                dve.wait_ge(s["root_in"], q + 3)
                rsqrt(q + 2, rs_tok, var_tok, sd_tok, tmp_tok, None)
                for h in range(2):
                    if q >= 1:
                        dve.wait_ge(s["zlo_ready"], 2 * (q - 1) + h + 1)
                    r = rs_tok[:, 8 * h:8 * h + 8].unsqueeze(2).broadcast_to([P, 8, D_MODEL])
                    dve.tensor_tensor(z_tok[h].rearrange("p (t d) -> p t d", t=8),
                                      centred[q][h][:].rearrange("p (t d) -> p t d", t=8), r,
                                      ALU.mult).then_inc(s["ztok_ready"], 1)
                if q == 0:
                    dve.wait_ge(s["pool_pair"], 5)
                    dve.transpose(pr[2].rearrange("p i c -> p (i c)"), pr[0].rearrange("p i c -> p (i c)"))\
                        .then_inc(s["pair_v"], 1)
                    dve.wait_ge(s["par_in"], 16 * N_PAR)
                    dve.tensor_copy(b_wide, b_col[0:64, :].broadcast_to([64, P])).then_inc(s["wide_ready"], 1)
                if q == 3:
                    dve.wait_ge(s["pe_prep"], 1)
                    step(dve.tensor_scalar(qb_col, bank[7][:, 0:1], Q_SCALE, None, ALU.mult))
                    step(dve.tensor_copy(kb_col, bank[7][:, 1:2]))
                    step(dve.tensor_copy(v_row[:], bank[7][:, 128:192]))
                    step(dve.tensor_tensor(rw_sb, rw_sb, bank[7][:, 8:16].unsqueeze(1).broadcast_to([P, 2, EXPERTS]),
                                           ALU.add))
                    dve.tensor_tensor(g_row[:], bank[7][:, 192:256], bg_row, ALU.add).then_inc(s["vec_copied"], 1)
                    dve.wait_ge(s["vec_copied"], 1)
            dve.wait_ge(s["zhi_ready"], 2 * QUADS)
            dve.tensor_tensor(z_parts[1][:, :, 1, :], z_tok[1].rearrange("p (t d) -> p t d", t=8),
                              z_parts[1][:, :, 0, :], ALU.subtract).then_inc(s["zlo_last"], 1)
            dve.wait_ge(s["pe_bias"], 1)
            dve.tensor_copy(bias_t[0:32, :], bank[2][0:32, 0:256]).then_inc(s["bias_copied"], 1)
            dve.wait_ge(s["bias_copied"], 1)
            dve.tensor_tensor(bias_t[32:64, :], bank[2][0:32, 0:256], bias_t[0:32, :], ALU.subtract)\
                .then_inc(s["bias_copied"], 1)

            def last_tokens():
                dve.wait_ge(s["ztr_ready"], 2 * QUADS)
                dve.tensor_copy(z_stack_v[:, 1, :, :, 4 * (QUADS - 1):],
                                stacked[QUADS - 1][1][:].bitcast(fp16).rearrange("p (i h l) -> p l h i", i=4, h=2))\
                    .then_inc(s["zst_last"], 1)

            def pair_tokens(j, first=False):
                if not first:
                    dve.wait_ge(s["v_ps"], 4 * j)
                src = z_stack[:].rearrange("p l n -> p (l n)")[:, bass.ds(j * (PAIR * N_SEQ), PAIR * N_SEQ)]
                dve.tensor_copy(z_pair[:].bitcast(fp32), src.bitcast(fp32)).then_inc(s["zpair_ready"], 1)

            def soften(j, c, first=False):
                dve.wait_ge(s["s_ps"], 2 * j + c + 1)
                for g in range(2):
                    dve.tensor_reduce(maxes[:, 2 * c + g, :],
                                      bank[2 * c + g][:].rearrange("p (l m) -> p l m", l=CHUNK), AX.X, ALU.max)\
                        .then_inc(s["max_ready"], 1)
                if not first:
                    dve.wait_ge(s["et_ready"], 2 * j + c - 1)
                for g in range(2):
                    dve.wait_ge(s["max_ready"], 4 * j + 2 * c + g + 1)
                    dve.tensor_tensor(s_exp[:, c, g, :].rearrange("p (l m) -> p l m", l=CHUNK),
                                      bank[2 * c + g][:].rearrange("p (l m) -> p l m", l=CHUNK),
                                      maxes[:, 2 * c + g, :].unsqueeze(2).broadcast_to([P, CHUNK, N_SEQ]),
                                      ALU.subtract).then_inc(s["sub_ready"], 1)

            def turn(j, c, first=False):
                dve.wait_ge(s["exp_ready"], 2 * j + c + 1)
                if not first:
                    dve.wait_ge(s["av_ps"], 2 * j + c - 1)
                dve.transpose(e_t[:, c, :, :].rearrange("p g t -> p (g t)"),
                              s_exp[:, c, :, :].rearrange("p g t -> p (g t)")).then_inc(s["et_ready"], 1)

            def normalise(j, c, src=bank[6], last=False):
                dve.wait_ge(s["av_ps"], 2 * j + c + 1)
                av = src[:, 0:4 * 2 * VCOL].rearrange("p (a v) -> p a v", v=VCOL)
                rd = rden[:, c, :].rearrange("p (a h) -> p a h", h=GROUP)
                dve.reciprocal(rd, av[:, :, 32:36]).then_inc(s["rden_ready"], 1)
                dve.wait_ge(s["rden_ready"], 2 * j + c + 1)
                if last:
                    dve.wait_ge(s["at_ps"], j)
                else:
                    dve.wait_ge(s["vt_ready"], 4 * (j + 2))
                dve.tensor_tensor(att_n[:, c, :].rearrange("p (a h d) -> p a h d", h=GROUP, d=D_HEAD),
                                  av[:, :, 0:32].rearrange("p a (h d) -> p a h d", h=GROUP),
                                  rd.unsqueeze(3).broadcast_to([P, 8, GROUP, D_HEAD]),
                                  ALU.mult).then_inc(s["norm_ready"], 1)

            def apply_gate(j, c, par):
                dve.wait_ge(s["vb_ready"], 2 * j + c + 1)
                dve.wait_ge(s["gate_ready"], j + 1)
                dve.scalar_tensor_tensor(out=att[:, :, c, :], in0=gate_v[par][:, c, :, :], scalar=1.0,
                                         in1=att_n[:, c, :].rearrange("p (q v) -> p q v", q=4),
                                         op0=ALU.add, op1=ALU.mult).then_inc(s["att_ready"], 1)

            def gate_sum(j, first=False):
                dve.wait_ge(s["g_ps"], j + 1)
                if not first:
                    dve.wait_ge(s["gate_ready"], j)
                dve.tensor_tensor(g_pre[:].rearrange("p (t v) -> p t v", t=8),
                                  bank[7][:].rearrange("p (t v) -> p t v", t=8),
                                  g_row[:].unsqueeze(1).broadcast_to([P, 8, D_MODEL]), ALU.add)\
                    .then_inc(s["gpre_ready"], 1)

            def values_turned(j, c, g, par, early=False):
                dve.wait_ge(s["v_ps"], 4 * j + 2 * c + g + 1)
                if not early:
                    dve.wait_ge(s["av_ps"], 2 * j + c - 3)
                dve.transpose(v_tile[par][:, c, g, :, 0:32], bank[4 + g][:].rearrange("p (l m) -> p l m", l=CHUNK))\
                    .then_inc(s["vt_ready"], 1)

            def spread_queries(j, first=False):
                if first:
                    dve.wait_ge(s["qh_ready"], 1)
                    for h in range(GROUP):
                        dve.tensor_scalar(q_exp[:, 0, :, h, :], q_hi[:].rearrange("p (l n) -> p l n", l=CHUNK),
                                          head_mask[:, h:h + 1], None, ALU.mult).then_inc(s["qexp_hi_ready"], 1)
                dve.wait_ge(s["q_lo_ready"], j + 1)
                if not first:
                    dve.wait_ge(s["s_ps"], 2 * j)
                for h in range(GROUP):
                    dve.tensor_scalar(q_exp[:, 1, :, h, :], q_lo[:].rearrange("p (l n) -> p l n", l=CHUNK),
                                      head_mask[:, h:h + 1], None, ALU.mult).then_inc(s["qexp_lo_ready"], 1)

            def add_rows(j):
                dve.wait_ge(s["wo_ps"], j + 1)
                for c in range(2):
                    dst = x_rows[:, :, bass.ds(PAIR * j + CHUNK * c, CHUNK)]
                    dve.scalar_tensor_tensor(
                        out=dst, in0=bank[7][:, 256 * c:256 * c + 256].rearrange("p (l n) -> p n l", l=CHUNK),
                        scalar=bo_col, in1=dst, op0=ALU.add, op1=ALU.add).then_inc(s["x1_ready"], 1)

            def dve_step(j, par, first=False, second=False, last=False):
                soften(j, 0, first=first)
                if first:
                    values_turned(0, 1, 0, 0, early=True)
                    values_turned(0, 1, 1, 0, early=True)
                if not last:
                    pair_tokens(j + 1)
                soften(j, 1, first=first)
                if not first:
                    normalise(j - 1, 0)
                if not first and not second:
                    add_rows(j - 2)
                turn(j, 0, first=first)
                if not last:
                    values_turned(j + 1, 0, 0, 1 - par, early=first)
                    values_turned(j + 1, 0, 1, 1 - par, early=first)
                    spread_queries(j + 1)
                if not first:
                    normalise(j - 1, 1, src=bank[4] if last else bank[6])
                if not last:
                    gate_sum(j + 1)
                turn(j, 1, first=first)
                if not first:
                    apply_gate(j - 1, 0, 1 - par)
                    apply_gate(j - 1, 1, 1 - par)
                if not last:
                    values_turned(j + 1, 1, 0, 1 - par, early=first)
                    values_turned(j + 1, 1, 1, 1 - par, early=first)

            dve.wait_ge(s["zst0"], QUADS)
            pair_tokens(0, first=True)
            last_tokens()
            dve.wait_ge(s["zst1"], QUADS - 1)
            dve.wait_ge(s["zst_last"], 1)
            spread_queries(0, first=True)
            gate_sum(0, first=True)
            values_turned(0, 0, 0, 0, early=True)
            values_turned(0, 0, 1, 0, early=True)
            dve_step(0, 0, first=True)
            dve_step(1, 1, second=True)
            with dve.Fori(0, PAIRS // 2 - 2) as i:
                dve_step(2 * i + 2, 0)
                dve_step(2 * i + 3, 1)
            dve_step(PAIRS - 2, 0)
            dve_step(PAIRS - 1, 1, last=True)
            normalise(PAIRS - 1, 0, src=bank[5], last=True)
            dve.memset(rw_pad, 0.0).then_inc(s["rw_ready"], 1)
            dve.wait_ge(s["rw_ready"], 1)
            dve.tensor_copy(rw_pad[:, :, 0:EXPERTS], rw_sb).then_inc(s["rw_ready"], 1)
            head, tail = slice(0, L_COL - 2 * PAIR), slice(L_COL - 2 * PAIR, L_COL)
            for n in range(TILES // 2):
                dve.bn_stats(bn2[:, n, 0:6], x_rows[:, n, head]).then_inc(s["stats_ready"], 1)
            normalise(PAIRS - 1, 1, last=True)
            apply_gate(PAIRS - 1, 0, 1)
            apply_gate(PAIRS - 1, 1, 1)
            add_rows(PAIRS - 2)
            dve.wait_ge(s["att_hi_ready"], PAIRS)
            dve.tensor_tensor(att_low, att[:], att_high, ALU.subtract).then_inc(s["att_lo_ready"], 1)
            for n in range(TILES // 2, TILES):
                dve.bn_stats(bn2[:, n, 0:6], x_rows[:, n, head]).then_inc(s["stats_ready"], 1)
            add_rows(PAIRS - 1)

            dve.wait_ge(s["x1_ready"], 2 * PAIRS)
            for n in range(TILES):
                dve.bn_stats(bn2[:, n, 6:12], x_rows[:, n, tail]).then_inc(s["stats_ready"], 1)
            dve.wait_ge(s["stats_ready"], 3 * TILES)
            for n in range(TILES):
                dve.bn_aggr(mv[:, n, :], bn2[:, n, :]).then_inc(s["mean_ready"], 1)
            dve.wait_ge(s["mean_ready"], 2 * TILES)
            dve.tensor_scalar(var_col, mv[:, :, 1], EPS_TOK, None, ALU.add).then_inc(s["root_in"], 1)
            dve.wait_ge(s["root_in"], 7)
            dve.wait_ge(s["route_p"], N_TABLES)
            step(dve.tensor_copy(iota_f, r_iota128))
            step(dve.tensor_copy(thr_f, r_thr))
            step(dve.tensor_copy(tid_f, r_tid))
            step(dve.tensor_copy(rev_f, r_rev))
            rsqrt(6, rs_col, var_col, sd_col, tmp_col, None)
            dve.scalar_tensor_tensor(out=neg_mean, in0=mv[:, :, 0], scalar=-1.0, in1=rs_col,
                                     op0=ALU.mult, op1=ALU.mult).then_inc(s["rs_ready"], 1)
            step(dve.tensor_copy(spare_row, small_i[:, 0:1]))
            step(dve.tensor_scalar(spare_row, spare_row, float(TOKENS + 1), None, ALU.add))

            dve.wait_ge(s["lt_ps"], 1)
            all_experts = [P, TILES, EXPERTS]
            rev_b = rev_f.unsqueeze(1).broadcast_to(all_experts)
            by_tile = bank[6][:].rearrange("p (t k e) -> p k t e", t=4, k=4)[:, :, :, 0:EXPERTS]
            step(dve.tensor_tensor(r_logit.rearrange("p (k t) e -> p k t e", k=4), by_tile,
                                   rs_col.rearrange("p (k t) -> p k t", k=4).unsqueeze(3)
                                   .broadcast_to([P, 4, 4, EXPERTS]), ALU.mult))
            step(dve.tensor_tensor(r_logit, r_logit, rb_row.unsqueeze(1).broadcast_to(all_experts), ALU.add))
            for k, (among, largest) in enumerate(((r_logit, r_m1), (r_rest, r_m2))):
                step(dve.tensor_reduce(largest, among, AX.X, ALU.max))
                step(dve.tensor_tensor(r_mark, among, largest.unsqueeze(2).broadcast_to(all_experts), ALU.is_equal))
                step(dve.tensor_tensor(r_mark, r_mark, rev_b, ALU.mult))
                step(dve.tensor_reduce(r_first, r_mark, AX.X, ALU.max))
                step(dve.tensor_tensor(r_top[:, k], r_first.unsqueeze(2).broadcast_to(all_experts), rev_b,
                                       ALU.is_equal))
                if k == 0:
                    step(dve.scalar_tensor_tensor(out=r_rest, in0=r_top[:, 0], scalar=-3.0e38, in1=r_logit,
                                                  op0=ALU.mult, op1=ALU.add))
            step(dve.tensor_tensor(r_sel.rearrange("p (e n) -> p n e", e=EXPERTS), r_top[:, 0], r_top[:, 1], ALU.add))
            dve.tensor_tensor_scan(r_incl, r_keep, r_sel, 0.0, ALU.mult, ALU.add).then_inc(s["sel_ready"], 1)
            dve.tensor_tensor(r_exp, r_m2, r_m1, ALU.subtract).then_inc(s["shift_ready"], 1)
            dve.wait_ge(s["route_ps"], 1)
            step(dve.tensor_tensor(r_cmp, bank[3][:, 128:136].unsqueeze(2).broadcast_to([P, EXPERTS, TILES]),
                                   thr_f.unsqueeze(1).broadcast_to([P, EXPERTS, TILES]), ALU.is_gt))
            step(dve.tensor_reduce(r_nb, r_cmp, AX.X, ALU.add))
            step(dve.tensor_tensor_scan(r_cum, r_one8, r_nb, 0.0, ALU.mult, ALU.add))
            step(dve.tensor_tensor(r_base, r_cum, r_nb, ALU.subtract))
            step(dve.scalar_tensor_tensor(out=r_slot.rearrange("p (e n) -> p e n", e=EXPERTS),
                                          in0=r_base.unsqueeze(2).broadcast_to([P, EXPERTS, TILES]),
                                          scalar=float(SLOTS),
                                          in1=bank[3][:, 0:128].rearrange("p (e n) -> p e n", e=EXPERTS),
                                          op0=ALU.mult, op1=ALU.add))
            slot_v = r_slot.rearrange("p (e n) -> p n e", e=EXPERTS)
            for k in range(TOP_K):
                step(dve.tensor_tensor(r_tmp[:, k], r_top[:, k], slot_v, ALU.mult))
            step(dve.tensor_reduce(r_slots, r_tmp.rearrange("p k n e -> p (k n) e"), AX.X, ALU.add))
            dve.wait_ge(s["den_ready"], 1)
            dve.reciprocal(r_w[:, 0:TILES], r_den).then_inc(s["wfirst_ready"], 1)
            step(dve.tensor_copy(r_ints[:, 0:32], r_slots))
            step(dve.tensor_scalar(r_ints[:, 64:96], r_ints[:, 0:32], 7, None, ALU.logical_shift_right))
            step(dve.tensor_copy(r_b, r_ints[:, 64:96]))
            dve.tensor_tensor(r_block, iota_f[:, 0:BLOCKS].unsqueeze(1).broadcast_to([P, ASSIGN, BLOCKS]),
                              r_b.unsqueeze(2).broadcast_to([P, ASSIGN, BLOCKS]), ALU.is_equal)\
                .then_inc(s["block_ready"], 1)
            dve.wait_ge(s["block_ready"], 1)
            step(dve.tensor_scalar(r_ints[:, 32:64], r_ints[:, 0:32], SLOTS - 1, None, ALU.bitwise_and))
            step(dve.tensor_copy(r_p, r_ints[:, 32:64]))
            step(dve.tensor_tensor(r_values[:, 0:TILES, 0:BLOCKS], r_block[:, 0:TILES, :],
                                   tid_f.unsqueeze(2).broadcast_to([P, TILES, BLOCKS]), ALU.mult))
            for piece in range(PIECES):
                cols = slice(PIECE * piece, PIECE * (piece + 1))
                dve.tensor_tensor(r_place[:, cols, :], iota_f.unsqueeze(1).broadcast_to([P, PIECE, P]),
                                  r_p[:, cols].unsqueeze(2).broadcast_to([P, PIECE, P]), ALU.is_equal)\
                    .then_inc(s["place_ready"], 1)
            step(dve.tensor_tensor(r_ecmp, iota_f[:, 0:BLOCKS].unsqueeze(2).broadcast_to([P, BLOCKS, EXPERTS]),
                                   r_cum.unsqueeze(1).broadcast_to([P, BLOCKS, EXPERTS]), ALU.is_ge))
            step(dve.tensor_reduce(r_tab[:, 0:BLOCKS], r_ecmp, AX.X, ALU.add))
            step(dve.tensor_scalar(t_expert, r_tab[:, 0:BLOCKS], EXPERTS - 1.0, None, ALU.min))
            dve.wait_ge(s["tab_ps"], 1)
            tok = bank[4][:, 0:BLOCKS]
            empty = r_tab[:, 128:128 + BLOCKS]
            step(dve.tensor_scalar(t_gather, tok, -1.0, 0.0, ALU.add, ALU.max))
            step(dve.tensor_scalar(empty, tok, 0.0, spare_row, ALU.is_equal, ALU.mult))
            step(dve.tensor_reduce(t_weight, bank[4][:, BLOCKS:3 * BLOCKS].rearrange("p (s b) -> p b s", s=2),
                                   AX.X, ALU.add))
            dve.scalar_tensor_tensor(out=t_scatter, in0=empty, scalar=-1.0, in1=tok, op0=ALU.add, op1=ALU.add)\
                .then_inc(s["tables_ready"], 1)
            dve.wait_ge(s["tables_ready"], 1)

            def tokens_low(b, par, first=False):
                dve.wait_ge(s["xh_ready"], b + 1)
                dve.tensor_tensor(x_lo[par], bank[4][:, 0:L_COL].rearrange("p (c t) -> p c t", c=2), x_hi[par],
                                  ALU.subtract).then_inc(s["xl_ready"], 1)

            def expert_of(b):
                return dve.value_load(t_expert[0:1, bass.ds(b, 1)], min_val=0, max_val=EXPERTS - 1)

            def gate_bias(b, par, e, first=False):
                dve.wait_ge(s["gu_ps"], 2 * b + 1)
                if not first:
                    dve.wait_ge(s["silu_ready"], b - 1)
                dve.tensor_tensor(g_sum[par], bank[2 * par][:], gate_b_all[:, bass.ds(e * FF, FF)], ALU.add)\
                    .then_inc(s["gadd_ready"], 1)

            def up_bias(b, par, e, first=False):
                dve.wait_ge(s["gu_ps"], 2 * b + 2)
                dve.tensor_tensor(u_sum[par], bank[2 * par + 1][:], up_b_all[:, bass.ds(e * FF, FF)], ALU.add)\
                    .then_inc(s["uadd_ready"], 1)

            def gated(b, par, first=False):
                dve.wait_ge(s["silu_ready"], b + 1)
                dve.wait_ge(s["uadd_ready"], b + 1)
                if not first:
                    dve.wait_ge(s["ht_ps"], b - 1)
                dve.tensor_tensor(h_sb[par], g_silu[par], u_sum[par], ALU.mult).then_inc(s["h_ready"], 1)

            def hidden_low(b, par):
                dve.wait_ge(s["hh_ready"], b + 1)
                dve.tensor_tensor(h_lo[par], bank[5][:].rearrange("p (c t) -> p c t", c=4), h_hi[par],
                                  ALU.subtract).then_inc(s["hl_ready"], 1)

            def down_bias(b, par, e, first=False):
                dve.wait_ge(s["y_ps"], b + 1)
                dve.tensor_tensor(y_sum[par], bank[6][:, 0:L_COL], down_b_all[:, bass.ds(e * L_COL, L_COL)], ALU.add)\
                    .then_inc(s["yadd_ready"], 1)

            def dve_block(b, par, first=False, more=2):
                if more >= 1:
                    e1 = expert_of(b + 1)
                    gate_bias(b + 1, 1 - par, e1, first=first)
                hidden_low(b, par)
                if more >= 1:
                    up_bias(b + 1, 1 - par, e1)
                if more >= 2:
                    tokens_low(b + 2, par)
                if more >= 1:
                    gated(b + 1, 1 - par, first=first)
                down_bias(b, par, expert_of(b), first=first)

            tokens_low(0, 0)
            tokens_low(1, 1)
            e0 = expert_of(0)
            dve.wait_ge(s["bias_rows"], 32)
            gate_bias(0, 0, e0, first=True)
            dve.wait_ge(s["up_rows"], 32)
            up_bias(0, 0, e0)
            gated(0, 0, first=True)
            dve_block(0, 0, first=True)
            with dve.Fori(0, BODY) as i:
                for k in range(4):
                    dve_block(4 * i + k + 1, (k + 1) % 2)
            dve_block(BLOCKS - 2, 1, more=1)
            dve_block(BLOCKS - 1, 0, more=0)


_INS = ['x', 'L0_conv_pairs', 'L0_conv_ln_m_g', 'L0_conv_ln_m_b', 'L0_conv_ln_p_g', 'L0_conv_ln_p_b', 'L0_conv_Wq',
        'L0_conv_Wk', 'L0_conv_Wv', 'L0_conv_Wg', 'L0_conv_bg', 'L0_conv_Wb', 'L0_conv_Wo', 'L0_conv_bo',
        'L0_ffn_router_w', 'L0_ffn_router_b', 'L0_ffn_gate_w', 'L0_ffn_gate_b', 'L0_ffn_up_w', 'L0_ffn_up_b',
        'L0_ffn_down_w', 'L0_ffn_down_b']


def kernel(**inputs):
    import numpy as _np
    import concourse.bacc as _bacc
    from concourse import mybir as _mybir
    from concourse.bass_utils import run_bass_kernel_spmd as _run

    nc = _bacc.Bacc("TRN2", target_bir_lowering=False, num_devices=1)
    arrays, args = {}, []
    for name in _INS:
        a = _np.ascontiguousarray(inputs[name])
        arrays[f"in_{name}_dram"] = a
        args.append(nc.dram_tensor(f"in_{name}_dram", a.shape, _mybir.dt.from_np(a.dtype), kind="ExternalInput").ap())
    args.append(nc.dram_tensor("out_dram", (TOKENS + SLOTS, L_COL), _mybir.dt.float32, kind="ExternalOutput").ap())
    build(nc, *args)
    r = _run(nc, [arrays], core_ids=[0])
    return r.results[0]["out_dram"][:TOKENS].reshape(1, D_MODEL, N_SEQ, L_COL)
```
